# Optimizing a Trainium2 kernel written in Bass

```python
import numpy as np
import jax
import jax.numpy as jnp

def _softmax(x, axis=-1):
    return jax.nn.softmax(x, axis=axis)

def _gelu(x):
    return jax.nn.gelu(x, approximate=True)

def _silu(x):
    return jax.nn.silu(x)

def _sigmoid(x):
    return jax.nn.sigmoid(x)

def _layernorm(x, axis=-1, eps=1e-05):
    m = jnp.mean(x, axis=axis, keepdims=True)
    v = jnp.var(x, axis=axis, keepdims=True)
    return (x - m) / jnp.sqrt(v + eps)

def _scatter_add(tgt, idx, src, axis=0):
    return tgt.at[idx].add(src)

def _segment_sum(src, seg, n):
    return jax.ops.segment_sum(src, seg, n)
kernel_name = 'mk_seq_postln_d1_jaxref_r8_218c4b'

def setup_inputs(seed: int=0):
    np.random.seed(seed)
    _w = jnp.asarray

    def _L0_attn_setup():
        import jax, jax.numpy as jnp
        import numpy as np
        B, T, C = (4, 512, 128)
        NUM_LAYERS = 24
        LAYER_ID = 0
        EPS = 1e-05

        def _ln(x, w, b):
            m = x.mean(-1, keepdims=True)
            v = x.var(-1, keepdims=True)
            return (x - m) / jnp.sqrt(v + EPS) * w + b

        def _time_shift(x):
            return jnp.pad(x, ((0, 0), (1, 0), (0, 0)))[:, :-1]

        def _wkv(w, u, k, v):

            def step(carry, kv_t):
                aa, bb, pp = carry
                kt, vt = kv_t
                ww = u + kt
                p = jnp.maximum(pp, ww)
                e1 = jnp.exp(pp - p)
                e2 = jnp.exp(ww - p)
                y = (e1 * aa + e2 * vt) / (e1 * bb + e2)
                ww2 = pp + w
                p2 = jnp.maximum(ww2, kt)
                e1 = jnp.exp(ww2 - p2)
                e2 = jnp.exp(kt - p2)
                return ((e1 * aa + e2 * vt, e1 * bb + e2, p2), y)
            Bz, Tz, Cz = k.shape
            init = (jnp.zeros((Bz, Cz), k.dtype), jnp.zeros((Bz, Cz), k.dtype), jnp.full((Bz, Cz), -1e+38, k.dtype))
            kT = jnp.swapaxes(k, 0, 1)
            vT = jnp.swapaxes(v, 0, 1)
            _, y = jax.lax.scan(step, init, (kT, vT))
            return jnp.swapaxes(y, 0, 1)
        key = jax.random.key(seed)
        ks = jax.random.split(key, 9)
        s = 0.02
        ratio_0_to_1 = LAYER_ID / (NUM_LAYERS - 1)
        ratio_1_to_almost0 = 1.0 - LAYER_ID / NUM_LAYERS
        h = np.arange(C, dtype=np.float64)
        time_decay = (-5.0 + 8.0 * (h / (C - 1)) ** (0.7 + 1.3 * ratio_0_to_1)).astype(np.float32)
        zigzag = ((np.arange(C) + 1) % 3 - 1) * 0.5
        time_first = (np.ones(C) * np.log(0.3) + zigzag).astype(np.float32)
        xi = np.arange(C, dtype=np.float64) / C
        tmk = (xi ** ratio_1_to_almost0).astype(np.float32)
        tmv = (xi ** ratio_1_to_almost0 + 0.3 * ratio_0_to_1).astype(np.float32)
        tmr = (xi ** (0.5 * ratio_1_to_almost0)).astype(np.float32)
        cmk = (xi ** ratio_1_to_almost0).astype(np.float32)
        H = 4 * C
        return {'x': jax.random.normal(ks[0], (B, T, C), jnp.float32), 'ln0_w': jnp.ones(C), 'ln0_b': jnp.zeros(C), 'ln1_w': jnp.ones(C), 'ln1_b': jnp.zeros(C), 'ln2_w': jnp.ones(C), 'ln2_b': jnp.zeros(C), 'time_decay': jnp.asarray(time_decay), 'time_first': jnp.asarray(time_first), 'tmk': jnp.asarray(tmk), 'tmv': jnp.asarray(tmv), 'tmr': jnp.asarray(tmr), 'Wk': jax.random.normal(ks[1], (C, C), jnp.float32) * s, 'Wv': jax.random.normal(ks[2], (C, C), jnp.float32) * s, 'Wr': jax.random.normal(ks[3], (C, C), jnp.float32) * s, 'Wo': jax.random.normal(ks[4], (C, C), jnp.float32) * s, 'cmk': jnp.asarray(cmk), 'cmr': jnp.asarray(cmk), 'Wfk': jax.random.normal(ks[5], (H, C), jnp.float32) * s, 'Wfr': jax.random.normal(ks[6], (C, C), jnp.float32) * s, 'Wfv': jax.random.normal(ks[7], (C, H), jnp.float32) * s}
    _L0_attn_in = _L0_attn_setup()

    def _L0_ffn_setup():
        import jax, jax.numpy as jnp
        import numpy as np
        D = 128
        E = 12
        HS = 2 * D
        HR = 3 * D
        TAU = 1.5

        def _geglu(h):
            a, g = jnp.split(h, 2, axis=-1)
            return a * jax.nn.gelu(g, approximate=False)
        key = jax.random.key(seed)
        ks = jax.random.split(key, 12)

        def xavier(k, shape):
            fan_in, fan_out = (shape[-2], shape[-1])
            lim = jnp.sqrt(6.0 / (fan_in + fan_out))
            return jax.random.uniform(k, shape, jnp.float32, -lim, lim)
        x = jax.random.normal(ks[0], (2, 128, D), jnp.float32)
        Ws1 = xavier(ks[1], (D, 2 * HS))
        bs1 = jnp.zeros((2 * HS,), jnp.float32)
        Ws2 = xavier(ks[2], (HS, D))
        bs2 = jnp.zeros((D,), jnp.float32)
        We1 = xavier(ks[3], (E, D, 2 * HR))
        be1 = jnp.zeros((E, 2 * HR), jnp.float32)
        We2 = xavier(ks[4], (E, HR, D))
        be2 = jnp.zeros((E, D), jnp.float32)
        Wr = xavier(ks[5], (D, E))
        br = jnp.zeros((E,), jnp.float32)
        return {'x': x, 'Ws1': Ws1, 'bs1': bs1, 'Ws2': Ws2, 'bs2': bs2, 'We1': We1, 'be1': be1, 'We2': We2, 'be2': be2, 'Wr': Wr, 'br': br}
    _L0_ffn_in = _L0_ffn_setup()
    _d = {'L0_attn_x': _L0_attn_in['x'], 'L0_attn_ln0_w': _L0_attn_in['ln0_w'], 'L0_attn_ln0_b': _L0_attn_in['ln0_b'], 'L0_attn_ln1_w': _L0_attn_in['ln1_w'], 'L0_attn_ln1_b': _L0_attn_in['ln1_b'], 'L0_attn_ln2_w': _L0_attn_in['ln2_w'], 'L0_attn_ln2_b': _L0_attn_in['ln2_b'], 'L0_attn_time_decay': _L0_attn_in['time_decay'], 'L0_attn_time_first': _L0_attn_in['time_first'], 'L0_attn_tmk': _L0_attn_in['tmk'], 'L0_attn_tmv': _L0_attn_in['tmv'], 'L0_attn_tmr': _L0_attn_in['tmr'], 'L0_attn_Wk': _L0_attn_in['Wk'], 'L0_attn_Wv': _L0_attn_in['Wv'], 'L0_attn_Wr': _L0_attn_in['Wr'], 'L0_attn_Wo': _L0_attn_in['Wo'], 'L0_attn_cmk': _L0_attn_in['cmk'], 'L0_attn_cmr': _L0_attn_in['cmr'], 'L0_attn_Wfk': _L0_attn_in['Wfk'], 'L0_attn_Wfr': _L0_attn_in['Wfr'], 'L0_attn_Wfv': _L0_attn_in['Wfv'], 'L0_ffn_Ws1': _L0_ffn_in['Ws1'], 'L0_ffn_bs1': _L0_ffn_in['bs1'], 'L0_ffn_Ws2': _L0_ffn_in['Ws2'], 'L0_ffn_bs2': _L0_ffn_in['bs2'], 'L0_ffn_We1': _L0_ffn_in['We1'], 'L0_ffn_be1': _L0_ffn_in['be1'], 'L0_ffn_We2': _L0_ffn_in['We2'], 'L0_ffn_be2': _L0_ffn_in['be2'], 'L0_ffn_Wr': _L0_ffn_in['Wr'], 'L0_ffn_br': _L0_ffn_in['br']}
    _x0 = _d['L0_attn_x']
    _d['L0_attn_x'] = jax.random.normal(jax.random.fold_in(jax.random.key(seed), 1), (16, 256, 128), dtype=_x0.dtype)
    del _x0
    return _d

def reference(L0_attn_x, L0_attn_ln0_w, L0_attn_ln0_b, L0_attn_ln1_w, L0_attn_ln1_b, L0_attn_ln2_w, L0_attn_ln2_b, L0_attn_time_decay, L0_attn_time_first, L0_attn_tmk, L0_attn_tmv, L0_attn_tmr, L0_attn_Wk, L0_attn_Wv, L0_attn_Wr, L0_attn_Wo, L0_attn_cmk, L0_attn_cmr, L0_attn_Wfk, L0_attn_Wfr, L0_attn_Wfv, L0_ffn_Ws1, L0_ffn_bs1, L0_ffn_Ws2, L0_ffn_bs2, L0_ffn_We1, L0_ffn_be1, L0_ffn_We2, L0_ffn_be2, L0_ffn_Wr, L0_ffn_br):

    def _L0_attn_ref(x, ln0_w, ln0_b, ln1_w, ln1_b, ln2_w, ln2_b, time_decay, time_first, tmk, tmv, tmr, Wk, Wv, Wr, Wo, cmk, cmr, Wfk, Wfr, Wfv):
        import jax, jax.numpy as jnp
        import numpy as np
        B, T, C = (4, 512, 128)
        NUM_LAYERS = 24
        LAYER_ID = 0
        EPS = 1e-05

        def _ln(x, w, b):
            m = x.mean(-1, keepdims=True)
            v = x.var(-1, keepdims=True)
            return (x - m) / jnp.sqrt(v + EPS) * w + b

        def _time_shift(x):
            return jnp.pad(x, ((0, 0), (1, 0), (0, 0)))[:, :-1]

        def _wkv(w, u, k, v):

            def step(carry, kv_t):
                aa, bb, pp = carry
                kt, vt = kv_t
                ww = u + kt
                p = jnp.maximum(pp, ww)
                e1 = jnp.exp(pp - p)
                e2 = jnp.exp(ww - p)
                y = (e1 * aa + e2 * vt) / (e1 * bb + e2)
                ww2 = pp + w
                p2 = jnp.maximum(ww2, kt)
                e1 = jnp.exp(ww2 - p2)
                e2 = jnp.exp(kt - p2)
                return ((e1 * aa + e2 * vt, e1 * bb + e2, p2), y)
            Bz, Tz, Cz = k.shape
            init = (jnp.zeros((Bz, Cz), k.dtype), jnp.zeros((Bz, Cz), k.dtype), jnp.full((Bz, Cz), -1e+38, k.dtype))
            kT = jnp.swapaxes(k, 0, 1)
            vT = jnp.swapaxes(v, 0, 1)
            _, y = jax.lax.scan(step, init, (kT, vT))
            return jnp.swapaxes(y, 0, 1)
        x = _ln(x, ln0_w, ln0_b)
        h = _ln(x, ln1_w, ln1_b)
        xx = _time_shift(h)
        xk = h * tmk + xx * (1 - tmk)
        xv = h * tmv + xx * (1 - tmv)
        xr = h * tmr + xx * (1 - tmr)
        k = jnp.einsum('btc,oc->bto', xk, Wk)
        v = jnp.einsum('btc,oc->bto', xv, Wv)
        sr = jax.nn.sigmoid(jnp.einsum('btc,oc->bto', xr, Wr))
        w = -jnp.exp(time_decay)
        att = _wkv(w, time_first, k, v)
        rwkv = jnp.einsum('btc,oc->bto', sr * att, Wo)
        x = x + rwkv
        h2 = _ln(x, ln2_w, ln2_b)
        xx2 = _time_shift(h2)
        xk2 = h2 * cmk + xx2 * (1 - cmk)
        xr2 = h2 * cmr + xx2 * (1 - cmr)
        kf = jnp.einsum('btc,hc->bth', xk2, Wfk)
        kf = jnp.square(jax.nn.relu(kf))
        kv = jnp.einsum('bth,ch->btc', kf, Wfv)
        rkv = jax.nn.sigmoid(jnp.einsum('btc,oc->bto', xr2, Wfr)) * kv
        return x + rkv

    def _L0_ffn_ref(x, Ws1, bs1, Ws2, bs2, We1, be1, We2, be2, Wr, br):
        import jax, jax.numpy as jnp
        import numpy as np
        D = 128
        E = 12
        HS = 2 * D
        HR = 3 * D
        TAU = 1.5

        def _geglu(h):
            a, g = jnp.split(h, 2, axis=-1)
            return a * jax.nn.gelu(g, approximate=False)
        B, T, Dm = x.shape
        xf = x.reshape(-1, Dm)
        ys = _geglu(xf @ Ws1 + bs1) @ Ws2 + bs2
        logits = (xf @ Wr + br) / TAU
        top_val, top_idx = jax.lax.top_k(logits, 2)
        top_w = jax.nn.softmax(top_val, axis=-1)
        onehot = jax.nn.one_hot(top_idx, E, dtype=x.dtype)
        w = jnp.einsum('nke,nk->ne', onehot, top_w)
        h = jnp.einsum('nd,edh->enh', xf, We1) + be1[:, None, :]
        act = _geglu(h)
        yE = jnp.einsum('enh,ehd->end', act, We2) + be2[:, None, :]
        yr = jnp.einsum('end,ne->nd', yE, w)
        return (ys + yr).reshape(B, T, Dm)
    x = L0_attn_x
    x = _layernorm(x + _L0_attn_ref(x, L0_attn_ln0_w, L0_attn_ln0_b, L0_attn_ln1_w, L0_attn_ln1_b, L0_attn_ln2_w, L0_attn_ln2_b, L0_attn_time_decay, L0_attn_time_first, L0_attn_tmk, L0_attn_tmv, L0_attn_tmr, L0_attn_Wk, L0_attn_Wv, L0_attn_Wr, L0_attn_Wo, L0_attn_cmk, L0_attn_cmr, L0_attn_Wfk, L0_attn_Wfr, L0_attn_Wfv), axis=-1)
    x = _layernorm(x + _L0_ffn_ref(x, L0_ffn_Ws1, L0_ffn_bs1, L0_ffn_Ws2, L0_ffn_bs2, L0_ffn_We1, L0_ffn_be1, L0_ffn_We2, L0_ffn_be2, L0_ffn_Wr, L0_ffn_br), axis=-1)
    return x

_drawn_inputs = setup_inputs


def setup_inputs(seed=0):
    import zlib

    import numpy as np

    out = dict(_drawn_inputs(seed))
    spreads = {'L0_attn_ln0_w': (1.0, 0.2),
     'L0_attn_ln0_b': (0.0, 0.1),
     'L0_attn_ln1_w': (1.0, 0.6),
     'L0_attn_ln1_b': (0.0, 0.8),
     'L0_attn_ln2_w': (1.0, 0.6),
     'L0_attn_ln2_b': (0.0, 0.8),
     'L0_ffn_bs1': (0.0, 0.1),
     'L0_ffn_bs2': (0.0, 0.1),
     'L0_ffn_be1': (0.0, 0.1),
     'L0_ffn_be2': (0.0, 0.1),
     'L0_ffn_br': (0.0, 0.1)}
    factors = {'L0_attn_time_decay': 6.753,
     'L0_attn_time_first': 8.0,
     'L0_attn_tmk': 8.0,
     'L0_attn_tmv': 8.0,
     'L0_attn_tmr': 8.0,
     'L0_attn_Wk': 8.0,
     'L0_attn_Wv': 4.585,
     'L0_attn_Wr': 8.0,
     'L0_attn_Wo': 4.786,
     'L0_attn_cmk': 8.0,
     'L0_attn_cmr': 8.0,
     'L0_attn_Wfk': 5.642,
     'L0_attn_Wfr': 8.0,
     'L0_attn_Wfv': 5.415}
    for name, (base, spread) in spreads.items():
        noise = np.random.default_rng([zlib.crc32(name.encode()), seed]).standard_normal(out[name].shape)
        drawn = base * np.exp(spread * noise) if base else spread * noise
        out[name] = jnp.asarray(drawn.astype(out[name].dtype))
    for name, factor in factors.items():
        out[name] = (out[name] * factor).astype(out[name].dtype)
    return out
```

```python
import concourse.bass as bass
from concourse import mybir
from contextlib import ExitStack


def build(nc, x, out, vecs, rows, sqw, wfk, wfv, wrt, ws1, ws2, we1, we2, be1, be2, bs2):
    F32, BF16 = mybir.dt.float32, mybir.dt.bfloat16
    I32, U32 = mybir.dt.int32, mybir.dt.uint32
    ALU = mybir.AluOpType
    ACT = mybir.ActivationFunctionType
    AX = mybir.AxisListType
    ds = bass.ds

    B, T, C = x.shape
    P = 128
    N = B * T
    NT = N // P
    CT = 4
    CH = NT // CT
    W = CT * P
    SQ = W // T
    E = we1.shape[0]
    HR = we2.shape[1]
    HK = HR // P
    H1 = 2 * HR
    HF = wfk.shape[1] // P
    HS = ws2.shape[0] // P
    K = 2
    SLOTS = K * N
    TILES = (SLOTS + E * (P - 1)) // P
    U = 3
    assert TILES % U == 0
    EPS, NEG, TAU = 1e-5, -1e38, 1.5
    JB = 16
    NJ = K * NT
    NQ = NJ // JB

    x_v = x.rearrange("b t c -> (b t) c").rearrange("(n p) c -> p n c", p=P)
    out_v = out.rearrange("b t c -> (b t) c").rearrange("(n p) c -> p n c", p=P)
    table = nc.dram_tensor("token_table", (N, C), F32, kind="Internal").ap()
    table_v = table.rearrange("(n p) c -> p n c", p=P)
    routed = nc.dram_tensor("routed_rows", (SLOTS, C), F32, kind="Internal").ap()
    routed_v = routed.rearrange("(k n p) c -> p k n c", p=P, k=K)

    ctx = ExitStack()
    with ctx:
        def sb(name, shape, dt=F32):
            return ctx.enter_context(nc.sbuf_tensor(name, shape, dt))

        def sem(name):
            return ctx.enter_context(nc.semaphore(name))

        x_all = sb("x_all", [P, NT, C])
        x0_all = sb("x0_all", [P, NT, C])
        xnT_all = sb("xnT_all", [P, N])
        y_first = x0_all
        y_second = xnT_all[:, :].rearrange("p (n c) -> p n c", c=C)
        we1_sb = sb("we1_sb", [P, E, H1])
        we2_sb = sb("we2_sb", [P, E, HK, C])
        BE2, BS2 = E * H1, E * H1 + E * C
        sq_sb = sb("sq_sb", [P, 5, C])
        mixa = sb("mixa", [P, 3, C])
        mixb = sb("mixb", [P, 3, C])
        wfk_sb = sb("wfk_sb", [P, HF * P])
        wfv_sb = sb("wfv_sb", [P, HF, C])
        wrt_sb = sb("wrt_sb", [P, E])
        ws1_sb = sb("ws1_sb", [P, 2 * HS * P])
        ws2_sb = sb("ws2_sb", [P, HS, C])
        NV = vecs.shape[1]
        v_sb = sb("v_sb", [P, NV])
        LN1W, LN1B, LN2W, LN2B, DECAY, FIRST, TMK, TMV, TMR, CMK, CMR, BS1 = range(12)
        NB = (E * H1 + E * C + C) // P
        braw = sb("braw", [P, NB])
        bleft = sb("bleft", [P, NB])
        bleft2 = sb("bleft2", [P, NB])
        bpart = [sb(f"bpart{n}", [P, NB], BF16) for n in range(3)]
        B1, B2 = E * H1 // P, (E * H1 + E * C) // P
        rows_sb = sb("rows_sb", [P, 2 * C + E])
        ln0w, ln0b, br_sb = rows_sb[:, 0:C], rows_sb[:, C:2 * C], rows_sb[:, 2 * C:2 * C + E]
        dec = sb("dec", [P, 6])

        def col(n):
            return v_sb[:, n:n + 1]

        ident = sb("ident", [P, P])
        ones_bf = sb("ones_bf", [P, P], BF16)
        upper = sb("upper", [P, P], BF16)
        lane_i = sb("lane_i", [P, P], I32)
        lane_bf = sb("lane_bf", [P, P], BF16)
        lane_f = sb("lane_f", [P, P])
        part_i = sb("part_i", [P, 1], I32)
        part_f = sb("part_f", [P, 1])
        left_i = sb("left_i", [P, NJ], I32)
        left_bf = sb("left_bf", [P, NJ], BF16)
        thr_i = sb("thr_i", [P, NT], I32)
        thr_f = sb("thr_f", [P, NT])
        keep_first = sb("keep_first", [P, E])
        keep_i = sb("keep_i", [P, E], I32)
        scan_on = sb("scan_on", [P, E, NT])
        half = sb("half", [P, CT])
        wait_here = sb("wait_here", [1, 1])
        g_wait = sb("g_wait", [1, 3])

        lg = sb("lg", [P, NT, E])

        block_buffers = ExitStack()

        def tmp(name, shape, dt=F32):
            return block_buffers.enter_context(nc.sbuf_tensor(name, shape, dt))

        bst = {n: tmp(f"bst{n}", [P, CT, 6]) for n in "0123"}
        mv = {n: tmp(f"mv{n}", [P, CT, 2]) for n in "0123"}
        veps = {n: tmp(f"veps{n}", [P, CT]) for n in "0123"}
        rstd = {n: tmp(f"rstd{n}", [P, CT]) for n in "0123"}
        nmr = {n: tmp(f"nmr{n}", [P, CT]) for n in "0123"}
        z0 = tmp("z0", [P, CT, C])
        z0w = tmp("z0w", [P, CT, C])
        z1 = tmp("z1", [P, CT, C])
        hT = tmp("hT", [P, SQ, T + 1])
        pp = tmp("pp", [P, SQ, T + 1])
        ab = tmp("ab", [P, 2, SQ, T + 1])
        gap = tmp("gap", [P, 2, W])
        below_p = tmp("below_p", [P, 2, W])
        below_m = tmp("below_m", [P, 2, W])
        e_plus = tmp("e_plus", [P, 2, W])
        e_minus = tmp("e_minus", [P, 2, W])
        old_in_state, new_in_output = e_plus[:, 0, :], e_plus[:, 1, :]
        new_in_state, old_in_output = e_minus[:, 0, :], e_minus[:, 1, :]
        e2v = tmp("e2v", [P, W])
        new_v = tmp("new_v", [P, W])
        nd = tmp("nd", [P, 2, W])
        th = tmp("th", [P, W])
        rec = tmp("rec", [P, W])
        yT = tmp("yT", [P, W])
        x1c = tmp("x1c", [P, CT, C])
        z2 = tmp("z2", [P, CT, C])
        h2T = tmp("h2T", [P, SQ, T + 1])
        d2 = tmp("d2", [P, SQ, T])
        xk2 = tmp("xk2", [P, W])
        xr2 = tmp("xr2", [P, W])
        kf = tmp("kf", [P, HF, W])
        th2 = tmp("th2", [P, W])
        x2c = tmp("x2c", [P, W])
        x3c = tmp("x3c", [P, CT, C])
        xnc = tmp("xnc", [P, CT, C])
        xnTc = tmp("xnTc", [P, W])

        block_buffers.close()
        xn_all = sb("xn_all", [P, NT, C])
        bias_rows = sb("bias_rows", [P, E * H1 + E * C + C], BF16)
        top = [sb(f"top{k}", [P, NT]) for k in range(K)]
        which = sb("which", [P, NT])
        fall = sb("fall", [P, NT])
        rel = sb("rel", [P, NT])
        total = sb("total", [P, NT])
        wt = [sb(f"wt{k}", [P, NT]) for k in range(K)]
        ntl = sb("ntl", [P, E])
        cumt = sb("cumt", [P, E])
        start = sb("start", [P, E])
        slot = sb("slot", [P, K, NT])
        slot_i = sb("slot_i", [P, NJ], I32)
        lane_s = sb("lane_s", [P, NJ], I32)
        tile_s = sb("tile_s", [P, NJ], I32)
        lane_j = sb("lane_j", [P, NJ], BF16)
        tile_j = sb("tile_j", [P, NJ], BF16)
        owner_f = sb("owner_f", [1, TILES])
        owner = sb("owner", [1, TILES + 1], I32)
        oh_lane = sb("oh_lane", [P, JB, P], BF16)
        oh_tile = sb("oh_tile", [P, JB, TILES], BF16)
        tile_val = sb("tile_val", [P, JB, 2, TILES], BF16)
        row_f = sb("row_f", [P, TILES])
        row_g = sb("row_g", [P, TILES])
        row_out = sb("row_out", [P, TILES], U32)
        row_in = sb("row_in", [P, TILES], U32)
        gsh = sb("gsh", [P, HS, W])
        ash = sb("ash", [P, HS, W])
        routing_buffers = ExitStack()

        def scratch(name, shape, dt=F32):
            return routing_buffers.enter_context(nc.sbuf_tensor(name, shape, dt))

        sc_pos = scratch("sc_pos", [P, NT, E])
        eq = scratch("eq", [P, NT, E])
        pick = [scratch(f"pick{k}", [P, NT, E]) for k in range(K)]
        lg2 = scratch("lg2", [P, NT, E])
        sel = scratch("sel", [P, NT, E], BF16)
        tot = scratch("tot", [P, E, NT])
        incl = scratch("incl", [P, E, NT])
        more = scratch("more", [P, E, NT])
        before = scratch("before", [1, TILES, E])
        routing_buffers.close()
        xg = [sb(f"xg{m}", [P, C]) for m in range(U)]
        xT = [sb(f"xT{m}", [P, P]) for m in range(U)]
        gi = [sb(f"gi{m}", [P, 1], U32) for m in range(U)]
        si = [sb(f"si{m}", [P, 1], U32) for m in range(U)]
        gl = sb("gl", [P, HR])
        actv = sb("actv", [P, HR])
        actT = sb("actT", [P, HR])
        yo = [sb(f"yo{m}", [P, C]) for m in range(U)]
        fin = [gsh[:, m, :].rearrange("p (n c) -> p n c", c=C) for m in range(2)]
        fo = [ash[:, m, :].rearrange("p (n c) -> p n c", c=C) for m in range(2)]
        fst = [sb(f"fst{m}", [P, CT, 6]) for m in range(2)]
        fmv = [sb(f"fmv{m}", [P, CT, 2]) for m in range(2)]
        fve = [sb(f"fve{m}", [P, CT]) for m in range(2)]
        frs = [sb(f"frs{m}", [P, CT]) for m in range(2)]
        fnm = [sb(f"fnm{m}", [P, CT]) for m in range(2)]

        banks = [ctx.enter_context(nc.psum_tensor(f"bank{i}", [P, 512], F32)) for i in range(8)]
        pk, pv, pr, pT, pf0, pf1, pkv, po = banks
        pf = (pf0, pf1)

        s = {}
        for n in ("w_loaded mix_w_ready x_loaded consts pool_consts edges scaled parts parts_moved "
                  "bn0 bn1 bn2 bn3 pow0 pow1 pow2 pow3 nmr0 nmr1 nmr2 nmr3 "
                  "z0_ready z0w_ready x0_ready z1_ready hT_psum hT_ready k_ready v_ready r_ready "
                  "pp_ready delta_ready gaps_ready exp_plus exp_minus wkv_step y_half nd_ready den_ready th_ready yT_ready "
                  "po_ready x1_ready z2_ready h2_psum h2_ready d2_ready mixed2 fk_ready relu_done "
                  "sq_pool sq_act r2_ready th2_ready kv_ready x2_step x3_ready xn_ready xnT_psum xnT_ready "
                  "logits_psum logits_ready table_written xnT_kept expert_w_loaded iotas split").split():
            s[n] = sem(n)

        first_block = ExitStack()
        block = first_block.enter_context(nc.Block())

        L_WAITS = 15 * 16

        @block.sync
        def _(sp):
            sp.dma_start(x_all[:, 0:CT, :], x_v[:, 0:CT, :]).then_inc(s["x_loaded"], 16)
            sp.dma_start(rows_sb[:, :], rows.partition_broadcast(P)).then_inc(s["w_loaded"], 16)
            sp.dma_start(v_sb[:, :], vecs).then_inc(s["w_loaded"], 16)
            sp.dma_start(sq_sb[:, :, :], sqw.rearrange("s p c -> p s c")).then_inc(s["w_loaded"], 16)
            sp.dma_start(wfk_sb[:, :], wfk).then_inc(s["w_loaded"], 16)
            sp.dma_start(wfv_sb[:, :, :], wfv.rearrange("(j p) c -> p j c", p=P)).then_inc(s["w_loaded"], 16)
            sp.dma_start(wrt_sb[:, :], wrt).then_inc(s["w_loaded"], 16)
            with sp.Fori(1, CH) as c:
                sp.wait_ge(s["x_loaded"], c * 16)
                sp.dma_start(x_all[:, ds(c * CT, CT), :], x_v[:, ds(c * CT, CT), :]).then_inc(s["x_loaded"], 16)
            for to, of in ((braw[:, 0:B1], be1.rearrange("e h -> (e h)").rearrange("(p a) -> p a", a=B1)),
                           (braw[:, B1:B2], be2.rearrange("e h -> (e h)").rearrange("(p a) -> p a", a=B2 - B1)),
                           (braw[:, B2:NB], bs2.rearrange("(p a) -> p a", a=NB - B2)),
                           (ws1_sb[:, :], ws1), (ws2_sb[:, :, :], ws2.rearrange("(j p) c -> p j c", p=P)),
                           (we1_sb[:, :, :], we1.rearrange("e d h -> d e h")),
                           (we2_sb[:, :, :, :], we2.rearrange("e (j p) c -> p e j c", p=P))):
                sp.dma_start(to, of).then_inc(s["expert_w_loaded"], 16)
            with sp.Fori(0, CH) as c:
                sp.wait_ge(s["xn_ready"], c + 1)
                sp.dma_start(table_v[:, ds(c * CT, CT), :], xnc[:, :, :]).then_inc(s["table_written"], 16)
                sp.wait_ge(s["xnT_ready"], c + 1)
                sp.dma_start(xnT_all[:, ds(c * W, W)], xnTc[:, :]).then_inc(s["xnT_kept"], 16)

        def stages(eng, turn):
            for i in range(4):
                turn(i, i, *[i - n if i >= n else None for n in (1, 2, 3)])
            with eng.Fori(4, CH) as i:
                turn(i, i, i - 1, i - 2, i - 3)
            for i in range(CH, CH + 3):
                turn(i, *[i - n if i - n < CH else None for n in (0, 1, 2, 3)])

        def after(eng, name, count):
            if not (isinstance(count, int) and count <= 0):
                eng.wait_ge(s[name], count)

        def upto(i, most):
            return min(i, most) if isinstance(i, int) else i

        @block.vector
        def _(v):
            nv = nc.vector
            nv.memset(hT[:, :, 0:1], 0.0)
            nv.memset(h2T[:, :, 0:1], 0.0)
            nv.memset(pp[:, :, 0:1], NEG)
            nv.memset(ab[:, :, :, 0:1], 0.0)
            nv.memset(ones_bf[:, :], 1.0)
            nv.memset(scan_on[:, :, :], 1.0)
            nv.memset(half[:, :], -0.5).then_inc(s["edges"], 1)
            v.wait_ge(s["w_loaded"], 6 * 16)
            nv.tensor_scalar(dec[:, 2:5], v_sb[:, TMK:TMR + 1], -1.0, 1.0, ALU.mult, ALU.add).then_inc(s["scaled"], 1)
            v.wait_ge(s["scaled"], 1)
            for n in range(3):
                nv.tensor_scalar(mixa[:, n, :], sq_sb[:, n, :], col(TMK + n), None, ALU.mult)
                last = nv.tensor_scalar(mixb[:, n, :], sq_sb[:, n, :], dec[:, 2 + n:3 + n], None, ALU.mult)
            last.then_inc(s["mix_w_ready"], 1)
            v.wait_ge(s["consts"], 1)
            nv.tensor_scalar(dec[:, 0:1], dec[:, 5:6], -1.0, None, ALU.mult).then_inc(s["scaled"], 1)
            v.wait_ge(s["scaled"], 2)
            nv.memset(scan_on[:, :, 0:1], 0.0)
            v.wait_ge(s["iotas"], 1)
            nv.tensor_copy(lane_bf[:, :], lane_i[:, :])
            nv.tensor_copy(lane_f[:, :], lane_i[:, :])
            nv.tensor_copy(part_f[:, :], part_i[:, :])
            nv.tensor_copy(left_bf[:, :], left_i[:, :])
            nv.tensor_copy(thr_f[:, :], thr_i[:, :])
            nv.tensor_copy(keep_first[:, :], keep_i[:, :]).then_inc(s["scaled"], 1)

            def stats(n, tiles, c):
                bn = s["bn" + n]
                for t in range(CT):
                    last = nv.bn_stats(bst[n][:, t, :], tiles[:, t, :])
                last.then_inc(bn, 1)
                v.wait_ge(bn, c * 3 + 1)
                nv.memset(wait_here[:, :], 0.0)
                for t in range(CT):
                    last = nv.bn_aggr(mv[n][:, t, :], bst[n][:, t, :])
                last.then_inc(bn, 1)
                v.wait_ge(bn, c * 3 + 2)
                nv.tensor_scalar(veps[n][:, :], mv[n][:, :, 1], EPS, None, ALU.add).then_inc(bn, 1)

            def offset(n, c):
                v.wait_ge(s["pow" + n], c + 1)
                nv.scalar_tensor_tensor(nmr[n][:, :], mv[n][:, :, 0], -1.0, rstd[n][:, :],
                                        ALU.mult, ALU.mult).then_inc(s["nmr" + n], 1)

            def turn(i, c1, c2, c3, c4):
                if c3 is not None:
                    after(v, "x2_step", c3 * 2)
                    after(v, "nmr2", c3)
                    v.wait_ge(s["po_ready"], c3 + 1)
                    nv.tensor_tensor(x1c[:, :, :], x0_all[:, ds(c3 * CT, CT), :],
                                     po[:, :].rearrange("p (n c) -> p n c", c=C), ALU.add).then_inc(s["x1_ready"], 1)
                    v.wait_ge(s["x1_ready"], c3 + 1)
                    stats("2", x1c, c3)
                if c4 is not None:
                    after(v, "nmr3", c4)
                    v.wait_ge(s["x3_ready"], c4 + 1)
                    stats("3", x3c, c4)
                if c3 is not None:
                    after(v, "z2_ready", c3)
                    offset("2", c3)
                if c2 is not None:
                    after(v, "yT_ready", c2)
                    v.wait_ge(s["k_ready"], c2 + 1)
                    for q in range(SQ):
                        last = nv.tensor_tensor_scan(pp[:, q, 1:T + 1], dec[:, 0:1].to_broadcast([P, T]),
                                                     pk[:, q * T:(q + 1) * T], NEG, ALU.add, ALU.max)
                    last.then_inc(s["pp_ready"], 1)
                    v.wait_ge(s["pp_ready"], c2 + 1)
                    nv.scalar_tensor_tensor(gap[:, 0, :].rearrange("p (q t) -> p q t", t=T), pp[:, :, 0:T], dec[:, 0:1],
                                            pk[:, :].rearrange("p (q t) -> p q t", t=T), ALU.add, ALU.subtract)
                    nv.scalar_tensor_tensor(gap[:, 1, :].rearrange("p (q t) -> p q t", t=T),
                                            pk[:, :].rearrange("p (q t) -> p q t", t=T), col(FIRST), pp[:, :, 0:T],
                                            ALU.add, ALU.subtract).then_inc(s["delta_ready"], 1)
                    v.wait_ge(s["delta_ready"], c2 + 1)
                    after(v, "exp_minus", c2)
                    nv.tensor_scalar(below_p[:, :, :], gap[:, :, :], 0.0, None, ALU.min)
                    nv.tensor_scalar(below_m[:, :, :], gap[:, :, :], 0.0, None, ALU.max).then_inc(s["gaps_ready"], 1)
                if c4 is not None:
                    after(v, "xn_ready", c4)
                    offset("3", c4)
                if c1 is not None:
                    after(v, "nmr0", c1)
                    v.wait_ge(s["x_loaded"], (c1 + 1) * 16)
                    stats("0", x_all[:, ds(c1 * CT, CT), :], c1)
                if c2 is not None:
                    v.wait_ge(s["exp_plus"], c2 + 1)
                    v.wait_ge(s["exp_minus"], c2 + 1)
                    v.wait_ge(s["v_ready"], c2 + 1)
                    after(v, "den_ready", c2)
                    nv.tensor_tensor(e2v[:, :], new_in_state, pv[:, :], ALU.mult).then_inc(s["wkv_step"], 1)
                    nv.tensor_tensor(new_v[:, :], new_in_output, pv[:, :], ALU.mult).then_inc(s["wkv_step"], 1)
                    v.wait_ge(s["wkv_step"], c2 * 3 + 1)
                    for q in range(SQ):
                        at = slice(q * T, (q + 1) * T)
                        nv.tensor_tensor_scan(ab[:, 0, q, 1:T + 1], old_in_state[:, at], e2v[:, at], 0.0, ALU.mult, ALU.add)
                        last = nv.tensor_tensor_scan(ab[:, 1, q, 1:T + 1], old_in_state[:, at], new_in_state[:, at], 0.0,
                                                     ALU.mult, ALU.add)
                    last.then_inc(s["wkv_step"], 1)
                    v.wait_ge(s["wkv_step"], c2 * 3 + 3)
                    for n in range(2):
                        last = nv.tensor_tensor(nd[:, n, :].rearrange("p (q t) -> p q t", t=T), ab[:, n, :, 0:T],
                                                old_in_output.rearrange("p (q t) -> p q t", t=T), ALU.mult)
                    last.then_inc(s["nd_ready"], 1)
                if c1 is not None:
                    after(v, "z0_ready", c1)
                    offset("0", c1)
                if c3 is not None:
                    v.wait_ge(s["d2_ready"], c3 + 1)
                    after(v, "r2_ready", c3)
                    for m, to in ((CMK, xk2), (CMR, xr2)):
                        last = nv.scalar_tensor_tensor(to[:, :].rearrange("p (q t) -> p q t", t=T), d2[:, :, :], col(m),
                                                       h2T[:, :, 0:T], ALU.mult, ALU.add)
                    last.then_inc(s["mixed2"], 1)
                if c2 is not None:
                    v.wait_ge(s["den_ready"], c2 + 1)
                    nv.reciprocal(rec[:, :], nd[:, 1, :]).then_inc(s["y_half"], 1)
                    v.wait_ge(s["th_ready"], c2 + 1)
                    after(v, "po_ready", c2)
                    nv.scalar_tensor_tensor(yT[:, :], th[:, :], 1.0, nd[:, 0, :], ALU.add, ALU.mult).then_inc(s["y_half"], 1)
                    v.wait_ge(s["y_half"], c2 * 2 + 2)
                    nv.scalar_tensor_tensor(yT[:, :], yT[:, :], 0.5, rec[:, :], ALU.mult, ALU.mult).then_inc(s["yT_ready"], 1)
                if c1 is not None:
                    after(v, "nmr1", c1)
                    v.wait_ge(s["x0_ready"], c1 + 1)
                    stats("1", x0_all[:, ds(c1 * CT, CT), :], c1)
                if c4 is not None:
                    v.wait_ge(s["logits_psum"], c4 + 1)
                    nv.tensor_tensor(lg[:, ds(c4 * CT, CT), :], pT[:, 0:CT * E].rearrange("p (n e) -> p n e", e=E),
                                     br_sb.unsqueeze(1).to_broadcast([P, CT, E]), ALU.add).then_inc(s["logits_ready"], 1)
                if c1 is not None:
                    after(v, "z1_ready", c1)
                    offset("1", c1)
                if c3 is not None:
                    v.wait_ge(s["th2_ready"], c3 + 1)
                    v.wait_ge(s["kv_ready"], c3 + 1)
                    after(v, "x3_ready", c3)
                    nv.scalar_tensor_tensor(x2c[:, :], th2[:, :], 1.0, pkv[:, :], ALU.add, ALU.mult).then_inc(s["x2_step"], 1)
                    v.wait_ge(s["x2_step"], c3 * 2 + 1)
                    nv.scalar_tensor_tensor(x2c[:, :], x2c[:, :], 0.5, x1c[:, :, :].rearrange("p n c -> p (n c)"),
                                            ALU.mult, ALU.add).then_inc(s["x2_step"], 1)

            stages(v, turn)

        @block.scalar
        def _(a):
            na = nc.scalar
            a.wait_ge(s["w_loaded"], 6 * 16)
            na.activation(dec[:, 5:6], col(DECAY), ACT.Exp).then_inc(s["consts"], 1)

            def apply(n, to, of):
                for t in range(CT):
                    last = na.activation(to[:, t, :], of[:, t, :], ACT.Identity,
                                         bias=nmr[n][:, t:t + 1], scale=rstd[n][:, t:t + 1])
                return last

            def turn(i, c1, c2, c3, c4):
                if c3 is not None:
                    v1 = c3 + 1
                    a.wait_ge(s["nmr2"], v1)
                    after(a, "h2_psum", c3)
                    apply("2", z2, x1c).then_inc(s["z2_ready"], 1)
                if c4 is not None:
                    a.wait_ge(s["nmr3"], c4 + 1)
                    after(a, "xnT_psum", c4)
                    after(a, "table_written", c4 * 16)
                    apply("3", xnc, x3c).then_inc(s["xn_ready"], 1)
                if c2 is not None:
                    a.wait_ge(s["gaps_ready"], c2 + 1)
                    after(a, "yT_ready", c2)
                    na.activation(e_minus[:, :, :], below_m[:, :, :], ACT.Exp, scale=-1.0).then_inc(s["exp_minus"], 1)
                    na.activation(e_plus[:, :, :], below_p[:, :, :], ACT.Exp).then_inc(s["exp_plus"], 1)
                if c3 is not None:
                    a.wait_ge(s["h2_psum"], c3 + 1)
                    after(a, "mixed2", c3)
                    na.activation(h2T[:, :, 1:T + 1], pT[:, :].rearrange("p (q t) -> p q t", t=T), ACT.Identity,
                                  bias=col(LN2B), scale=col(LN2W)).then_inc(s["h2_ready"], 1)
                if c1 is not None:
                    a.wait_ge(s["nmr0"], c1 + 1)
                    after(a, "z0w_ready", c1)
                    apply("0", z0, x_all[:, ds(c1 * CT, CT), :]).then_inc(s["z0_ready"], 1)
                if c2 is not None:
                    a.wait_ge(s["r_ready"], c2 + 1)
                    na.activation(th[:, :], pr[:, :], ACT.Tanh, scale=0.5).then_inc(s["th_ready"], 1)
                if c4 is not None:
                    a.wait_ge(s["xnT_psum"], c4 + 1)
                    after(a, "logits_psum", c4)
                    after(a, "xnT_kept", c4 * 16)
                    na.activation(xnTc[:, :], pT[:, :], ACT.Copy).then_inc(s["xnT_ready"], 1)
                if c3 is not None:
                    after(a, "kv_ready", c3)
                    for j in range(HF):
                        a.wait_ge(s["fk_ready"], c3 * HF + j + 1)
                        na.activation(kf[:, j, :], pf[j % 2][:, :], ACT.Relu).then_inc(s["relu_done"], 1)
                        if j % 2:
                            a.wait_ge(s["relu_done"], c3 * HF + j + 1)
                            na.activation(kf[:, j, :], kf[:, j, :], ACT.Square).then_inc(s["sq_act"], 1)
                    a.wait_ge(s["r2_ready"], c3 + 1)
                    after(a, "x2_step", c3 * 2)
                    na.activation(th2[:, :], pr[:, :], ACT.Tanh, scale=0.5).then_inc(s["th2_ready"], 1)
                if c1 is not None:
                    a.wait_ge(s["nmr1"], c1 + 1)
                    after(a, "hT_psum", c1)
                    apply("1", z1, x0_all[:, ds(c1 * CT, CT), :]).then_inc(s["z1_ready"], 1)
                    a.wait_ge(s["hT_psum"], c1 + 1)
                    after(a, "r_ready", c1)
                    na.activation(hT[:, :, 1:T + 1], pT[:, :].rearrange("p (q t) -> p q t", t=T), ACT.Identity,
                                  bias=col(LN1B), scale=col(LN1W)).then_inc(s["hT_ready"], 1)

            stages(a, turn)

        @block.gpsimd
        def _(g):
            ng = nc.gpsimd
            ng.memset(ident[:, :], 0.0).then_inc(s["pool_consts"], 1)
            g.wait_ge(s["pool_consts"], 1)
            ng.affine_select(out=ident[:, :], in_=ident[:, :], compare_op=ALU.not_equal, fill=1.0,
                             base=0, pattern=[[-1, P]], channel_multiplier=1).then_inc(s["pool_consts"], 1)
            g.wait_ge(s["edges"], 1)
            ng.affine_select(out=upper[:, :], in_=ones_bf[:, :], compare_op=ALU.is_gt, fill=0.0,
                             base=0, pattern=[[1, P]], channel_multiplier=-1)
            ng.iota(lane_i[:, :], pattern=[[1, P]], base=0, channel_multiplier=0)
            ng.iota(part_i[:, :], pattern=[[1, 1]], base=0, channel_multiplier=1)
            ng.iota(left_i[:, :], pattern=[[-1, NJ]], base=NJ, channel_multiplier=0)
            ng.iota(thr_i[:, :], pattern=[[P, NT]], base=0, channel_multiplier=0)
            ng.iota(keep_i[:, :], pattern=[[-1, E]], base=E, channel_multiplier=0).then_inc(s["iotas"], 1)
            g.wait_ge(s["w_loaded"], 6 * 16)

            def power(n, c):
                g.wait_ge(s["bn" + n], c * 3 + 3)
                after(g, "nmr" + n, c)
                ng.tensor_tensor(rstd[n][:, :], veps[n][:, :], half[:, :], ALU.pow).then_inc(s["pow" + n], 1)

            def turn(i, c1, c2, c3, c4):
                if c3 is not None:
                    after(g, "z2_ready", c3)
                    power("2", c3)
                if c4 is not None:
                    after(g, "xn_ready", c4)
                    power("3", c4)
                if c1 is not None:
                    after(g, "z0_ready", c1)
                    power("0", c1)
                if c3 is not None:
                    g.wait_ge(s["h2_ready"], c3 + 1)
                    after(g, "mixed2", c3)
                    ng.tensor_tensor(d2[:, :, :], h2T[:, :, 1:T + 1], h2T[:, :, 0:T], ALU.subtract).then_inc(s["d2_ready"], 1)
                if c2 is not None:
                    g.wait_ge(s["nd_ready"], c2 + 1)
                    g.wait_ge(s["wkv_step"], c2 * 3 + 3)
                    ng.tensor_tensor(nd[:, 0, :], nd[:, 0, :], new_v[:, :], ALU.add)
                    ng.tensor_tensor(nd[:, 1, :], nd[:, 1, :], new_in_output, ALU.add).then_inc(s["den_ready"], 1)
                if c1 is not None:
                    g.wait_ge(s["z0_ready"], c1 + 1)
                    after(g, "x0_ready", c1)
                    ng.tensor_tensor(z0w[:, :, :], z0[:, :, :], ln0w.unsqueeze(1).to_broadcast([P, CT, C]),
                                     ALU.mult).then_inc(s["z0w_ready"], 1)
                    g.wait_ge(s["z0w_ready"], c1 + 1)
                    ng.tensor_tensor(x0_all[:, ds(c1 * CT, CT), :], z0w[:, :, :],
                                     ln0b.unsqueeze(1).to_broadcast([P, CT, C]), ALU.add).then_inc(s["x0_ready"], 1)
                if c3 is not None:
                    for j in range(0, HF, 2):
                        g.wait_ge(s["relu_done"], c3 * HF + j + 1)
                        ng.tensor_tensor(kf[:, j, :], kf[:, j, :], kf[:, j, :], ALU.mult).then_inc(s["sq_pool"], 1)
                if c1 is not None:
                    after(g, "z1_ready", c1)
                    power("1", c1)
                if c3 is not None:
                    g.wait_ge(s["x2_step"], c3 * 2 + 2)
                    after(g, "xn_ready", c3)
                    ng.tensor_tensor(x3c[:, :, :], x2c[:, :].rearrange("p (n c) -> p n c", c=C),
                                     x_all[:, ds(c3 * CT, CT), :], ALU.add).then_inc(s["x3_ready"], 1)

            stages(g, turn)

        @block.tensor
        def _(t):
            nt = nc.tensor
            t.wait_ge(s["w_loaded"], 6 * 16)
            t.wait_ge(s["mix_w_ready"], 1)
            t.wait_ge(s["pool_consts"], 2)
            t.wait_ge(s["edges"], 1)

            def turned(of):
                for n in range(CT):
                    last = nt.transpose(pT[:, n * P:(n + 1) * P], of[:, n, :], ident[:, :])
                return last

            def turn(i, c1, c2, c3, c4):
                if c2 is not None:
                    t.wait_ge(s["hT_ready"], c2 + 1)
                    for n, (to, name, free, count) in enumerate((
                            (pk, "k_ready", "delta_ready", c2), (pv, "v_ready", "wkv_step", c2 * 3),
                            (pr, "r_ready", "th_ready", c2))):
                        after(t, free, count)
                        if n == 2 and not (isinstance(i, int) and i < 3):
                            after(t, "th2_ready", upto(i, CH + 2) - 2)
                        o = to[:, :].rearrange("p (q t) -> p q t", t=T)
                        nt.matmul(o, mixa[:, n, :], hT[:, :, 1:T + 1], start=True, stop=False)
                        nt.matmul(o, mixb[:, n, :], hT[:, :, 0:T], start=False, stop=True).then_inc(s[name], 1)
                if c3 is not None:
                    t.wait_ge(s["z2_ready"], c3 + 1)
                    after(t, "hT_ready", upto(i, CH))
                    after(t, "logits_ready", c3 - 1)
                    turned(z2).then_inc(s["h2_psum"], 1)
                if c4 is not None:
                    t.wait_ge(s["xn_ready"], c4 + 1)
                    after(t, "h2_ready", upto(i - 1, CH))
                    after(t, "logits_ready", c4)
                    turned(xnc).then_inc(s["xnT_psum"], 1)
                if c3 is not None:
                    t.wait_ge(s["mixed2"], c3 + 1)
                    for j in range(HF):
                        after(t, "relu_done", c3 * HF + (j - 1))
                        nt.matmul(pf[j % 2][:, :], wfk_sb[:, j * P:(j + 1) * P], xk2[:, :],
                                  start=True, stop=True).then_inc(s["fk_ready"], 1)
                    after(t, "th_ready", upto(i, CH))
                    for n in range(CT):
                        last = nt.matmul(pr[:, n * P:(n + 1) * P], xr2[:, n * P:(n + 1) * P], sq_sb[:, 4, :],
                                         start=True, stop=True)
                    last.then_inc(s["r2_ready"], 1)
                if c4 is not None:
                    t.wait_ge(s["xnT_ready"], c4 + 1)
                    for n in range(CT):
                        last = nt.matmul(pT[:, n * E:(n + 1) * E], xnTc[:, n * P:(n + 1) * P], wrt_sb[:, :],
                                         start=True, stop=True)
                    last.then_inc(s["logits_psum"], 1)
                if c3 is not None:
                    t.wait_ge(s["sq_act"], (c3 + 1) * (HF // 2))
                    t.wait_ge(s["sq_pool"], (c3 + 1) * (HF // 2))
                    after(t, "x2_step", c3 * 2)
                    for n in range(CT):
                        for j in range(HF):
                            last = nt.matmul(pkv[:, n * P:(n + 1) * P], kf[:, j, n * P:(n + 1) * P], wfv_sb[:, j, :],
                                             start=j == 0, stop=j == HF - 1)
                    last.then_inc(s["kv_ready"], 1)
                if c2 is not None:
                    t.wait_ge(s["yT_ready"], c2 + 1)
                    after(t, "x1_ready", c2)
                    for n in range(CT):
                        last = nt.matmul(po[:, n * P:(n + 1) * P], yT[:, n * P:(n + 1) * P], sq_sb[:, 3, :],
                                         start=True, stop=True)
                    last.then_inc(s["po_ready"], 1)
                if c1 is not None:
                    t.wait_ge(s["z1_ready"], c1 + 1)
                    after(t, "hT_ready", c1)
                    if c3 is not None:
                        t.wait_ge(s["h2_ready"], c3 + 1)
                    if c4 is not None:
                        t.wait_ge(s["logits_ready"], c4 + 1)
                    turned(z1).then_inc(s["hT_psum"], 1)

            stages(t, turn)

        s2 = {}
        for n in ("route prefix_ready totals_ready fall_exp gap_ready slots_ready rows_zero rows_moved xn_loaded "
                  "lanes_ready tiles_step tiles_ready map_used map_ready rows_step rows_ready owner_ready split "
                  "sh_gate sh_up sh_gelu sh_act sh_out sh_added "
                  "ready_gi ready_si xT_psum xT_ready gate_ready up_ready gelu_ready act_ready actT_psum "
                  "actT_ready y_ready yo_ready "
                  "gather_begun scatter_begun fin_sum fin_ready fin_pow fin_nmr fin_out").split():
            s2[n] = sem("e_" + n)
        gathered = [sem(f"gathered{m}") for m in range(U)]
        scattered = [sem(f"scattered{m}") for m in range(U)]
        y_loaded = [sem(f"y_loaded{m}") for m in range(2)]
        stored = [sem(f"stored{m}") for m in range(2)]
        LAST = TILES // U - 1

        ps_a, ps_g, ps_t, ps_y, ps_x = banks[0], banks[1], banks[2], banks[3], banks[4]
        sh_ps = banks[0:2 * HS]
        sh_y, ps_map, ps_pre, ps_tot = banks[4], banks[5], banks[6], banks[7]

        first_block.close()
        experts = ctx.enter_context(nc.Block())

        @experts.sync
        def _(sp):
            sp.wait_ge(s["table_written"], CH * 16)
            sp.wait_ge(s["xnT_kept"], CH * 16)
            sp.dma_start(xn_all[:, :, :], table_v).then_inc(s2["xn_loaded"], 16)
            sp.wait_ge(s2["rows_zero"], 2)
            sp.wait_ge(s2["split"], 5)
            for n in range(3):
                for lo, hi, base in ((0, B1, 0), (B1, B2, BE2), (B2, NB, BS2)):
                    sp.dma_start(bias_rows[n:n + 1, base:base + (hi - lo) * P],
                                 bpart[n][:, lo:hi]).then_inc(s2["rows_moved"], 16)
            for m in range(U):
                sp.wait_ge(scattered[m], (LAST + 1) * 16)

            def load(c, m):
                sp.dma_start(y_first[:, ds(c * CT, CT), :], routed_v[:, 0, ds(c * CT, CT), :]).then_inc(y_loaded[m], 16)
                sp.dma_start(y_second[:, ds(c * CT, CT), :], routed_v[:, 1, ds(c * CT, CT), :]).then_inc(y_loaded[m], 16)

            load(0, 0)
            load(1, 1)
            with sp.Fori(1, CH // 2) as r:
                for m in range(2):
                    sp.wait_ge(y_loaded[m], r * 32)
                    load(r * 2 + m, m)

        def tiles(eng, group):
            group(0)
            with eng.Fori(1, LAST) as r:
                group(r)
            group(LAST)

        def after2(eng, name, count):
            if not (isinstance(count, int) and count <= 0):
                eng.wait_ge(name if not isinstance(name, str) else s2[name], count)

        def halves(eng, step):
            step(0)
            with eng.Fori(1, CH // 2) as r:
                step(r)

        @experts.gpsimd
        def _(g):
            ng = nc.gpsimd
            ng.memset(bias_rows[:, :], 0.0).then_inc(s2["rows_zero"], 1)

            def take_wait(at, name, n):
                after2(g, name, n)
                ng.tensor_tensor(g_wait[:, at:at + 1], g_wait[:, 0:1], g_wait[:, 0:1], ALU.add).then_inc(s2[name], 1)

            ng.memset(g_wait[:, :], 0.0).then_inc(s2["rows_zero"], 1)
            g.wait_ge(s2["rows_zero"], 2)

            def gather(m, n):
                after2(g, "xT_psum", n - U + 1)
                g.wait_ge(s2["ready_gi"], n + 1)
                take_wait(1, "gather_begun", n)
                ng.indirect_dma_start(xg[m][:, :], None, table,
                                      bass.IndirectOffsetOnAxis(ap=gi[m][:, 0:1], axis=0)).then_inc(gathered[m], 16)

            def scatter(m, n):
                g.wait_ge(s2["yo_ready"], n + 1)
                take_wait(2, "scatter_begun", n)
                ng.indirect_dma_start(routed, bass.IndirectOffsetOnAxis(ap=si[m][:, 0:1], axis=0), yo[m][:, :], None,
                                      bounds_check=SLOTS - 1, oob_is_err=False).then_inc(scattered[m], 16)

            for m in range(U):
                gather(m, m)

            def group(r):
                for m in range(U):
                    if not (isinstance(r, int) and r == LAST):
                        gather(m, r * U + m + U)
                    scatter(m, r * U + m)

            tiles(g, group)

            def step(r):
                for m in range(2):
                    g.wait_ge(s2["fin_ready"], (r * 2 + m) * 3 + 3)
                    after2(g, "fin_out", (r - 1) * 2 + m + 1)
                    ng.tensor_tensor(frs[m][:, :], fve[m][:, :], half[:, :], ALU.pow).then_inc(s2["fin_pow"], 1)

            halves(g, step)

        @experts.vector
        def _(v):
            nv = nc.vector
            done = [0]

            def routed_by(ins):
                done[0] += 1
                ins.then_inc(s2["route"], 1)
                v.wait_ge(s2["route"], done[0])

            v.wait_ge(s["expert_w_loaded"], 7 * 16)
            for n, (of, to) in enumerate(((braw, bleft), (bleft, bleft2))):
                nv.tensor_copy(bpart[n][:, :], of[:, :]).then_inc(s2["split"], 1)
                v.wait_ge(s2["split"], 2 * n + 1)
                nv.tensor_tensor(to[:, :], of[:, :], bpart[n][:, :], ALU.subtract).then_inc(s2["split"], 1)
                v.wait_ge(s2["split"], 2 * n + 2)
            nv.tensor_copy(bpart[2][:, :], bleft2[:, :]).then_inc(s2["split"], 1)

            def over(ap, n):
                return ap.unsqueeze(2).to_broadcast([P, ap.shape[1], n])

            def under(ap, n):
                return ap.unsqueeze(1).to_broadcast([P, n, ap.shape[1]])

            for k, of in enumerate((lg, lg2)):
                routed_by(nv.tensor_reduce(top[k][:, :], of[:, :, :], AX.X, ALU.max))
                routed_by(nv.tensor_tensor(eq[:, :, :], of[:, :, :], over(top[k][:, :], E), ALU.is_equal))
                routed_by(nv.tensor_tensor(eq[:, :, :], eq[:, :, :], under(keep_first[:, :], NT), ALU.mult))
                routed_by(nv.tensor_reduce(which[:, :], eq[:, :, :], AX.X, ALU.max))
                routed_by(nv.tensor_tensor(pick[k][:, :, :], under(keep_first[:, :], NT), over(which[:, :], E), ALU.is_equal))
                if k == 0:
                    routed_by(nv.scalar_tensor_tensor(lg2[:, :, :], pick[0][:, :, :], -1e30, lg[:, :, :], ALU.mult, ALU.add))
            nv.tensor_tensor(fall[:, :], top[1][:, :], top[0][:, :], ALU.subtract).then_inc(s2["gap_ready"], 1)
            routed_by(nv.tensor_tensor(sel[:, :, :], pick[0][:, :, :], pick[1][:, :, :], ALU.add))
            v.wait_ge(s2["totals_ready"], 1)
            routed_by(nv.tensor_copy(tot[:, :, :], ps_tot[:, 0:NT * E].rearrange("p (n e) -> p e n", e=E)))
            routed_by(nv.tensor_tensor_scan(incl[:, :, :].rearrange("p e n -> p (e n)"),
                                            scan_on[:, :, :].rearrange("p e n -> p (e n)"),
                                            tot[:, :, :].rearrange("p e n -> p (e n)"), 0.0, ALU.mult, ALU.add))
            routed_by(nv.tensor_tensor(more[:, :, :], over(incl[:, :, NT - 1], NT), under(thr_f[:, :], E), ALU.is_gt))
            routed_by(nv.tensor_reduce(ntl[:, :], more[:, :, :], AX.X, ALU.add))
            routed_by(nv.tensor_tensor_scan(cumt[:, :], scan_on[:, 0, 1:E + 1], ntl[:, :], 0.0, ALU.mult, ALU.add))
            routed_by(nv.tensor_tensor(start[:, :], cumt[:, :], ntl[:, :], ALU.subtract))
            routed_by(nv.tensor_scalar(start[:, :], start[:, :], float(P), None, ALU.mult))
            routed_by(nv.tensor_tensor(more[:, :, :], incl[:, :, :], tot[:, :, :], ALU.subtract))
            routed_by(nv.tensor_tensor(more[:, :, :], more[:, :, :], over(start[:, :], NT), ALU.add))
            v.wait_ge(s2["prefix_ready"], 1)
            routed_by(nv.tensor_tensor(sc_pos[:, :, :], ps_pre[:, 0:NT * E].rearrange("p (n e) -> p n e", e=E),
                                       more[:, :, :].rearrange("p e n -> p n e"), ALU.add))
            for k in range(K):
                routed_by(nv.tensor_tensor(eq[:, :, :], pick[k][:, :, :], sc_pos[:, :, :], ALU.mult))
                routed_by(nv.tensor_reduce(slot[:, k, :], eq[:, :, :], AX.X, ALU.add))
            routed_by(nv.tensor_copy(slot_i[:, :], slot[:, :, :].rearrange("p k n -> p (k n)")))
            routed_by(nv.tensor_scalar(tile_s[:, :], slot_i[:, :], P.bit_length() - 1, None, ALU.arith_shift_right))
            routed_by(nv.tensor_scalar(lane_s[:, :], slot_i[:, :], P - 1, None, ALU.bitwise_and))
            routed_by(nv.tensor_copy(tile_j[:, :], tile_s[:, :]))
            routed_by(nv.tensor_copy(lane_j[:, :], lane_s[:, :]))
            routed_by(nv.tensor_tensor(before[:, :, :], cumt[0:1, :].unsqueeze(1).to_broadcast([1, TILES, E]),
                                       lane_f[0:1, 0:TILES].unsqueeze(2).to_broadcast([1, TILES, E]), ALU.is_le))
            routed_by(nv.tensor_reduce(owner_f[:, :], before[:, :, :], AX.X, ALU.add))
            routed_by(nv.tensor_scalar(owner_f[:, :], owner_f[:, :], float(E - 1), None, ALU.min))
            nv.tensor_copy(owner[0:1, 0:TILES], owner_f[:, :]).then_inc(s2["owner_ready"], 1)
            v.wait_ge(s2["fall_exp"], 1)
            routed_by(nv.tensor_scalar(total[:, :], rel[:, :], 1.0, None, ALU.add))
            routed_by(nv.reciprocal(wt[0][:, :], total[:, :]))
            routed_by(nv.tensor_tensor(wt[1][:, :], rel[:, :], wt[0][:, :], ALU.mult))
            v.wait_ge(s2["xn_loaded"], 16)

            def map_batch(q):
                after2(v, "map_used", q)
                nv.tensor_tensor(oh_lane[:, :, :], lane_j[:, ds(q * JB, JB)].unsqueeze(2).to_broadcast([P, JB, P]),
                                 lane_bf[:, :].unsqueeze(1).to_broadcast([P, JB, P]), ALU.is_equal)
                nv.tensor_tensor(oh_tile[:, :, :], tile_j[:, ds(q * JB, JB)].unsqueeze(2).to_broadcast([P, JB, TILES]),
                                 lane_bf[:, 0:TILES].unsqueeze(1).to_broadcast([P, JB, TILES]),
                                 ALU.is_equal).then_inc(s2["tiles_step"], 1)
                v.wait_ge(s2["tiles_step"], q + 1)
                nv.tensor_scalar(tile_val[:, :, 0, :], oh_tile[:, :, :], part_f[:, 0:1], None, ALU.mult)
                nv.tensor_tensor(tile_val[:, :, 1, :], oh_tile[:, :, :],
                                 left_bf[:, ds(q * JB, JB)].unsqueeze(2).to_broadcast([P, JB, TILES]),
                                 ALU.mult).then_inc(s2["tiles_ready"], 1)

            def shared_act(c):
                for j in range(HS):
                    v.wait_ge(s2["sh_gelu"], c * HS + j + 1)
                    v.wait_ge(s2["sh_up"], c * HS + j + 1)
                    if j == 0:
                        after2(v, "sh_out", c)
                    nv.scalar_tensor_tensor(ash[:, j, :], sh_ps[j][:, :], col(BS1 + j), gsh[:, j, :],
                                            ALU.add, ALU.mult).then_inc(s2["sh_act"], 1)

            def shared_add(c):
                v.wait_ge(s2["sh_out"], c + 1)
                nv.tensor_tensor(x_all[:, ds(c * CT, CT), :], xn_all[:, ds(c * CT, CT), :],
                                 sh_y[:, :].rearrange("p (n c) -> p n c", c=C), ALU.add).then_inc(s2["sh_added"], 1)

            def batch(q):
                map_batch(q)
                for h in range(CH // NQ):
                    c = q * (CH // NQ) + h
                    shared_act(c)
                    if not (isinstance(c, int) and c == 0):
                        shared_add(c - 1)

            batch(0)
            with v.Fori(1, NQ) as q:
                batch(q)
            v.wait_ge(s2["map_ready"], 1)
            nv.tensor_scalar(row_f[:, :], ps_map[:, TILES:2 * TILES], -float(P), float(SLOTS), ALU.mult,
                             ALU.add).then_inc(s2["rows_step"], 1)
            v.wait_ge(s2["rows_step"], 1)
            nv.tensor_tensor(row_g[:, :], row_f[:, :], ps_map[:, 0:TILES], ALU.add).then_inc(s2["rows_step"], 1)
            v.wait_ge(s2["rows_step"], 2)
            nv.tensor_copy(row_out[:, :], row_g[:, :]).then_inc(s2["rows_step"], 1)
            v.wait_ge(s2["rows_step"], 3)
            nv.tensor_scalar(row_in[:, :], row_out[:, :], N - 1, None, ALU.bitwise_and).then_inc(s2["rows_step"], 1)
            v.wait_ge(s2["rows_step"], 4)
            for m in range(U):
                nv.tensor_copy(gi[m][:, :], row_in[:, m:m + 1]).then_inc(s2["ready_gi"], 1)
            shared_add(CH - 1)

            def take_x(m, n):
                v.wait_ge(s2["xT_psum"], n + 1)
                after2(v, "up_ready", n - U + 1)
                nv.tensor_copy(xT[m][:, :], ps_x[:, 0:P]).then_inc(s2["xT_ready"], 1)

            take_x(0, 0)

            def group(r):
                for m in range(U):
                    n = r * U + m
                    final = isinstance(n, int) and n == TILES - 1
                    if not final:
                        take_x((m + 1) % U, n + 1)
                    v.wait_ge(s2["up_ready"], n + 1)
                    v.wait_ge(s2["gelu_ready"], n + 1)
                    after2(v, "actT_psum", n)
                    nv.tensor_tensor(actv[:, :], ps_a[:, 0:HR], gl[:, :], ALU.mult).then_inc(s2["act_ready"], 1)
                    if not (isinstance(r, int) and r == LAST):
                        v.wait_ge(gathered[m], (r + 1) * 16)
                        nv.tensor_copy(gi[m][:, :], row_in[:, ds(n + U, 1)]).then_inc(s2["ready_gi"], 1)
                    if not (isinstance(n, int) and n == 0):
                        give_y((m - 1) % U, n - 1, r if m else r - 1)
                    if final:
                        give_y(m, n, r)

            def give_y(m, n, r):
                after2(v, scattered[m], r * 16)
                nv.tensor_copy(si[m][:, :], row_out[:, ds(n, 1)])
                v.wait_ge(s2["y_ready"], n + 1)
                nv.tensor_copy(yo[m][:, :], ps_y[:, 0:C]).then_inc(s2["yo_ready"], 1)

            tiles(v, group)

            def step(r):
                for m in range(2):
                    c = r * 2 + m
                    v.wait_ge(y_loaded[m], (r + 1) * 32)
                    after2(v, "fin_out", c - 1)
                    for k, (y, acc) in enumerate(((y_first, x_all[:, ds(c * CT, CT), :]), (y_second, fin[m]))):
                        for t in range(CT):
                            last = nv.scalar_tensor_tensor(fin[m][:, t, :], y[:, ds(c * CT + t, 1), :].rearrange("p a c -> p (a c)"),
                                                           wt[k][:, ds(c * CT + t, 1)], acc[:, t, :], ALU.mult, ALU.add)
                        last.then_inc(s2["fin_sum"], 1)
                        v.wait_ge(s2["fin_sum"], c * 2 + k + 1)
                    for t in range(CT):
                        last = nv.bn_stats(fst[m][:, t, :], fin[m][:, t, :])
                    last.then_inc(s2["fin_ready"], 1)
                    v.wait_ge(s2["fin_ready"], c * 3 + 1)
                    nv.memset(wait_here[:, :], 0.0)
                    for t in range(CT):
                        last = nv.bn_aggr(fmv[m][:, t, :], fst[m][:, t, :])
                    last.then_inc(s2["fin_ready"], 1)
                    v.wait_ge(s2["fin_ready"], c * 3 + 2)
                    nv.tensor_scalar(fve[m][:, :], fmv[m][:, :, 1], EPS, None, ALU.add).then_inc(s2["fin_ready"], 1)
                    if not (isinstance(c, int) and c == 0):
                        minus(1 - m, c - 1)

            def minus(m, c):
                v.wait_ge(s2["fin_pow"], c + 1)
                nv.scalar_tensor_tensor(fnm[m][:, :], fmv[m][:, :, 0], -1.0, frs[m][:, :],
                                        ALU.mult, ALU.mult).then_inc(s2["fin_nmr"], 1)

            halves(v, step)
            minus(1, CH - 1)

        @experts.scalar
        def _(a):
            na = nc.scalar
            a.wait_ge(s2["gap_ready"], 1)
            na.activation(rel[:, :], fall[:, :], ACT.Exp, scale=1.0 / TAU).then_inc(s2["fall_exp"], 1)

            def shared(c):
                for j in range(HS):
                    a.wait_ge(s2["sh_gate"], c * HS + j + 1)
                    if j == 0:
                        after2(a, "sh_act", c * HS)
                    na.activation(gsh[:, j, :], sh_ps[HS + j][:, :], ACT.Gelu, bias=col(BS1 + HS + j)).then_inc(s2["sh_gelu"], 1)

            shared(0)
            with a.Fori(1, CH) as c:
                shared(c)

            def turn_act(n):
                a.wait_ge(s2["actT_psum"], n + 1)
                after2(a, "y_ready", n)
                na.activation(actT[:, :], ps_t[:, 0:HR], ACT.Copy).then_inc(s2["actT_ready"], 1)

            def group(r):
                for m in range(U):
                    n = r * U + m
                    a.wait_ge(s2["gate_ready"], n + 1)
                    after2(a, "act_ready", n)
                    na.activation(gl[:, :], ps_g[:, 0:HR], ACT.Gelu).then_inc(s2["gelu_ready"], 1)
                    if not (isinstance(n, int) and n == 0):
                        turn_act(n - 1)

            tiles(a, group)
            turn_act(TILES - 1)

            def step(r):
                for m in range(2):
                    c = r * 2 + m
                    a.wait_ge(s2["fin_nmr"], c + 1)
                    after2(a, stored[m], r * 16)
                    for t in range(CT):
                        last = na.activation(fo[m][:, t, :], fin[m][:, t, :], ACT.Identity,
                                             bias=fnm[m][:, t:t + 1], scale=frs[m][:, t:t + 1])
                    last.then_inc(s2["fin_out"], 1)
                    a.wait_ge(s2["fin_out"], c + 1)
                    a.dma_start(out_v[:, ds(c * CT, CT), :], fo[m][:, :, :]).then_inc(stored[m], 16)

            halves(a, step)
            for m in range(2):
                a.wait_ge(stored[m], CH // 2 * 16)

        @experts.tensor
        def _(t):
            nt = nc.tensor
            t.wait_ge(s["expert_w_loaded"], 7 * 16)
            t.wait_ge(s["xnT_kept"], CH * 16)
            def counts():
                t.wait_ge(s2["route"], 12)
                for ps, w, name in ((ps_tot, ones_bf, "totals_ready"), (ps_pre, upper, "prefix_ready")):
                    nt.matmul(ps[:, 0:NT * E], w[:, :], sel[:, :, :].rearrange("p n e -> p (n e)"),
                              start=True, stop=True).then_inc(s2[name], 1)

            def biased(to, row, width):
                return nt.matmul(to, ones_bf[:, :], bias_rows[:, ds(row, width)], start=False, stop=True)

            def shared_in(c):
                for half_, name, free in ((HS, "sh_gate", "sh_gelu"), (0, "sh_up", "sh_act")):
                    for j in range(HS):
                        after2(t, free, c * HS - HS + j + 1)
                        nt.matmul(sh_ps[half_ + j][:, :], ws1_sb[:, (half_ + j) * P:(half_ + j + 1) * P],
                                  xnT_all[:, ds(c * W, W)], start=True, stop=True).then_inc(s2[name], 1)

            def shared_out(c):
                t.wait_ge(s2["sh_act"], (c + 1) * HS)
                after2(t, "sh_added", c)
                for n in range(CT):
                    for j in range(HS):
                        nt.matmul(sh_y[:, n * P:(n + 1) * P], ash[:, j, n * P:(n + 1) * P], ws2_sb[:, j, :],
                                  start=j == 0, stop=False)
                    last = biased(sh_y[:, n * P:(n + 1) * P], BS2, C)
                last.then_inc(s2["sh_out"], 1)

            def map_batch(q):
                t.wait_ge(s2["tiles_ready"], q + 1)
                for j in range(JB):
                    last = nt.matmul(ps_map[:, 0:2 * TILES], oh_lane[:, j, :],
                                     tile_val[:, j, :, :].rearrange("p a n -> p (a n)"),
                                     start=first_of(q) and j == 0, stop=last_of(q) and j == JB - 1)
                last.then_inc(s2["map_used"], 1)

            def first_of(q):
                return isinstance(q, int) and q == 0

            def last_of(q):
                return isinstance(q, int) and q == NQ - 1

            def batch(q):
                map_batch(q)
                for h in range(CH // NQ):
                    c = q * (CH // NQ) + h
                    if not (isinstance(c, int) and c == 0):
                        shared_in(c)
                        shared_out(c - 1)

            shared_in(0)
            counts()
            t.wait_ge(s2["rows_moved"], 9 * 16)
            batch(0)
            with t.Fori(1, NQ - 1) as q:
                batch(q)
            map_batch(NQ - 1)
            t.wait_ge(s2["map_used"], NQ)
            nt.matmul(ps_pre[:, 0:1], ones_bf[:, :], bias_rows[:, 0:1], start=True, stop=True).then_inc(s2["map_ready"], 1)
            for c in range(CH - CH // NQ, CH):
                shared_in(c)
                shared_out(c - 1)
            shared_out(CH - 1)

            t.wait_ge(s2["owner_ready"], 1)

            def expert_of(n):
                return t.value_load(owner[0:1, ds(n, 1)], min_val=0, max_val=E - 1)

            def turn_x(m, n, r):
                t.wait_ge(gathered[m], (r + 1) * 16)
                after2(t, "xT_ready", n)
                nt.transpose(ps_x[:, 0:P], xg[m][:, :], ident[:, :]).then_inc(s2["xT_psum"], 1)

            def hidden(m, to, e, off):
                nt.matmul(to[:, 0:HR], xT[m][:, :], we1_sb[:, ds(e, 1), off:off + HR].rearrange("p a h -> p (a h)"),
                          start=True, stop=False)
                return biased(to[:, 0:HR], e * H1 + off, HR)

            def turn_act(n):
                t.wait_ge(s2["act_ready"], n + 1)
                after2(t, "actT_ready", n)
                for j in range(HK):
                    last = nt.transpose(ps_t[:, j * P:(j + 1) * P], actv[:, j * P:(j + 1) * P], ident[:, :])
                last.then_inc(s2["actT_psum"], 1)

            def second(n, e):
                t.wait_ge(s2["actT_ready"], n + 1)
                after2(t, "yo_ready", n)
                for j in range(HK):
                    nt.matmul(ps_y[:, 0:C], actT[:, j * P:(j + 1) * P],
                              we2_sb[:, ds(e, 1), j, :].rearrange("p a c -> p (a c)"), start=j == 0, stop=False)
                biased(ps_y[:, 0:C], BE2 + e * C, C).then_inc(s2["y_ready"], 1)

            t.wait_ge(s2["sh_added"], CH)
            turn_x(0, 0, 0)

            def group(r):
                e_before = None if isinstance(r, int) and r == 0 else expert_of(r * U - 1)
                experts_ = [expert_of(r * U + m) for m in range(U)]
                for m in range(U):
                    n, e = r * U + m, experts_[m]
                    e_last = experts_[m - 1] if m else e_before
                    t.wait_ge(s2["xT_ready"], n + 1)
                    after2(t, "gelu_ready", n)
                    hidden(m, ps_g, e, HR).then_inc(s2["gate_ready"], 1)
                    if e_last is not None:
                        turn_act(n - 1)
                    if not (isinstance(n, int) and n == TILES - 1):
                        turn_x((m + 1) % U, n + 1, r + (m + 1) // U)
                    after2(t, "act_ready", n)
                    hidden(m, ps_a, e, 0).then_inc(s2["up_ready"], 1)
                    if e_last is not None:
                        second(n - 1, e_last)
                return experts_[-1]

            group(0)
            with t.Fori(1, LAST) as r:
                group(r)
            e_end = group(LAST)
            turn_act(TILES - 1)
            second(TILES - 1, e_end)


def kernel(**inputs):
    import numpy as np
    import concourse.bacc as bacc
    from concourse.bass_utils import run_bass_kernel_spmd

    a = {k.removeprefix("L0_"): np.asarray(v) for k, v in inputs.items()}
    columns = [a[f"attn_{n}"] for n in ("ln1_w", "ln1_b", "ln2_w", "ln2_b", "time_decay", "time_first",
                                        "tmk", "tmv", "tmr", "cmk", "cmr")]
    columns += list(a["ffn_bs1"].reshape(-1, 128))
    arrays = {
        "x": a["attn_x"],
        "vecs": np.stack(columns, axis=1),
        "rows": np.concatenate([a["attn_ln0_w"], a["attn_ln0_b"], a["ffn_br"]]),
        "sqw": np.stack([a[f"attn_{n}"].T for n in ("Wk", "Wv", "Wr", "Wo", "Wfr")]),
        "wfk": a["attn_Wfk"].T,
        "wfv": a["attn_Wfv"].T,
        "wrt": a["ffn_Wr"],
        "ws1": a["ffn_Ws1"],
        "ws2": a["ffn_Ws2"],
        "we1": a["ffn_We1"],
        "we2": a["ffn_We2"],
        "be1": a["ffn_be1"],
        "be2": a["ffn_be2"],
        "bs2": a["ffn_bs2"],
    }
    arrays = {k: np.ascontiguousarray(v) for k, v in arrays.items()}
    nc = bacc.Bacc("TRN2", target_bir_lowering=False, num_devices=1)
    aps = {k: nc.dram_tensor(k, v.shape, mybir.dt.from_np(v.dtype), kind="ExternalInput").ap() for k, v in arrays.items()}
    out = nc.dram_tensor("out", a["attn_x"].shape, mybir.dt.float32, kind="ExternalOutput").ap()
    build(nc, out=out, **aps)
    return run_bass_kernel_spmd(nc, [arrays], core_ids=[0]).results[0]["out"]
```

```python
import concourse.bass as bass
from concourse import mybir
from contextlib import ExitStack


def build(nc, x, out, vecs, rows, sqw, wfk, wfv, wrt, ws1, ws2, we1, we2, be1, be2, bs2):
    F32, BF16 = mybir.dt.float32, mybir.dt.bfloat16
    I32, U32 = mybir.dt.int32, mybir.dt.uint32
    ALU = mybir.AluOpType
    ACT = mybir.ActivationFunctionType
    AX = mybir.AxisListType
    ds = bass.ds

    B, T, C = x.shape
    P = 128
    N = B * T
    NT = N // P
    CT = 4
    CH = NT // CT
    W = CT * P
    SQ = W // T
    E = we1.shape[0]
    HR = we2.shape[1]
    HK = HR // P
    H1 = 2 * HR
    HF = wfk.shape[1] // P
    HS = ws2.shape[0] // P
    K = 2
    SLOTS = K * N
    TILES = (SLOTS + E * (P - 1)) // P
    U = 5
    assert TILES % U == 0
    EPS, NEG, TAU = 1e-5, -1e38, 1.5
    JB = 16
    NJ = K * NT
    NQ = NJ // JB

    x_v = x.rearrange("b t c -> (b t) c").rearrange("(n p) c -> p n c", p=P)
    out_v = out.rearrange("b t c -> (b t) c").rearrange("(n p) c -> p n c", p=P)
    table = nc.dram_tensor("token_table", (N, C), F32, kind="Internal").ap()
    table_v = table.rearrange("(n p) c -> p n c", p=P)
    routed = nc.dram_tensor("routed_rows", (SLOTS, C), F32, kind="Internal").ap()
    routed_v = routed.rearrange("(k n p) c -> p k n c", p=P, k=K)

    ctx = ExitStack()
    with ctx:
        def sb(name, shape, dt=F32):
            return ctx.enter_context(nc.sbuf_tensor(name, shape, dt))

        def sem(name):
            return ctx.enter_context(nc.semaphore(name))

        x_all = sb("x_all", [P, NT, C])
        x0_all = sb("x0_all", [P, NT, C])
        xnT_all = sb("xnT_all", [P, N])
        y_first = x0_all
        y_second = xnT_all[:, :].rearrange("p (n c) -> p n c", c=C)
        we1_sb = sb("we1_sb", [P, E, H1])
        we2_sb = sb("we2_sb", [P, E, HK, C])
        BE2, BS2 = E * H1, E * H1 + E * C
        sq_sb = sb("sq_sb", [P, 5, C])
        mixa = sb("mixa", [P, 3, C])
        mixb = sb("mixb", [P, 3, C])
        wfk_sb = sb("wfk_sb", [P, HF * P])
        wfv_sb = sb("wfv_sb", [P, HF, C])
        wrt_sb = sb("wrt_sb", [P, E])
        ws1_sb = sb("ws1_sb", [P, 2 * HS * P])
        ws2_sb = sb("ws2_sb", [P, HS, C])
        NV = vecs.shape[1]
        v_sb = sb("v_sb", [P, NV])
        LN1W, LN1B, LN2W, LN2B, DECAY, FIRST, TMK, TMV, TMR, CMK, CMR, BS1 = range(12)
        NB = (E * H1 + E * C + C) // P
        braw = sb("braw", [P, NB])
        bleft = sb("bleft", [P, NB])
        bleft2 = sb("bleft2", [P, NB])
        bpart = [sb(f"bpart{n}", [P, NB], BF16) for n in range(3)]
        B1, B2 = E * H1 // P, (E * H1 + E * C) // P
        rows_sb = sb("rows_sb", [P, 2 * C + E])
        ln0w, ln0b, br_sb = rows_sb[:, 0:C], rows_sb[:, C:2 * C], rows_sb[:, 2 * C:2 * C + E]
        dec = sb("dec", [P, 6])

        def col(n):
            return v_sb[:, n:n + 1]

        ident = sb("ident", [P, P])
        ones_bf = sb("ones_bf", [P, P], BF16)
        upper = sb("upper", [P, P], BF16)
        lane_i = sb("lane_i", [P, P], I32)
        lane_bf = sb("lane_bf", [P, P], BF16)
        lane_f = sb("lane_f", [P, P])
        part_i = sb("part_i", [P, 1], I32)
        part_f = sb("part_f", [P, 1])
        left_i = sb("left_i", [P, NJ], I32)
        left_bf = sb("left_bf", [P, NJ], BF16)
        thr_i = sb("thr_i", [P, NT], I32)
        thr_f = sb("thr_f", [P, NT])
        keep_first = sb("keep_first", [P, E])
        keep_i = sb("keep_i", [P, E], I32)
        scan_on = sb("scan_on", [P, E, NT])
        half = sb("half", [P, CT])
        wait_here = sb("wait_here", [1, 1])
        g_wait = sb("g_wait", [1, 3])

        lg = sb("lg", [P, NT, E])

        block_buffers = ExitStack()

        def tmp(name, shape, dt=F32):
            return block_buffers.enter_context(nc.sbuf_tensor(name, shape, dt))

        bst = {n: tmp(f"bst{n}", [P, CT, 6]) for n in "0123"}
        mv = {n: tmp(f"mv{n}", [P, CT, 2]) for n in "0123"}
        veps = {n: tmp(f"veps{n}", [P, CT]) for n in "0123"}
        rstd = {n: tmp(f"rstd{n}", [P, CT]) for n in "0123"}
        nmr = {n: tmp(f"nmr{n}", [P, CT]) for n in "0123"}
        z0 = tmp("z0", [P, CT, C])
        z0w = tmp("z0w", [P, CT, C])
        z1 = tmp("z1", [P, CT, C])
        hT = tmp("hT", [P, SQ, T + 1])
        pp = tmp("pp", [P, SQ, T + 1])
        ab = tmp("ab", [P, 2, SQ, T + 1])
        gap = tmp("gap", [P, 2, W])
        below_p = tmp("below_p", [P, 2, W])
        below_m = tmp("below_m", [P, 2, W])
        e_plus = tmp("e_plus", [P, 2, W])
        e_minus = tmp("e_minus", [P, 2, W])
        old_in_state, new_in_output = e_plus[:, 0, :], e_plus[:, 1, :]
        new_in_state, old_in_output = e_minus[:, 0, :], e_minus[:, 1, :]
        e2v = tmp("e2v", [P, W])
        new_v = tmp("new_v", [P, W])
        nd = tmp("nd", [P, 2, W])
        th = tmp("th", [P, W])
        rec = tmp("rec", [P, W])
        yT = tmp("yT", [P, W])
        x1c = tmp("x1c", [P, CT, C])
        z2 = tmp("z2", [P, CT, C])
        h2T = tmp("h2T", [P, SQ, T + 1])
        d2 = tmp("d2", [P, SQ, T])
        xk2 = tmp("xk2", [P, W])
        xr2 = tmp("xr2", [P, W])
        kf = tmp("kf", [P, HF, W])
        th2 = tmp("th2", [P, W])
        x2c = tmp("x2c", [P, W])
        x3c = tmp("x3c", [P, CT, C])
        xnc = tmp("xnc", [P, CT, C])
        xnTc = tmp("xnTc", [P, W])

        block_buffers.close()
        xn_all = sb("xn_all", [P, NT, C])
        bias_rows = sb("bias_rows", [P, E * H1 + E * C + C], BF16)
        top = [sb(f"top{k}", [P, NT]) for k in range(K)]
        which = sb("which", [P, NT])
        fall = sb("fall", [P, NT])
        rel = sb("rel", [P, NT])
        total = sb("total", [P, NT])
        wt = [sb(f"wt{k}", [P, NT]) for k in range(K)]
        ntl = sb("ntl", [P, E])
        cumt = sb("cumt", [P, E])
        start = sb("start", [P, E])
        slot = sb("slot", [P, K, NT])
        slot_i = sb("slot_i", [P, NJ], I32)
        lane_s = sb("lane_s", [P, NJ], I32)
        tile_s = sb("tile_s", [P, NJ], I32)
        lane_j = sb("lane_j", [P, NJ], BF16)
        tile_j = sb("tile_j", [P, NJ], BF16)
        owner_f = sb("owner_f", [1, TILES])
        owner = sb("owner", [1, TILES + 1])
        GROUPS = TILES // U
        BITS = (E - 1).bit_length()
        places = sb("places", [1, U + 1])
        owner_at = sb("owner_at", [1, GROUPS, U + 1])
        packed_f = sb("packed_f", [1, GROUPS])
        packed = sb("packed", [1, GROUPS], I32)
        oh_lane = sb("oh_lane", [P, JB, P], BF16)
        oh_tile = sb("oh_tile", [P, JB, TILES], BF16)
        tile_val = sb("tile_val", [P, JB, 2, TILES], BF16)
        row_f = sb("row_f", [P, TILES])
        row_g = sb("row_g", [P, TILES])
        row_out = sb("row_out", [P, TILES], U32)
        row_in = sb("row_in", [P, TILES], U32)
        gsh = sb("gsh", [P, HS, W])
        ash = sb("ash", [P, HS, W])
        routing_buffers = ExitStack()

        def scratch(name, shape, dt=F32):
            return routing_buffers.enter_context(nc.sbuf_tensor(name, shape, dt))

        sc_pos = scratch("sc_pos", [P, NT, E])
        eq = scratch("eq", [P, NT, E])
        pick = [scratch(f"pick{k}", [P, NT, E]) for k in range(K)]
        lg2 = scratch("lg2", [P, NT, E])
        sel = scratch("sel", [P, NT, E], BF16)
        tot = scratch("tot", [P, E, NT])
        incl = scratch("incl", [P, E, NT])
        more = scratch("more", [P, E, NT])
        before = scratch("before", [1, TILES, E])
        routing_buffers.close()
        xg = [sb(f"xg{m}", [P, C]) for m in range(U)]
        xT = [sb(f"xT{m}", [P, P]) for m in range(U)]
        gi = [sb(f"gi{m}", [P, 1], U32) for m in range(U)]
        si = [sb(f"si{m}", [P, 1], U32) for m in range(U)]
        gl = sb("gl", [P, HR])
        actv = sb("actv", [P, HR])
        actT = sb("actT", [P, HR])
        yo = [sb(f"yo{m}", [P, C]) for m in range(U)]
        fin = [gsh[:, m, :].rearrange("p (n c) -> p n c", c=C) for m in range(2)]
        fo = [ash[:, m, :].rearrange("p (n c) -> p n c", c=C) for m in range(2)]
        fst = [sb(f"fst{m}", [P, CT, 6]) for m in range(2)]
        fmv = [sb(f"fmv{m}", [P, CT, 2]) for m in range(2)]
        fve = [sb(f"fve{m}", [P, CT]) for m in range(2)]
        frs = [sb(f"frs{m}", [P, CT]) for m in range(2)]
        fnm = [sb(f"fnm{m}", [P, CT]) for m in range(2)]

        banks = [ctx.enter_context(nc.psum_tensor(f"bank{i}", [P, 512], F32)) for i in range(8)]
        pk, pv, pr, pT, pf0, pf1, pkv, po = banks
        pf = (pf0, pf1)

        s = {}
        for n in ("w_loaded mix_w_ready x_loaded consts pool_consts edges scaled parts parts_moved "
                  "bn0 bn1 bn2 bn3 pow0 pow1 pow2 pow3 nmr0 nmr1 nmr2 nmr3 "
                  "z0_ready z0w_ready x0_ready z1_ready hT_psum hT_ready k_ready v_ready r_ready "
                  "pp_ready delta_ready gaps_ready exp_plus exp_minus wkv_step y_half nd_ready den_ready th_ready yT_ready "
                  "po_ready x1_ready z2_ready h2_psum h2_ready d2_ready mixed2 fk_ready relu_done "
                  "sq_pool sq_act r2_ready th2_ready kv_ready x2_step x3_ready xn_ready xnT_psum xnT_ready "
                  "logits_psum logits_ready table_written xnT_kept expert_w_loaded iotas split").split():
            s[n] = sem(n)

        first_block = ExitStack()
        block = first_block.enter_context(nc.Block())

        L_WAITS = 15 * 16

        @block.sync
        def _(sp):
            sp.dma_start(x_all[:, 0:CT, :], x_v[:, 0:CT, :]).then_inc(s["x_loaded"], 16)
            sp.dma_start(rows_sb[:, :], rows.partition_broadcast(P)).then_inc(s["w_loaded"], 16)
            sp.dma_start(v_sb[:, :], vecs).then_inc(s["w_loaded"], 16)
            sp.dma_start(sq_sb[:, :, :], sqw.rearrange("s p c -> p s c")).then_inc(s["w_loaded"], 16)
            sp.dma_start(wfk_sb[:, :], wfk).then_inc(s["w_loaded"], 16)
            sp.dma_start(wfv_sb[:, :, :], wfv.rearrange("(j p) c -> p j c", p=P)).then_inc(s["w_loaded"], 16)
            sp.dma_start(wrt_sb[:, :], wrt).then_inc(s["w_loaded"], 16)
            with sp.Fori(1, CH) as c:
                sp.wait_ge(s["x_loaded"], c * 16)
                sp.dma_start(x_all[:, ds(c * CT, CT), :], x_v[:, ds(c * CT, CT), :]).then_inc(s["x_loaded"], 16)
            for to, of in ((braw[:, 0:B1], be1.rearrange("e h -> (e h)").rearrange("(p a) -> p a", a=B1)),
                           (braw[:, B1:B2], be2.rearrange("e h -> (e h)").rearrange("(p a) -> p a", a=B2 - B1)),
                           (braw[:, B2:NB], bs2.rearrange("(p a) -> p a", a=NB - B2)),
                           (ws1_sb[:, :], ws1), (ws2_sb[:, :, :], ws2.rearrange("(j p) c -> p j c", p=P)),
                           (we1_sb[:, :, :], we1.rearrange("e d h -> d e h")),
                           (we2_sb[:, :, :, :], we2.rearrange("e (j p) c -> p e j c", p=P))):
                sp.dma_start(to, of).then_inc(s["expert_w_loaded"], 16)
            with sp.Fori(0, CH) as c:
                sp.wait_ge(s["xn_ready"], c + 1)
                sp.dma_start(table_v[:, ds(c * CT, CT), :], xnc[:, :, :]).then_inc(s["table_written"], 16)
                sp.wait_ge(s["xnT_ready"], c + 1)
                sp.dma_start(xnT_all[:, ds(c * W, W)], xnTc[:, :]).then_inc(s["xnT_kept"], 16)

        def stages(eng, turn):
            for i in range(4):
                turn(i, i, *[i - n if i >= n else None for n in (1, 2, 3)])
            with eng.Fori(4, CH) as i:
                turn(i, i, i - 1, i - 2, i - 3)
            for i in range(CH, CH + 3):
                turn(i, *[i - n if i - n < CH else None for n in (0, 1, 2, 3)])

        def after(eng, name, count):
            if not (isinstance(count, int) and count <= 0):
                eng.wait_ge(s[name], count)

        def upto(i, most):
            return min(i, most) if isinstance(i, int) else i

        @block.vector
        def _(v):
            nv = nc.vector
            nv.memset(hT[:, :, 0:1], 0.0)
            nv.memset(h2T[:, :, 0:1], 0.0)
            nv.memset(pp[:, :, 0:1], NEG)
            nv.memset(ab[:, :, :, 0:1], 0.0)
            nv.memset(ones_bf[:, :], 1.0)
            nv.memset(scan_on[:, :, :], 1.0)
            nv.memset(half[:, :], -0.5).then_inc(s["edges"], 1)
            v.wait_ge(s["w_loaded"], 6 * 16)
            nv.tensor_scalar(dec[:, 2:5], v_sb[:, TMK:TMR + 1], -1.0, 1.0, ALU.mult, ALU.add).then_inc(s["scaled"], 1)
            v.wait_ge(s["scaled"], 1)
            for n in range(3):
                nv.tensor_scalar(mixa[:, n, :], sq_sb[:, n, :], col(TMK + n), None, ALU.mult)
                last = nv.tensor_scalar(mixb[:, n, :], sq_sb[:, n, :], dec[:, 2 + n:3 + n], None, ALU.mult)
            last.then_inc(s["mix_w_ready"], 1)
            v.wait_ge(s["consts"], 1)
            nv.tensor_scalar(dec[:, 0:1], dec[:, 5:6], -1.0, None, ALU.mult).then_inc(s["scaled"], 1)
            v.wait_ge(s["scaled"], 2)
            nv.memset(scan_on[:, :, 0:1], 0.0)
            v.wait_ge(s["iotas"], 1)
            nv.tensor_copy(lane_bf[:, :], lane_i[:, :])
            nv.tensor_copy(lane_f[:, :], lane_i[:, :])
            nv.tensor_copy(part_f[:, :], part_i[:, :])
            nv.tensor_copy(left_bf[:, :], left_i[:, :])
            nv.tensor_copy(thr_f[:, :], thr_i[:, :])
            nv.tensor_copy(keep_first[:, :], keep_i[:, :]).then_inc(s["scaled"], 1)

            def stats(n, tiles, c):
                bn = s["bn" + n]
                for t in range(CT):
                    last = nv.bn_stats(bst[n][:, t, :], tiles[:, t, :])
                last.then_inc(bn, 1)
                v.wait_ge(bn, c * 3 + 1)
                nv.memset(wait_here[:, :], 0.0)
                for t in range(CT):
                    last = nv.bn_aggr(mv[n][:, t, :], bst[n][:, t, :])
                last.then_inc(bn, 1)
                v.wait_ge(bn, c * 3 + 2)
                nv.tensor_scalar(veps[n][:, :], mv[n][:, :, 1], EPS, None, ALU.add).then_inc(bn, 1)

            def offset(n, c):
                v.wait_ge(s["pow" + n], c + 1)
                nv.scalar_tensor_tensor(nmr[n][:, :], mv[n][:, :, 0], -1.0, rstd[n][:, :],
                                        ALU.mult, ALU.mult).then_inc(s["nmr" + n], 1)

            def turn(i, c1, c2, c3, c4):
                if c3 is not None:
                    after(v, "x2_step", c3 * 2)
                    after(v, "nmr2", c3)
                    v.wait_ge(s["po_ready"], c3 + 1)
                    nv.tensor_tensor(x1c[:, :, :], x0_all[:, ds(c3 * CT, CT), :],
                                     po[:, :].rearrange("p (n c) -> p n c", c=C), ALU.add).then_inc(s["x1_ready"], 1)
                    v.wait_ge(s["x1_ready"], c3 + 1)
                    stats("2", x1c, c3)
                if c4 is not None:
                    after(v, "nmr3", c4)
                    v.wait_ge(s["x3_ready"], c4 + 1)
                    stats("3", x3c, c4)
                if c3 is not None:
                    after(v, "z2_ready", c3)
                    offset("2", c3)
                if c2 is not None:
                    after(v, "yT_ready", c2)
                    v.wait_ge(s["k_ready"], c2 + 1)
                    for q in range(SQ):
                        last = nv.tensor_tensor_scan(pp[:, q, 1:T + 1], dec[:, 0:1].to_broadcast([P, T]),
                                                     pk[:, q * T:(q + 1) * T], NEG, ALU.add, ALU.max)
                    last.then_inc(s["pp_ready"], 1)
                    v.wait_ge(s["pp_ready"], c2 + 1)
                    nv.scalar_tensor_tensor(gap[:, 0, :].rearrange("p (q t) -> p q t", t=T), pp[:, :, 0:T], dec[:, 0:1],
                                            pk[:, :].rearrange("p (q t) -> p q t", t=T), ALU.add, ALU.subtract)
                    nv.scalar_tensor_tensor(gap[:, 1, :].rearrange("p (q t) -> p q t", t=T),
                                            pk[:, :].rearrange("p (q t) -> p q t", t=T), col(FIRST), pp[:, :, 0:T],
                                            ALU.add, ALU.subtract).then_inc(s["delta_ready"], 1)
                    v.wait_ge(s["delta_ready"], c2 + 1)
                    after(v, "exp_minus", c2)
                    nv.tensor_scalar(below_p[:, :, :], gap[:, :, :], 0.0, None, ALU.min)
                    nv.tensor_scalar(below_m[:, :, :], gap[:, :, :], 0.0, None, ALU.max).then_inc(s["gaps_ready"], 1)
                if c4 is not None:
                    after(v, "xn_ready", c4)
                    offset("3", c4)
                if c1 is not None:
                    after(v, "nmr0", c1)
                    v.wait_ge(s["x_loaded"], (c1 + 1) * 16)
                    stats("0", x_all[:, ds(c1 * CT, CT), :], c1)
                if c2 is not None:
                    v.wait_ge(s["exp_plus"], c2 + 1)
                    v.wait_ge(s["exp_minus"], c2 + 1)
                    v.wait_ge(s["v_ready"], c2 + 1)
                    after(v, "den_ready", c2)
                    nv.tensor_tensor(e2v[:, :], new_in_state, pv[:, :], ALU.mult).then_inc(s["wkv_step"], 1)
                    nv.tensor_tensor(new_v[:, :], new_in_output, pv[:, :], ALU.mult).then_inc(s["wkv_step"], 1)
                    v.wait_ge(s["wkv_step"], c2 * 3 + 1)
                    for q in range(SQ):
                        at = slice(q * T, (q + 1) * T)
                        nv.tensor_tensor_scan(ab[:, 0, q, 1:T + 1], old_in_state[:, at], e2v[:, at], 0.0, ALU.mult, ALU.add)
                        last = nv.tensor_tensor_scan(ab[:, 1, q, 1:T + 1], old_in_state[:, at], new_in_state[:, at], 0.0,
                                                     ALU.mult, ALU.add)
                    last.then_inc(s["wkv_step"], 1)
                    v.wait_ge(s["wkv_step"], c2 * 3 + 3)
                    for n in range(2):
                        last = nv.tensor_tensor(nd[:, n, :].rearrange("p (q t) -> p q t", t=T), ab[:, n, :, 0:T],
                                                old_in_output.rearrange("p (q t) -> p q t", t=T), ALU.mult)
                    last.then_inc(s["nd_ready"], 1)
                if c1 is not None:
                    after(v, "z0_ready", c1)
                    offset("0", c1)
                if c3 is not None:
                    v.wait_ge(s["d2_ready"], c3 + 1)
                    after(v, "r2_ready", c3)
                    for m, to in ((CMK, xk2), (CMR, xr2)):
                        last = nv.scalar_tensor_tensor(to[:, :].rearrange("p (q t) -> p q t", t=T), d2[:, :, :], col(m),
                                                       h2T[:, :, 0:T], ALU.mult, ALU.add)
                    last.then_inc(s["mixed2"], 1)
                if c2 is not None:
                    v.wait_ge(s["den_ready"], c2 + 1)
                    nv.reciprocal(rec[:, :], nd[:, 1, :]).then_inc(s["y_half"], 1)
                    v.wait_ge(s["th_ready"], c2 + 1)
                    after(v, "po_ready", c2)
                    nv.scalar_tensor_tensor(yT[:, :], th[:, :], 1.0, nd[:, 0, :], ALU.add, ALU.mult).then_inc(s["y_half"], 1)
                    v.wait_ge(s["y_half"], c2 * 2 + 2)
                    nv.scalar_tensor_tensor(yT[:, :], yT[:, :], 0.5, rec[:, :], ALU.mult, ALU.mult).then_inc(s["yT_ready"], 1)
                if c1 is not None:
                    after(v, "nmr1", c1)
                    v.wait_ge(s["x0_ready"], c1 + 1)
                    stats("1", x0_all[:, ds(c1 * CT, CT), :], c1)
                if c4 is not None:
                    v.wait_ge(s["logits_psum"], c4 + 1)
                    nv.tensor_tensor(lg[:, ds(c4 * CT, CT), :], pT[:, 0:CT * E].rearrange("p (n e) -> p n e", e=E),
                                     br_sb.unsqueeze(1).to_broadcast([P, CT, E]), ALU.add).then_inc(s["logits_ready"], 1)
                if c1 is not None:
                    after(v, "z1_ready", c1)
                    offset("1", c1)
                if c3 is not None:
                    v.wait_ge(s["th2_ready"], c3 + 1)
                    v.wait_ge(s["kv_ready"], c3 + 1)
                    after(v, "x3_ready", c3)
                    nv.scalar_tensor_tensor(x2c[:, :], th2[:, :], 1.0, pkv[:, :], ALU.add, ALU.mult).then_inc(s["x2_step"], 1)
                    v.wait_ge(s["x2_step"], c3 * 2 + 1)
                    nv.scalar_tensor_tensor(x2c[:, :], x2c[:, :], 0.5, x1c[:, :, :].rearrange("p n c -> p (n c)"),
                                            ALU.mult, ALU.add).then_inc(s["x2_step"], 1)

            stages(v, turn)

        @block.scalar
        def _(a):
            na = nc.scalar
            a.wait_ge(s["w_loaded"], 6 * 16)
            na.activation(dec[:, 5:6], col(DECAY), ACT.Exp).then_inc(s["consts"], 1)

            def apply(n, to, of):
                for t in range(CT):
                    last = na.activation(to[:, t, :], of[:, t, :], ACT.Identity,
                                         bias=nmr[n][:, t:t + 1], scale=rstd[n][:, t:t + 1])
                return last

            def turn(i, c1, c2, c3, c4):
                if c3 is not None:
                    v1 = c3 + 1
                    a.wait_ge(s["nmr2"], v1)
                    after(a, "h2_psum", c3)
                    apply("2", z2, x1c).then_inc(s["z2_ready"], 1)
                if c4 is not None:
                    a.wait_ge(s["nmr3"], c4 + 1)
                    after(a, "xnT_psum", c4)
                    after(a, "table_written", c4 * 16)
                    apply("3", xnc, x3c).then_inc(s["xn_ready"], 1)
                if c2 is not None:
                    a.wait_ge(s["gaps_ready"], c2 + 1)
                    after(a, "yT_ready", c2)
                    na.activation(e_minus[:, :, :], below_m[:, :, :], ACT.Exp, scale=-1.0).then_inc(s["exp_minus"], 1)
                    na.activation(e_plus[:, :, :], below_p[:, :, :], ACT.Exp).then_inc(s["exp_plus"], 1)
                if c3 is not None:
                    a.wait_ge(s["h2_psum"], c3 + 1)
                    after(a, "mixed2", c3)
                    na.activation(h2T[:, :, 1:T + 1], pT[:, :].rearrange("p (q t) -> p q t", t=T), ACT.Identity,
                                  bias=col(LN2B), scale=col(LN2W)).then_inc(s["h2_ready"], 1)
                if c1 is not None:
                    a.wait_ge(s["nmr0"], c1 + 1)
                    after(a, "z0w_ready", c1)
                    apply("0", z0, x_all[:, ds(c1 * CT, CT), :]).then_inc(s["z0_ready"], 1)
                if c2 is not None:
                    a.wait_ge(s["r_ready"], c2 + 1)
                    na.activation(th[:, :], pr[:, :], ACT.Tanh, scale=0.5).then_inc(s["th_ready"], 1)
                if c4 is not None:
                    a.wait_ge(s["xnT_psum"], c4 + 1)
                    after(a, "logits_psum", c4)
                    after(a, "xnT_kept", c4 * 16)
                    na.activation(xnTc[:, :], pT[:, :], ACT.Copy).then_inc(s["xnT_ready"], 1)
                if c3 is not None:
                    after(a, "kv_ready", c3)
                    for j in range(HF):
                        a.wait_ge(s["fk_ready"], c3 * HF + j + 1)
                        na.activation(kf[:, j, :], pf[j % 2][:, :], ACT.Relu).then_inc(s["relu_done"], 1)
                        if j % 2:
                            a.wait_ge(s["relu_done"], c3 * HF + j + 1)
                            na.activation(kf[:, j, :], kf[:, j, :], ACT.Square).then_inc(s["sq_act"], 1)
                    a.wait_ge(s["r2_ready"], c3 + 1)
                    after(a, "x2_step", c3 * 2)
                    na.activation(th2[:, :], pr[:, :], ACT.Tanh, scale=0.5).then_inc(s["th2_ready"], 1)
                if c1 is not None:
                    a.wait_ge(s["nmr1"], c1 + 1)
                    after(a, "hT_psum", c1)
                    apply("1", z1, x0_all[:, ds(c1 * CT, CT), :]).then_inc(s["z1_ready"], 1)
                    a.wait_ge(s["hT_psum"], c1 + 1)
                    after(a, "r_ready", c1)
                    na.activation(hT[:, :, 1:T + 1], pT[:, :].rearrange("p (q t) -> p q t", t=T), ACT.Identity,
                                  bias=col(LN1B), scale=col(LN1W)).then_inc(s["hT_ready"], 1)

            stages(a, turn)

        @block.gpsimd
        def _(g):
            ng = nc.gpsimd
            ng.memset(ident[:, :], 0.0).then_inc(s["pool_consts"], 1)
            g.wait_ge(s["pool_consts"], 1)
            ng.affine_select(out=ident[:, :], in_=ident[:, :], compare_op=ALU.not_equal, fill=1.0,
                             base=0, pattern=[[-1, P]], channel_multiplier=1).then_inc(s["pool_consts"], 1)
            g.wait_ge(s["edges"], 1)
            ng.affine_select(out=upper[:, :], in_=ones_bf[:, :], compare_op=ALU.is_gt, fill=0.0,
                             base=0, pattern=[[1, P]], channel_multiplier=-1)
            ng.iota(lane_i[:, :], pattern=[[1, P]], base=0, channel_multiplier=0)
            ng.iota(part_i[:, :], pattern=[[1, 1]], base=0, channel_multiplier=1)
            ng.iota(left_i[:, :], pattern=[[-1, NJ]], base=NJ, channel_multiplier=0)
            ng.iota(thr_i[:, :], pattern=[[P, NT]], base=0, channel_multiplier=0)
            ng.iota(keep_i[:, :], pattern=[[-1, E]], base=E, channel_multiplier=0).then_inc(s["iotas"], 1)
            g.wait_ge(s["w_loaded"], 6 * 16)

            def power(n, c):
                g.wait_ge(s["bn" + n], c * 3 + 3)
                after(g, "nmr" + n, c)
                ng.tensor_tensor(rstd[n][:, :], veps[n][:, :], half[:, :], ALU.pow).then_inc(s["pow" + n], 1)

            def turn(i, c1, c2, c3, c4):
                if c3 is not None:
                    after(g, "z2_ready", c3)
                    power("2", c3)
                if c4 is not None:
                    after(g, "xn_ready", c4)
                    power("3", c4)
                if c1 is not None:
                    after(g, "z0_ready", c1)
                    power("0", c1)
                if c3 is not None:
                    g.wait_ge(s["h2_ready"], c3 + 1)
                    after(g, "mixed2", c3)
                    ng.tensor_tensor(d2[:, :, :], h2T[:, :, 1:T + 1], h2T[:, :, 0:T], ALU.subtract).then_inc(s["d2_ready"], 1)
                if c2 is not None:
                    g.wait_ge(s["nd_ready"], c2 + 1)
                    g.wait_ge(s["wkv_step"], c2 * 3 + 3)
                    ng.tensor_tensor(nd[:, 0, :], nd[:, 0, :], new_v[:, :], ALU.add)
                    ng.tensor_tensor(nd[:, 1, :], nd[:, 1, :], new_in_output, ALU.add).then_inc(s["den_ready"], 1)
                if c1 is not None:
                    g.wait_ge(s["z0_ready"], c1 + 1)
                    after(g, "x0_ready", c1)
                    ng.tensor_tensor(z0w[:, :, :], z0[:, :, :], ln0w.unsqueeze(1).to_broadcast([P, CT, C]),
                                     ALU.mult).then_inc(s["z0w_ready"], 1)
                    g.wait_ge(s["z0w_ready"], c1 + 1)
                    ng.tensor_tensor(x0_all[:, ds(c1 * CT, CT), :], z0w[:, :, :],
                                     ln0b.unsqueeze(1).to_broadcast([P, CT, C]), ALU.add).then_inc(s["x0_ready"], 1)
                if c3 is not None:
                    for j in range(0, HF, 2):
                        g.wait_ge(s["relu_done"], c3 * HF + j + 1)
                        ng.tensor_tensor(kf[:, j, :], kf[:, j, :], kf[:, j, :], ALU.mult).then_inc(s["sq_pool"], 1)
                if c1 is not None:
                    after(g, "z1_ready", c1)
                    power("1", c1)
                if c3 is not None:
                    g.wait_ge(s["x2_step"], c3 * 2 + 2)
                    after(g, "xn_ready", c3)
                    ng.tensor_tensor(x3c[:, :, :], x2c[:, :].rearrange("p (n c) -> p n c", c=C),
                                     x_all[:, ds(c3 * CT, CT), :], ALU.add).then_inc(s["x3_ready"], 1)

            stages(g, turn)

        @block.tensor
        def _(t):
            nt = nc.tensor
            t.wait_ge(s["w_loaded"], 6 * 16)
            t.wait_ge(s["mix_w_ready"], 1)
            t.wait_ge(s["pool_consts"], 2)
            t.wait_ge(s["edges"], 1)

            def turned(of):
                for n in range(CT):
                    last = nt.transpose(pT[:, n * P:(n + 1) * P], of[:, n, :], ident[:, :])
                return last

            def turn(i, c1, c2, c3, c4):
                if c2 is not None:
                    t.wait_ge(s["hT_ready"], c2 + 1)
                    for n, (to, name, free, count) in enumerate((
                            (pk, "k_ready", "delta_ready", c2), (pv, "v_ready", "wkv_step", c2 * 3),
                            (pr, "r_ready", "th_ready", c2))):
                        after(t, free, count)
                        if n == 2 and not (isinstance(i, int) and i < 3):
                            after(t, "th2_ready", upto(i, CH + 2) - 2)
                        o = to[:, :].rearrange("p (q t) -> p q t", t=T)
                        nt.matmul(o, mixa[:, n, :], hT[:, :, 1:T + 1], start=True, stop=False)
                        nt.matmul(o, mixb[:, n, :], hT[:, :, 0:T], start=False, stop=True).then_inc(s[name], 1)
                if c3 is not None:
                    t.wait_ge(s["z2_ready"], c3 + 1)
                    after(t, "hT_ready", upto(i, CH))
                    after(t, "logits_ready", c3 - 1)
                    turned(z2).then_inc(s["h2_psum"], 1)
                if c4 is not None:
                    t.wait_ge(s["xn_ready"], c4 + 1)
                    after(t, "h2_ready", upto(i - 1, CH))
                    after(t, "logits_ready", c4)
                    turned(xnc).then_inc(s["xnT_psum"], 1)
                if c3 is not None:
                    t.wait_ge(s["mixed2"], c3 + 1)
                    for j in range(HF):
                        after(t, "relu_done", c3 * HF + (j - 1))
                        nt.matmul(pf[j % 2][:, :], wfk_sb[:, j * P:(j + 1) * P], xk2[:, :],
                                  start=True, stop=True).then_inc(s["fk_ready"], 1)
                    after(t, "th_ready", upto(i, CH))
                    for n in range(CT):
                        last = nt.matmul(pr[:, n * P:(n + 1) * P], xr2[:, n * P:(n + 1) * P], sq_sb[:, 4, :],
                                         start=True, stop=True)
                    last.then_inc(s["r2_ready"], 1)
                if c4 is not None:
                    t.wait_ge(s["xnT_ready"], c4 + 1)
                    for n in range(CT):
                        last = nt.matmul(pT[:, n * E:(n + 1) * E], xnTc[:, n * P:(n + 1) * P], wrt_sb[:, :],
                                         start=True, stop=True)
                    last.then_inc(s["logits_psum"], 1)
                if c3 is not None:
                    t.wait_ge(s["sq_act"], (c3 + 1) * (HF // 2))
                    t.wait_ge(s["sq_pool"], (c3 + 1) * (HF // 2))
                    after(t, "x2_step", c3 * 2)
                    for n in range(CT):
                        for j in range(HF):
                            last = nt.matmul(pkv[:, n * P:(n + 1) * P], kf[:, j, n * P:(n + 1) * P], wfv_sb[:, j, :],
                                             start=j == 0, stop=j == HF - 1)
                    last.then_inc(s["kv_ready"], 1)
                if c2 is not None:
                    t.wait_ge(s["yT_ready"], c2 + 1)
                    after(t, "x1_ready", c2)
                    for n in range(CT):
                        last = nt.matmul(po[:, n * P:(n + 1) * P], yT[:, n * P:(n + 1) * P], sq_sb[:, 3, :],
                                         start=True, stop=True)
                    last.then_inc(s["po_ready"], 1)
                if c1 is not None:
                    t.wait_ge(s["z1_ready"], c1 + 1)
                    after(t, "hT_ready", c1)
                    if c3 is not None:
                        t.wait_ge(s["h2_ready"], c3 + 1)
                    if c4 is not None:
                        t.wait_ge(s["logits_ready"], c4 + 1)
                    turned(z1).then_inc(s["hT_psum"], 1)

            stages(t, turn)

        s2 = {}
        for n in ("route prefix_ready totals_ready fall_exp gap_ready slots_ready rows_zero rows_moved xn_loaded "
                  "lanes_ready tiles_step tiles_ready map_used map_ready rows_step rows_ready owner_ready split "
                  "sh_gate sh_up sh_gelu sh_raw sh_act sh_out sh_taken sh_added "
                  "ready_gi ready_si xT_psum xT_ready gate_ready up_ready gelu_ready act_ready actT_psum "
                  "actT_ready y_ready yo_ready "
                  "weights_ready first_weighed first_added gather_begun scatter_begun fin_sum fin_ready fin_pow fin_nmr fin_out").split():
            s2[n] = sem("e_" + n)
        YB = 4
        gathered = [sem(f"gathered{m}") for m in range(U)]
        scattered = [sem(f"scattered{m}") for m in range(U)]
        y_loaded = [sem(f"y_loaded{m}") for m in range(YB)]
        stored = [sem(f"stored{m}") for m in range(2)]
        LAST = TILES // U - 1

        ps_a, ps_g, ps_t, ps_y, ps_x = banks[0], banks[1], banks[2], banks[3], banks[4]
        sh_ps = banks[0:2 * HS]
        sh_y, ps_map, ps_pre, ps_tot = banks[4], banks[5], banks[6], banks[7]

        first_block.close()
        experts = ctx.enter_context(nc.Block())

        @experts.sync
        def _(sp):
            sp.wait_ge(s["table_written"], CH * 16)
            sp.wait_ge(s["xnT_kept"], CH * 16)
            sp.dma_start(xn_all[:, :, :], table_v).then_inc(s2["xn_loaded"], 16)
            sp.wait_ge(s2["rows_zero"], 2)
            sp.wait_ge(s2["split"], 5)
            for n in range(3):
                for lo, hi, base in ((0, B1, 0), (B1, B2, BE2), (B2, NB, BS2)):
                    sp.dma_start(bias_rows[n:n + 1, base:base + (hi - lo) * P],
                                 bpart[n][:, lo:hi]).then_inc(s2["rows_moved"], 16)
            for m in range(U):
                sp.wait_ge(scattered[m], (LAST + 1) * 16)

            def load(c, m):
                sp.dma_start(y_first[:, ds(c * CT, CT), :], routed_v[:, 0, ds(c * CT, CT), :]).then_inc(y_loaded[m], 16)
                sp.dma_start(y_second[:, ds(c * CT, CT), :], routed_v[:, 1, ds(c * CT, CT), :]).then_inc(y_loaded[m], 16)

            for m in range(YB):
                load(m, m)
            with sp.Fori(1, CH // YB) as r:
                for m in range(YB):
                    sp.wait_ge(y_loaded[m], r * 32)
                    load(r * YB + m, m)

        def tiles(eng, group):
            group(0)
            with eng.Fori(1, LAST) as r:
                group(r)
            group(LAST)

        def after2(eng, name, count):
            if not (isinstance(count, int) and count <= 0):
                eng.wait_ge(name if not isinstance(name, str) else s2[name], count)

        def last_stage(eng, step):
            def steps(r):
                for m in range(YB):
                    step(r * YB + m, m, m % 2, r * (YB // 2) + m // 2, r)

            steps(0)
            if CH // YB > 2:
                with eng.Fori(1, CH // YB - 1) as r:
                    steps(r)
            steps(CH // YB - 1)

        def chunk_ahead(c, m, r):
            return None if isinstance(c, int) and c == CH - 1 else (c + 1, (m + 1) % YB, r + (m + 1) // YB)

        def later(c):
            return not (isinstance(c, int) and c == 0)

        @experts.gpsimd
        def _(g):
            ng = nc.gpsimd
            ng.memset(bias_rows[:, :], 0.0).then_inc(s2["rows_zero"], 1)

            def take_wait(at, name, n):
                after2(g, name, n)
                ng.tensor_tensor(g_wait[:, at:at + 1], g_wait[:, 0:1], g_wait[:, 0:1], ALU.add).then_inc(s2[name], 1)

            ng.memset(g_wait[:, :], 0.0).then_inc(s2["rows_zero"], 1)
            g.wait_ge(s2["rows_zero"], 2)

            def gather(m, n):
                after2(g, "xT_psum", n - U + 1)
                g.wait_ge(s2["ready_gi"], n + 1)
                take_wait(1, "gather_begun", n)
                ng.indirect_dma_start(xg[m][:, :], None, table,
                                      bass.IndirectOffsetOnAxis(ap=gi[m][:, 0:1], axis=0)).then_inc(gathered[m], 16)

            def scatter(m, n):
                g.wait_ge(s2["yo_ready"], n + 1)
                take_wait(2, "scatter_begun", n)
                ng.indirect_dma_start(routed, bass.IndirectOffsetOnAxis(ap=si[m][:, 0:1], axis=0), yo[m][:, :], None,
                                      bounds_check=SLOTS - 1, oob_is_err=False).then_inc(scattered[m], 16)

            def shared_act(c):
                for j in range(HS):
                    g.wait_ge(s2["sh_gelu"], c * HS + j + 1)
                    g.wait_ge(s2["sh_raw"], c * HS + j + 1)
                    ng.tensor_tensor(ash[:, j, :], ash[:, j, :], gsh[:, j, :], ALU.mult).then_inc(s2["sh_act"], 1)

            def shared_add(c):
                g.wait_ge(s2["sh_taken"], c + 1)
                ng.tensor_tensor(x_all[:, ds(c * CT, CT), :], x_all[:, ds(c * CT, CT), :],
                                 xn_all[:, ds(c * CT, CT), :], ALU.add).then_inc(s2["sh_added"], 1)

            shared_act(0)
            g.wait_ge(s2["xn_loaded"], 16)
            with g.Fori(1, CH) as c:
                shared_act(c)
                shared_add(c - 1)
            shared_add(CH - 1)

            for m in range(U):
                gather(m, m)

            def group(r):
                for m in range(U):
                    if not (isinstance(r, int) and r == LAST):
                        gather(m, r * U + m + U)
                    scatter(m, r * U + m)

            tiles(g, group)

            def power(c, b):
                g.wait_ge(s2["fin_ready"], c * 3 + 3)
                after2(g, "fin_out", c - 1)
                ng.tensor_tensor(frs[b][:, :], fve[b][:, :], half[:, :], ALU.pow).then_inc(s2["fin_pow"], 1)

            def add_first(c):
                at = ds(c * CT, CT)
                g.wait_ge(s2["first_weighed"], c + 1)
                ng.tensor_tensor(x_all[:, at, :], x_all[:, at, :], y_first[:, at, :], ALU.add).then_inc(s2["first_added"], 1)

            def step(c, m, b, uses, r):
                if later(c):
                    power(c - 1, 1 - b)
                if chunk_ahead(c, m, r):
                    add_first(c + 1)

            add_first(0)
            last_stage(g, step)
            power(CH - 1, 1)

        @experts.vector
        def _(v):
            nv = nc.vector
            done = [0]

            def routed_by(ins):
                done[0] += 1
                ins.then_inc(s2["route"], 1)
                v.wait_ge(s2["route"], done[0])

            v.wait_ge(s["expert_w_loaded"], 7 * 16)
            for n, (of, to) in enumerate(((braw, bleft), (bleft, bleft2))):
                nv.tensor_copy(bpart[n][:, :], of[:, :]).then_inc(s2["split"], 1)
                v.wait_ge(s2["split"], 2 * n + 1)
                nv.tensor_tensor(to[:, :], of[:, :], bpart[n][:, :], ALU.subtract).then_inc(s2["split"], 1)
                v.wait_ge(s2["split"], 2 * n + 2)
            nv.tensor_copy(bpart[2][:, :], bleft2[:, :]).then_inc(s2["split"], 1)

            def over(ap, n):
                return ap.unsqueeze(2).to_broadcast([P, ap.shape[1], n])

            def under(ap, n):
                return ap.unsqueeze(1).to_broadcast([P, n, ap.shape[1]])

            for k, of in enumerate((lg, lg2)):
                routed_by(nv.tensor_reduce(top[k][:, :], of[:, :, :], AX.X, ALU.max))
                routed_by(nv.tensor_tensor(eq[:, :, :], of[:, :, :], over(top[k][:, :], E), ALU.is_equal))
                routed_by(nv.tensor_tensor(eq[:, :, :], eq[:, :, :], under(keep_first[:, :], NT), ALU.mult))
                routed_by(nv.tensor_reduce(which[:, :], eq[:, :, :], AX.X, ALU.max))
                routed_by(nv.tensor_tensor(pick[k][:, :, :], under(keep_first[:, :], NT), over(which[:, :], E), ALU.is_equal))
                if k == 0:
                    routed_by(nv.scalar_tensor_tensor(lg2[:, :, :], pick[0][:, :, :], -1e30, lg[:, :, :], ALU.mult, ALU.add))
            nv.tensor_tensor(fall[:, :], top[1][:, :], top[0][:, :], ALU.subtract).then_inc(s2["gap_ready"], 1)
            routed_by(nv.tensor_tensor(sel[:, :, :], pick[0][:, :, :], pick[1][:, :, :], ALU.add))
            v.wait_ge(s2["totals_ready"], 1)
            routed_by(nv.tensor_copy(tot[:, :, :], ps_tot[:, 0:NT * E].rearrange("p (n e) -> p e n", e=E)))
            routed_by(nv.tensor_tensor_scan(incl[:, :, :].rearrange("p e n -> p (e n)"),
                                            scan_on[:, :, :].rearrange("p e n -> p (e n)"),
                                            tot[:, :, :].rearrange("p e n -> p (e n)"), 0.0, ALU.mult, ALU.add))
            routed_by(nv.tensor_tensor(more[:, :, :], over(incl[:, :, NT - 1], NT), under(thr_f[:, :], E), ALU.is_gt))
            routed_by(nv.tensor_reduce(ntl[:, :], more[:, :, :], AX.X, ALU.add))
            routed_by(nv.tensor_tensor_scan(cumt[:, :], scan_on[:, 0, 1:E + 1], ntl[:, :], 0.0, ALU.mult, ALU.add))
            routed_by(nv.tensor_tensor(start[:, :], cumt[:, :], ntl[:, :], ALU.subtract))
            routed_by(nv.tensor_scalar(start[:, :], start[:, :], float(P), None, ALU.mult))
            routed_by(nv.tensor_tensor(more[:, :, :], incl[:, :, :], tot[:, :, :], ALU.subtract))
            routed_by(nv.tensor_tensor(more[:, :, :], more[:, :, :], over(start[:, :], NT), ALU.add))
            v.wait_ge(s2["prefix_ready"], 1)
            routed_by(nv.tensor_tensor(sc_pos[:, :, :], ps_pre[:, 0:NT * E].rearrange("p (n e) -> p n e", e=E),
                                       more[:, :, :].rearrange("p e n -> p n e"), ALU.add))
            for k in range(K):
                routed_by(nv.tensor_tensor(eq[:, :, :], pick[k][:, :, :], sc_pos[:, :, :], ALU.mult))
                routed_by(nv.tensor_reduce(slot[:, k, :], eq[:, :, :], AX.X, ALU.add))
            routed_by(nv.tensor_copy(slot_i[:, :], slot[:, :, :].rearrange("p k n -> p (k n)")))
            routed_by(nv.tensor_scalar(tile_s[:, :], slot_i[:, :], P.bit_length() - 1, None, ALU.arith_shift_right))
            routed_by(nv.tensor_scalar(lane_s[:, :], slot_i[:, :], P - 1, None, ALU.bitwise_and))
            routed_by(nv.tensor_copy(tile_j[:, :], tile_s[:, :]))
            routed_by(nv.tensor_copy(lane_j[:, :], lane_s[:, :]))
            routed_by(nv.tensor_tensor(before[:, :, :], cumt[0:1, :].unsqueeze(1).to_broadcast([1, TILES, E]),
                                       lane_f[0:1, 0:TILES].unsqueeze(2).to_broadcast([1, TILES, E]), ALU.is_le))
            routed_by(nv.tensor_reduce(owner_f[:, :], before[:, :, :], AX.X, ALU.add))
            routed_by(nv.tensor_scalar(owner_f[:, :], owner_f[:, :], float(E - 1), None, ALU.min))
            nv.memset(owner[:, 0:1], 0.0)
            for m in range(U + 1):
                nv.memset(places[:, m:m + 1], float(2 ** (BITS * m)))
            routed_by(nv.tensor_copy(owner[:, 1:TILES + 1], owner_f[:, :]))
            nv.tensor_tensor(owner_at[:, :, 0:U], owner[:, 0:TILES].rearrange("o (g m) -> o g m", m=U),
                             places[:, 0:U].unsqueeze(1).to_broadcast([1, GROUPS, U]), ALU.mult)
            routed_by(nv.tensor_scalar(owner_at[:, :, U], owner[:, 1:TILES + 1].rearrange("o (g m) -> o g m", m=U)[:, :, U - 1],
                                       float(2 ** (BITS * U)), None, ALU.mult))
            routed_by(nv.tensor_reduce(packed_f[:, :], owner_at[:, :, :], AX.X, ALU.add))
            nv.tensor_copy(packed[:, :], packed_f[:, :]).then_inc(s2["owner_ready"], 1)
            v.wait_ge(s2["fall_exp"], 1)
            routed_by(nv.tensor_scalar(total[:, :], rel[:, :], 1.0, None, ALU.add))
            routed_by(nv.reciprocal(wt[0][:, :], total[:, :]))
            nv.tensor_tensor(wt[1][:, :], rel[:, :], wt[0][:, :], ALU.mult).then_inc(s2["weights_ready"], 1)
            def map_batch(q):
                after2(v, "map_used", q)
                nv.tensor_tensor(oh_lane[:, :, :], lane_j[:, ds(q * JB, JB)].unsqueeze(2).to_broadcast([P, JB, P]),
                                 lane_bf[:, :].unsqueeze(1).to_broadcast([P, JB, P]), ALU.is_equal)
                nv.tensor_tensor(oh_tile[:, :, :], tile_j[:, ds(q * JB, JB)].unsqueeze(2).to_broadcast([P, JB, TILES]),
                                 lane_bf[:, 0:TILES].unsqueeze(1).to_broadcast([P, JB, TILES]),
                                 ALU.is_equal).then_inc(s2["tiles_step"], 1)
                v.wait_ge(s2["tiles_step"], q + 1)
                nv.tensor_scalar(tile_val[:, :, 0, :], oh_tile[:, :, :], part_f[:, 0:1], None, ALU.mult)
                nv.tensor_tensor(tile_val[:, :, 1, :], oh_tile[:, :, :],
                                 left_bf[:, ds(q * JB, JB)].unsqueeze(2).to_broadcast([P, JB, TILES]),
                                 ALU.mult).then_inc(s2["tiles_ready"], 1)

            map_batch(0)
            with v.Fori(1, NQ) as q:
                map_batch(q)
            v.wait_ge(s2["map_ready"], 1)
            nv.tensor_scalar(row_f[:, :], ps_map[:, TILES:2 * TILES], -float(P), float(SLOTS), ALU.mult,
                             ALU.add).then_inc(s2["rows_step"], 1)
            v.wait_ge(s2["rows_step"], 1)
            nv.tensor_tensor(row_g[:, :], row_f[:, :], ps_map[:, 0:TILES], ALU.add).then_inc(s2["rows_step"], 1)
            v.wait_ge(s2["rows_step"], 2)
            nv.tensor_copy(row_out[:, :], row_g[:, :]).then_inc(s2["rows_step"], 1)
            v.wait_ge(s2["rows_step"], 3)
            nv.tensor_scalar(row_in[:, :], row_out[:, :], N - 1, None, ALU.bitwise_and).then_inc(s2["rows_step"], 1)
            v.wait_ge(s2["rows_step"], 4)
            for m in range(U):
                nv.tensor_copy(gi[m][:, :], row_in[:, m:m + 1]).then_inc(s2["ready_gi"], 1)

            def take_x(m, n):
                v.wait_ge(s2["xT_psum"], n + 1)
                after2(v, "up_ready", n - U + 1)
                nv.tensor_copy(xT[m][:, :], ps_x[:, 0:P]).then_inc(s2["xT_ready"], 1)

            take_x(0, 0)

            def group(r):
                for m in range(U):
                    n = r * U + m
                    final = isinstance(n, int) and n == TILES - 1
                    if not final:
                        take_x((m + 1) % U, n + 1)
                    v.wait_ge(s2["up_ready"], n + 1)
                    v.wait_ge(s2["gelu_ready"], n + 1)
                    after2(v, "actT_psum", n)
                    nv.tensor_tensor(actv[:, :], ps_a[:, 0:HR], gl[:, :], ALU.mult).then_inc(s2["act_ready"], 1)
                    if not (isinstance(r, int) and r == LAST):
                        v.wait_ge(gathered[m], (r + 1) * 16)
                        nv.tensor_copy(gi[m][:, :], row_in[:, ds(n + U, 1)]).then_inc(s2["ready_gi"], 1)
                    if not (isinstance(n, int) and n == 0):
                        give_y((m - 1) % U, n - 1, r if m else r - 1)
                    if final:
                        give_y(m, n, r)

            def give_y(m, n, r):
                after2(v, scattered[m], r * 16)
                nv.tensor_copy(si[m][:, :], row_out[:, ds(n, 1)])
                v.wait_ge(s2["y_ready"], n + 1)
                nv.tensor_copy(yo[m][:, :], ps_y[:, 0:C]).then_inc(s2["yo_ready"], 1)

            tiles(v, group)

            v.wait_ge(s2["weights_ready"], 1)

            def step(c, m, b, uses, r):
                v.wait_ge(y_loaded[m], (r + 1) * 32)
                v.wait_ge(s2["first_added"], c + 1)
                after2(v, "fin_out", c - 1)
                for t in range(CT):
                    last = nv.scalar_tensor_tensor(fin[b][:, t, :], y_second[:, ds(c * CT + t, 1), :].rearrange("p a c -> p (a c)"),
                                                   wt[1][:, ds(c * CT + t, 1)],
                                                   x_all[:, ds(c * CT + t, 1), :].rearrange("p a c -> p (a c)"), ALU.mult, ALU.add)
                last.then_inc(s2["fin_sum"], 1)
                if later(c):
                    minus(c - 1, 1 - b)
                v.wait_ge(s2["fin_sum"], c + 1)
                for t in range(CT):
                    last = nv.bn_stats(fst[b][:, t, :], fin[b][:, t, :])
                last.then_inc(s2["fin_ready"], 1)
                v.wait_ge(s2["fin_ready"], c * 3 + 1)
                nv.memset(wait_here[:, :], 0.0)
                for t in range(CT):
                    last = nv.bn_aggr(fmv[b][:, t, :], fst[b][:, t, :])
                last.then_inc(s2["fin_ready"], 1)
                v.wait_ge(s2["fin_ready"], c * 3 + 2)
                nv.tensor_scalar(fve[b][:, :], fmv[b][:, :, 1], EPS, None, ALU.add).then_inc(s2["fin_ready"], 1)

            def minus(c, b):
                v.wait_ge(s2["fin_pow"], c + 1)
                nv.scalar_tensor_tensor(fnm[b][:, :], fmv[b][:, :, 0], -1.0, frs[b][:, :],
                                        ALU.mult, ALU.mult).then_inc(s2["fin_nmr"], 1)

            last_stage(v, step)
            minus(CH - 1, 1)

        @experts.scalar
        def _(a):
            na = nc.scalar
            a.wait_ge(s2["gap_ready"], 1)
            na.activation(rel[:, :], fall[:, :], ACT.Exp, scale=1.0 / TAU).then_inc(s2["fall_exp"], 1)

            def shared(c):
                for j in range(HS):
                    a.wait_ge(s2["sh_gate"], c * HS + j + 1)
                    after2(a, "sh_act", (c - 1) * HS + j + 1)
                    na.activation(gsh[:, j, :], sh_ps[HS + j][:, :], ACT.Gelu, bias=col(BS1 + HS + j)).then_inc(s2["sh_gelu"], 1)
                for j in range(HS):
                    a.wait_ge(s2["sh_up"], c * HS + j + 1)
                    if j == 0:
                        after2(a, "sh_out", c)
                    na.activation(ash[:, j, :], sh_ps[j][:, :], ACT.Identity, bias=col(BS1 + j)).then_inc(s2["sh_raw"], 1)

            def shared_take(c):
                a.wait_ge(s2["sh_out"], c + 1)
                na.activation(x_all[:, ds(c * CT, CT), :], sh_y[:, :].rearrange("p (n c) -> p n c", c=C),
                              ACT.Copy).then_inc(s2["sh_taken"], 1)

            shared(0)
            with a.Fori(1, CH) as c:
                shared(c)
                shared_take(c - 1)
            shared_take(CH - 1)

            def turn_act(n):
                a.wait_ge(s2["actT_psum"], n + 1)
                after2(a, "y_ready", n)
                na.activation(actT[:, :], ps_t[:, 0:HR], ACT.Copy).then_inc(s2["actT_ready"], 1)

            def group(r):
                for m in range(U):
                    n = r * U + m
                    a.wait_ge(s2["gate_ready"], n + 1)
                    after2(a, "act_ready", n)
                    na.activation(gl[:, :], ps_g[:, 0:HR], ACT.Gelu).then_inc(s2["gelu_ready"], 1)
                    if not (isinstance(n, int) and n == 0):
                        turn_act(n - 1)

            tiles(a, group)
            turn_act(TILES - 1)

            def normed(c, b, uses):
                a.wait_ge(s2["fin_nmr"], c + 1)
                after2(a, stored[b], uses * 16)
                for t in range(CT):
                    last = na.activation(fo[b][:, t, :], fin[b][:, t, :], ACT.Identity,
                                         bias=fnm[b][:, t:t + 1], scale=frs[b][:, t:t + 1])
                last.then_inc(s2["fin_out"], 1)
                a.wait_ge(s2["fin_out"], c + 1)
                a.dma_start(out_v[:, ds(c * CT, CT), :], fo[b][:, :, :]).then_inc(stored[b], 16)

            def weigh(c, m, r):
                a.wait_ge(y_loaded[m], (r + 1) * 32)
                for t in range(CT):
                    row = y_first[:, ds(c * CT + t, 1), :].rearrange("p a c -> p (a c)")
                    last = na.activation(row, row, ACT.Copy, scale=wt[0][:, ds(c * CT + t, 1)])
                last.then_inc(s2["first_weighed"], 1)

            def step(c, m, b, uses, r):
                ahead = chunk_ahead(c, m, r)
                if ahead:
                    weigh(*ahead)
                if later(c):
                    normed(c - 1, 1 - b, uses - (1 - b))

            a.wait_ge(s2["weights_ready"], 1)
            weigh(0, 0, 0)
            last_stage(a, step)
            normed(CH - 1, 1, CH // 2 - 1)
            for m in range(2):
                a.wait_ge(stored[m], CH // 2 * 16)

        @experts.tensor
        def _(t):
            nt = nc.tensor
            t.wait_ge(s["expert_w_loaded"], 7 * 16)
            t.wait_ge(s["xnT_kept"], CH * 16)
            def counts():
                t.wait_ge(s2["route"], 12)
                for ps, w, name in ((ps_tot, ones_bf, "totals_ready"), (ps_pre, upper, "prefix_ready")):
                    nt.matmul(ps[:, 0:NT * E], w[:, :], sel[:, :, :].rearrange("p n e -> p (n e)"),
                              start=True, stop=True).then_inc(s2[name], 1)

            def biased(to, row, width):
                return nt.matmul(to, ones_bf[:, :], bias_rows[:, ds(row, width)], start=False, stop=True)

            def shared_in(c):
                for half_, name, free in ((HS, "sh_gate", "sh_gelu"), (0, "sh_up", "sh_raw")):
                    for j in range(HS):
                        after2(t, free, c * HS - HS + j + 1)
                        nt.matmul(sh_ps[half_ + j][:, :], ws1_sb[:, (half_ + j) * P:(half_ + j + 1) * P],
                                  xnT_all[:, ds(c * W, W)], start=True, stop=True).then_inc(s2[name], 1)

            def shared_out(c):
                t.wait_ge(s2["sh_act"], (c + 1) * HS)
                after2(t, "sh_taken", c)
                for n in range(CT):
                    for j in range(HS):
                        nt.matmul(sh_y[:, n * P:(n + 1) * P], ash[:, j, n * P:(n + 1) * P], ws2_sb[:, j, :],
                                  start=j == 0, stop=False)
                    last = biased(sh_y[:, n * P:(n + 1) * P], BS2, C)
                last.then_inc(s2["sh_out"], 1)

            def map_batch(q):
                t.wait_ge(s2["tiles_ready"], q + 1)
                for j in range(JB):
                    last = nt.matmul(ps_map[:, 0:2 * TILES], oh_lane[:, j, :],
                                     tile_val[:, j, :, :].rearrange("p a n -> p (a n)"),
                                     start=first_of(q) and j == 0, stop=last_of(q) and j == JB - 1)
                last.then_inc(s2["map_used"], 1)

            def first_of(q):
                return isinstance(q, int) and q == 0

            def last_of(q):
                return isinstance(q, int) and q == NQ - 1

            LEAD = CH - NQ + 1
            shared_in(0)
            shared_in(1)
            counts()
            t.wait_ge(s2["rows_moved"], 9 * 16)
            shared_out(0)
            with t.Fori(2, LEAD) as c:
                shared_in(c)
                shared_out(c - 1)

            def batch(q):
                map_batch(q)
                shared_in(q + LEAD)
                shared_out(q + LEAD - 1)

            batch(0)
            with t.Fori(1, NQ - 1) as q:
                batch(q)
            map_batch(NQ - 1)
            t.wait_ge(s2["map_used"], NQ)
            nt.matmul(ps_pre[:, 0:1], ones_bf[:, :], bias_rows[:, 0:1], start=True, stop=True).then_inc(s2["map_ready"], 1)
            shared_out(CH - 1)

            t.wait_ge(s2["owner_ready"], 1)

            def experts_of(r):
                word = t.value_load(packed[0:1, ds(r, 1)])
                return [t.snap((word >> (BITS * m)) & (2 ** BITS - 1)).with_bounds(min_val=0, max_val=E - 1) for m in range(U + 1)]

            def turn_x(m, n, r):
                t.wait_ge(gathered[m], (r + 1) * 16)
                after2(t, "xT_ready", n)
                nt.transpose(ps_x[:, 0:P], xg[m][:, :], ident[:, :]).then_inc(s2["xT_psum"], 1)

            def hidden(m, to, e, off):
                nt.matmul(to[:, 0:HR], xT[m][:, :], we1_sb[:, ds(e, 1), off:off + HR].rearrange("p a h -> p (a h)"),
                          start=True, stop=False)
                return biased(to[:, 0:HR], e * H1 + off, HR)

            def turn_act(n):
                t.wait_ge(s2["act_ready"], n + 1)
                after2(t, "actT_ready", n)
                for j in range(HK):
                    last = nt.transpose(ps_t[:, j * P:(j + 1) * P], actv[:, j * P:(j + 1) * P], ident[:, :])
                last.then_inc(s2["actT_psum"], 1)

            def second(n, e):
                t.wait_ge(s2["actT_ready"], n + 1)
                after2(t, "yo_ready", n)
                for j in range(HK):
                    nt.matmul(ps_y[:, 0:C], actT[:, j * P:(j + 1) * P],
                              we2_sb[:, ds(e, 1), j, :].rearrange("p a c -> p (a c)"), start=j == 0, stop=False)
                biased(ps_y[:, 0:C], BE2 + e * C, C).then_inc(s2["y_ready"], 1)

            t.wait_ge(s2["sh_taken"], CH)
            turn_x(0, 0, 0)

            def group(r):
                of_tile = experts_of(r)
                for m in range(U):
                    n, e_last, e = r * U + m, of_tile[m], of_tile[m + 1]
                    begun = not (isinstance(n, int) and n == 0)
                    t.wait_ge(s2["xT_ready"], n + 1)
                    after2(t, "gelu_ready", n)
                    hidden(m, ps_g, e, HR).then_inc(s2["gate_ready"], 1)
                    if begun:
                        turn_act(n - 1)
                    if not (isinstance(n, int) and n == TILES - 1):
                        turn_x((m + 1) % U, n + 1, r + (m + 1) // U)
                    after2(t, "act_ready", n)
                    hidden(m, ps_a, e, 0).then_inc(s2["up_ready"], 1)
                    if begun:
                        second(n - 1, e_last)
                return of_tile[-1]

            group(0)
            with t.Fori(1, LAST) as r:
                group(r)
            e_end = group(LAST)
            turn_act(TILES - 1)
            second(TILES - 1, e_end)


def kernel(**inputs):
    import numpy as np
    import concourse.bacc as bacc
    from concourse.bass_utils import run_bass_kernel_spmd

    a = {k.removeprefix("L0_"): np.asarray(v) for k, v in inputs.items()}
    columns = [a[f"attn_{n}"] for n in ("ln1_w", "ln1_b", "ln2_w", "ln2_b", "time_decay", "time_first",
                                        "tmk", "tmv", "tmr", "cmk", "cmr")]
    columns += list(a["ffn_bs1"].reshape(-1, 128))
    arrays = {
        "x": a["attn_x"],
        "vecs": np.stack(columns, axis=1),
        "rows": np.concatenate([a["attn_ln0_w"], a["attn_ln0_b"], a["ffn_br"]]),
        "sqw": np.stack([a[f"attn_{n}"].T for n in ("Wk", "Wv", "Wr", "Wo", "Wfr")]),
        "wfk": a["attn_Wfk"].T,
        "wfv": a["attn_Wfv"].T,
        "wrt": a["ffn_Wr"],
        "ws1": a["ffn_Ws1"],
        "ws2": a["ffn_Ws2"],
        "we1": a["ffn_We1"],
        "we2": a["ffn_We2"],
        "be1": a["ffn_be1"],
        "be2": a["ffn_be2"],
        "bs2": a["ffn_bs2"],
    }
    arrays = {k: np.ascontiguousarray(v) for k, v in arrays.items()}
    nc = bacc.Bacc("TRN2", target_bir_lowering=False, num_devices=1)
    aps = {k: nc.dram_tensor(k, v.shape, mybir.dt.from_np(v.dtype), kind="ExternalInput").ap() for k, v in arrays.items()}
    out = nc.dram_tensor("out", a["attn_x"].shape, mybir.dt.float32, kind="ExternalOutput").ap()
    build(nc, out=out, **aps)
    return run_bass_kernel_spmd(nc, [arrays], core_ids=[0]).results[0]["out"]
```

```python
import concourse.bass as bass
from concourse import mybir
from contextlib import ExitStack


def build(nc, x, out, vecs, rows, sqw, wfk, wfv, wrt, ws1, ws2, we1, we2, be1, be2, bs2):
    F32, BF16 = mybir.dt.float32, mybir.dt.bfloat16
    I32, U32 = mybir.dt.int32, mybir.dt.uint32
    ALU = mybir.AluOpType
    ACT = mybir.ActivationFunctionType
    AX = mybir.AxisListType
    ds = bass.ds

    B, T, C = x.shape
    P = 128
    N = B * T
    NT = N // P
    CT = 4
    CH = NT // CT
    W = CT * P
    SQ = W // T
    E = we1.shape[0]
    HR = we2.shape[1]
    HK = HR // P
    H1 = 2 * HR
    HF = wfk.shape[1] // P
    HS = ws2.shape[0] // P
    K = 2
    SLOTS = K * N
    TILES = (SLOTS + E * (P - 1)) // P
    U = 5
    assert TILES % U == 0
    EPS, NEG, TAU = 1e-5, -1e38, 1.5
    JB = 8
    NJ = K * NT
    NQ = NJ // JB

    x_v = x.rearrange("b t c -> (b t) c").rearrange("(n p) c -> p n c", p=P)
    out_v = out.rearrange("b t c -> (b t) c").rearrange("(n p) c -> p n c", p=P)
    table = nc.dram_tensor("token_table", (N, C), F32, kind="Internal").ap()
    table_v = table.rearrange("(n p) c -> p n c", p=P)
    routed = nc.dram_tensor("routed_rows", (SLOTS, C), F32, kind="Internal").ap()
    routed_v = routed.rearrange("(k n p) c -> p k n c", p=P, k=K)

    ctx = ExitStack()
    with ctx:
        def sb(name, shape, dt=F32):
            return ctx.enter_context(nc.sbuf_tensor(name, shape, dt))

        def sem(name):
            return ctx.enter_context(nc.semaphore(name))

        x_all = sb("x_all", [P, NT, C])
        x0_all = sb("x0_all", [P, NT, C])
        xnT_all = sb("xnT_all", [P, N])
        y_first = x0_all
        y_second = xnT_all[:, :].rearrange("p (n c) -> p n c", c=C)
        we1_sb = sb("we1_sb", [P, E, H1])
        we2_sb = sb("we2_sb", [P, E, HK, C])
        BE2, BS2 = E * H1, E * H1 + E * C
        sq_sb = sb("sq_sb", [P, 5, C])
        mixa = sb("mixa", [P, 3, C])
        mixb = sb("mixb", [P, 3, C])
        wfk_sb = sb("wfk_sb", [P, HF * P])
        wfv_sb = sb("wfv_sb", [P, HF, C])
        wrt_sb = sb("wrt_sb", [P, E])
        ws1_sb = sb("ws1_sb", [P, 2 * HS * P])
        ws2_sb = sb("ws2_sb", [P, HS, C])
        NV = vecs.shape[1]
        v_sb = sb("v_sb", [P, NV])
        LN1W, LN1B, LN2W, LN2B, DECAY, FIRST, TMK, TMV, TMR, CMK, CMR, BS1 = range(12)
        NB = (E * H1 + E * C + C) // P
        braw = sb("braw", [P, NB])
        bleft = sb("bleft", [P, NB])
        bleft2 = sb("bleft2", [P, NB])
        bpart = [sb(f"bpart{n}", [P, NB], BF16) for n in range(3)]
        B1, B2 = E * H1 // P, (E * H1 + E * C) // P
        rows_sb = sb("rows_sb", [P, 2 * C + E])
        ln0w, ln0b, br_sb = rows_sb[:, 0:C], rows_sb[:, C:2 * C], rows_sb[:, 2 * C:2 * C + E]
        mix2 = sb("mix2", [P, 2, C])
        dec = sb("dec", [P, 6])

        def col(n):
            return v_sb[:, n:n + 1]

        ident = sb("ident", [P, P])
        ones_bf = sb("ones_bf", [P, P], BF16)
        upper = sb("upper", [P, P], BF16)
        lane_i = sb("lane_i", [P, P], I32)
        lane_bf = sb("lane_bf", [P, P], BF16)
        lane_f = sb("lane_f", [P, P])
        part_i = sb("part_i", [P, 1], I32)
        part_f = sb("part_f", [P, 1])
        left_i = sb("left_i", [P, NJ], I32)
        left_bf = sb("left_bf", [P, NJ], BF16)
        thr_i = sb("thr_i", [P, NT], I32)
        thr_f = sb("thr_f", [P, NT])
        keep_first = sb("keep_first", [P, E])
        keep_i = sb("keep_i", [P, E], I32)
        scan_on = sb("scan_on", [P, E, NT])
        half = sb("half", [P, CT])
        eps4 = sb("eps4", [P, CT])
        minus4 = sb("minus4", [P, CT])
        wait_here = sb("wait_here", [1, 1])
        g_wait = sb("g_wait", [1, 3])

        lg = sb("lg", [P, NT, E])

        block_buffers = ExitStack()

        def tmp(name, shape, dt=F32):
            return block_buffers.enter_context(nc.sbuf_tensor(name, shape, dt))

        bst = {n: tmp(f"bst{n}", [P, CT, 6]) for n in "0123"}
        mv = {n: tmp(f"mv{n}", [P, CT, 2]) for n in "0123"}
        veps = {n: tmp(f"veps{n}", [P, CT]) for n in "0123"}
        negm = {n: tmp(f"negm{n}", [P, CT]) for n in "0123"}
        rstd = {n: tmp(f"rstd{n}", [P, CT]) for n in "0123"}
        nmr = {n: tmp(f"nmr{n}", [P, CT]) for n in "0123"}
        z0 = tmp("z0", [P, CT, C])
        z0w = tmp("z0w", [P, CT, C])
        z1 = tmp("z1", [P, CT, C])
        hT = tmp("hT", [P, SQ, T + 1])
        pp = tmp("pp", [P, SQ, T + 1])
        ab = tmp("ab", [P, 2, SQ, T + 1])
        gap = tmp("gap", [P, 2, W])
        below_p = tmp("below_p", [P, 2, W])
        below_m = tmp("below_m", [P, 2, W])
        e_plus = tmp("e_plus", [P, 2, W])
        e_minus = tmp("e_minus", [P, 2, W])
        old_in_state, new_in_output = e_plus[:, 0, :], e_plus[:, 1, :]
        new_in_state, old_in_output = e_minus[:, 0, :], e_minus[:, 1, :]
        e2v = tmp("e2v", [P, W])
        new_v = tmp("new_v", [P, W])
        nd = tmp("nd", [P, 2, W])
        th = tmp("th", [P, W])
        rec = tmp("rec", [P, W])
        yT = tmp("yT", [P, W])
        x1c = tmp("x1c", [P, CT, C])
        z2 = tmp("z2", [P, CT, C])
        h2T = tmp("h2T", [P, SQ, T + 1])
        d2 = tmp("d2", [P, SQ, T])
        xk2 = tmp("xk2", [P, W])
        kf = tmp("kf", [P, HF, W])
        th2 = tmp("th2", [P, W])
        x2c = tmp("x2c", [P, W])
        s13 = tmp("s13", [P, CT, C])
        x3c = tmp("x3c", [P, CT, C])
        xnc = tmp("xnc", [P, CT, C])
        xnTc = tmp("xnTc", [P, W])

        block_buffers.close()
        xn_all = sb("xn_all", [P, NT, C])
        bias_rows = sb("bias_rows", [P, E * H1 + E * C + C], BF16)
        top = [sb(f"top{k}", [P, NT]) for k in range(K)]
        which = sb("which", [P, NT])
        fall = sb("fall", [P, NT])
        rel = sb("rel", [P, NT])
        total = sb("total", [P, NT])
        wt = [sb(f"wt{k}", [P, NT]) for k in range(K)]
        ntl = sb("ntl", [P, E])
        cumt = sb("cumt", [P, E])
        start = sb("start", [P, E])
        slot = sb("slot", [P, K, NT])
        slot_i = sb("slot_i", [P, NJ], I32)
        lane_s = sb("lane_s", [P, NJ], I32)
        tile_s = sb("tile_s", [P, NJ], I32)
        lane_j = sb("lane_j", [P, NJ], BF16)
        tile_j = sb("tile_j", [P, NJ], BF16)
        owner_f = sb("owner_f", [1, TILES])
        owner = sb("owner", [1, TILES + U])
        GROUPS = TILES // U
        BITS = (E - 1).bit_length()
        SPAN = U + 2
        LOW = 4
        assert LOW * BITS < 24 and (SPAN - LOW) * BITS < 24 and SPAN * BITS < 32
        places = sb("places", [1, SPAN])
        owner_at = sb("owner_at", [1, GROUPS, SPAN])
        part_of = [sb(f"part_of{n}", [1, GROUPS]) for n in range(2)]
        part_int = [sb(f"part_int{n}", [1, GROUPS], I32) for n in range(2)]
        packed = sb("packed", [1, GROUPS], I32)
        oh_lane = [sb(f"oh_lane{b}", [P, JB, P], BF16) for b in range(2)]
        oh_tile = [sb(f"oh_tile{b}", [P, JB, TILES], BF16) for b in range(2)]
        tile_val = [sb(f"tile_val{b}", [P, JB, 2, TILES], BF16) for b in range(2)]
        row_f = sb("row_f", [P, TILES])
        row_g = sb("row_g", [P, TILES])
        row_out = sb("row_out", [P, TILES], U32)
        row_in = sb("row_in", [P, TILES], U32)
        gsh = sb("gsh", [P, HS, W])
        ash = sb("ash", [P, HS, W])
        routing_buffers = ExitStack()

        def scratch(name, shape, dt=F32):
            return routing_buffers.enter_context(nc.sbuf_tensor(name, shape, dt))

        sc_pos = scratch("sc_pos", [P, NT, E])
        eq = scratch("eq", [P, NT, E])
        pick = [scratch(f"pick{k}", [P, NT, E]) for k in range(K)]
        lg2 = scratch("lg2", [P, NT, E])
        sel = scratch("sel", [P, NT, E], BF16)
        tot = scratch("tot", [P, E, NT])
        incl = scratch("incl", [P, E, NT])
        more = scratch("more", [P, E, NT])
        before = scratch("before", [1, TILES, E])
        routing_buffers.close()
        xg = [sb(f"xg{m}", [P, C]) for m in range(U)]
        xT = [sb(f"xT{m}", [P, P]) for m in range(U)]
        gi = [sb(f"gi{m}", [P, 1], U32) for m in range(U)]
        si = [sb(f"si{m}", [P, 1], U32) for m in range(U)]
        gl = sb("gl", [P, HR])
        actv = sb("actv", [P, HR])
        actT = sb("actT", [P, HR])
        yo = [sb(f"yo{m}", [P, C]) for m in range(U)]
        fin = [gsh[:, m, :].rearrange("p (n c) -> p n c", c=C) for m in range(2)]
        fo = [ash[:, m, :].rearrange("p (n c) -> p n c", c=C) for m in range(2)]
        fst = [sb(f"fst{m}", [P, CT, 6]) for m in range(2)]
        fmv = [sb(f"fmv{m}", [P, CT, 2]) for m in range(2)]
        fve = [sb(f"fve{m}", [P, CT]) for m in range(2)]
        fne = [sb(f"fne{m}", [P, CT]) for m in range(2)]
        frs = [sb(f"frs{m}", [P, CT]) for m in range(2)]
        fnm = [sb(f"fnm{m}", [P, CT]) for m in range(2)]

        banks = [ctx.enter_context(nc.psum_tensor(f"bank{i}", [P, 512], F32)) for i in range(8)]
        pk, pv, pr, pT, pf0, pf1, pkv, po = banks
        pf = (pf0, pf1)

        s = {}
        for n in ("w_loaded mix_w_ready x_loaded consts pool_consts edges scaled "
                  "bn0 bn1 bn2 bn3 pow0 pow1 pow2 pow3 nmr0 nmr1 nmr2 nmr3 "
                  "z0_ready z0w_ready x0_ready z1_ready hT_psum hT_ready k_ready v_ready r_ready "
                  "pp_ready delta_ready gaps_ready exp_ready ev_ready states_ready rec_ready s13_ready y_half nd_ready den_ready th_ready yT_ready "
                  "po_ready x1_ready z2_ready h2_psum h2_ready d2_ready mixed2 fk_ready relu_done "
                  "sq_pool sq_act r2_ready th2_ready kv_ready x2_step x3_ready xn_ready xnT_psum xnT_ready "
                  "logits_psum logits_ready table_written xnT_kept expert_w_loaded iotas").split():
            s[n] = sem(n)

        first_block = ExitStack()
        block = first_block.enter_context(nc.Block())

        @block.sync
        def _(sp):
            sp.dma_start(x_all[:, 0:CT, :], x_v[:, 0:CT, :]).then_inc(s["x_loaded"], 16)
            sp.dma_start(rows_sb[:, :], rows.partition_broadcast(P)).then_inc(s["w_loaded"], 16)
            sp.dma_start(v_sb[:, :], vecs).then_inc(s["w_loaded"], 16)
            sp.dma_start(sq_sb[:, :, :], sqw.rearrange("s p c -> p s c")).then_inc(s["w_loaded"], 16)
            sp.dma_start(wfk_sb[:, :], wfk).then_inc(s["w_loaded"], 16)
            sp.dma_start(wfv_sb[:, :, :], wfv.rearrange("(j p) c -> p j c", p=P)).then_inc(s["w_loaded"], 16)
            sp.dma_start(wrt_sb[:, :], wrt).then_inc(s["w_loaded"], 16)
            with sp.Fori(1, CH) as c:
                sp.wait_ge(s["x_loaded"], c * 16)
                sp.dma_start(x_all[:, ds(c * CT, CT), :], x_v[:, ds(c * CT, CT), :]).then_inc(s["x_loaded"], 16)
            for to, of in ((braw[:, 0:B1], be1.rearrange("e h -> (e h)").rearrange("(p a) -> p a", a=B1)),
                           (braw[:, B1:B2], be2.rearrange("e h -> (e h)").rearrange("(p a) -> p a", a=B2 - B1)),
                           (braw[:, B2:NB], bs2.rearrange("(p a) -> p a", a=NB - B2)),
                           (ws1_sb[:, :], ws1), (ws2_sb[:, :, :], ws2.rearrange("(j p) c -> p j c", p=P)),
                           (we1_sb[:, :, :], we1.rearrange("e d h -> d e h")),
                           (we2_sb[:, :, :, :], we2.rearrange("e (j p) c -> p e j c", p=P))):
                sp.dma_start(to, of).then_inc(s["expert_w_loaded"], 16)
            with sp.Fori(0, CH) as c:
                sp.wait_ge(s["xn_ready"], c + 1)
                sp.dma_start(table_v[:, ds(c * CT, CT), :], xnc[:, :, :]).then_inc(s["table_written"], 16)
                sp.wait_ge(s["xnT_ready"], c + 1)
                sp.dma_start(xnT_all[:, ds(c * W, W)], xnTc[:, :]).then_inc(s["xnT_kept"], 16)

        DEPTH = 4

        def pipeline(eng, turn):
            def run(i):
                def at(lag, step, *args):
                    if not isinstance(i, int) or 0 <= i - lag < CH:
                        step(i - lag, *args)

                turn(i, at)

            for i in range(DEPTH):
                run(i)
            with eng.Fori(DEPTH, CH) as i:
                run(i)
            for i in range(CH, CH + DEPTH):
                run(i)

        def after(eng, name, count):
            if not (isinstance(count, int) and count <= 0):
                eng.wait_ge(s[name], count)

        @block.vector
        def _(v):
            nv = nc.vector
            nv.memset(hT[:, :, 0:1], 0.0)
            nv.memset(h2T[:, :, 0:1], 0.0)
            nv.memset(pp[:, :, 0:1], NEG)
            nv.memset(ab[:, :, :, 0:1], 0.0)
            nv.memset(ones_bf[:, :], 1.0)
            nv.memset(scan_on[:, :, :], 1.0)
            nv.memset(eps4[:, :], EPS)
            nv.memset(minus4[:, :], -1.0)
            nv.memset(half[:, :], -0.5).then_inc(s["edges"], 1)
            def prepare():
                v.wait_ge(s["w_loaded"], 6 * 16)
                nv.tensor_scalar(dec[:, 1:2], col(CMR), -1.0, 1.0, ALU.mult, ALU.add)
                nv.tensor_scalar(dec[:, 2:5], v_sb[:, TMK:TMR + 1], -1.0, 1.0, ALU.mult, ALU.add).then_inc(s["scaled"], 1)
                v.wait_ge(s["scaled"], 1)
                for n in range(3):
                    nv.tensor_scalar(mixa[:, n, :], sq_sb[:, n, :], col(TMK + n), None, ALU.mult)
                    last = nv.tensor_scalar(mixb[:, n, :], sq_sb[:, n, :], dec[:, 2 + n:3 + n], None, ALU.mult)
                nv.tensor_scalar(mix2[:, 0, :], sq_sb[:, 4, :], col(CMR), None, ALU.mult)
                last = nv.tensor_scalar(mix2[:, 1, :], sq_sb[:, 4, :], dec[:, 1:2], None, ALU.mult)
                last.then_inc(s["mix_w_ready"], 1)
                v.wait_ge(s["consts"], 1)
                nv.tensor_scalar(dec[:, 0:1], dec[:, 5:6], -1.0, None, ALU.mult).then_inc(s["scaled"], 1)
                v.wait_ge(s["scaled"], 2)
                nv.memset(scan_on[:, :, 0:1], 0.0)
                v.wait_ge(s["iotas"], 1)
                nv.tensor_copy(lane_bf[:, :], lane_i[:, :])
                nv.tensor_copy(lane_f[:, :], lane_i[:, :])
                nv.tensor_copy(part_f[:, :], part_i[:, :])
                nv.tensor_copy(left_bf[:, :], left_i[:, :])
                nv.tensor_copy(thr_f[:, :], thr_i[:, :])
                nv.tensor_copy(keep_first[:, :], keep_i[:, :]).then_inc(s["scaled"], 1)

            def stats(n, tiles, c):
                bn = s["bn" + n]
                for t in range(CT):
                    last = nv.bn_stats(bst[n][:, t, :], tiles[:, t, :])
                last.then_inc(bn, 1)
                v.wait_ge(bn, c * 2 + 1)
                nv.memset(wait_here[:, :], 0.0)
                for t in range(CT):
                    last = nv.bn_aggr(mv[n][:, t, :], bst[n][:, t, :])
                last.then_inc(bn, 1)

            def stats0(c):
                after(v, "nmr0", c)
                v.wait_ge(s["x_loaded"], (c + 1) * 16)
                stats("0", x_all[:, ds(c * CT, CT), :], c)

            def stats1(c):
                after(v, "nmr1", c)
                v.wait_ge(s["x0_ready"], c + 1)
                stats("1", x0_all[:, ds(c * CT, CT), :], c)

            def stats2(c):
                after(v, "nmr2", c)
                v.wait_ge(s["x1_ready"], c + 1)
                stats("2", x1c, c)

            def stats3(c):
                after(v, "nmr3", c)
                v.wait_ge(s["x3_ready"], c + 1)
                stats("3", x3c, c)

            def by_sequence(ap):
                return ap.rearrange("p (q t) -> p q t", t=T)

            def maximum(c):
                after(v, "delta_ready", c)
                v.wait_ge(s["k_ready"], c + 1)
                for q in range(SQ):
                    last = nv.tensor_tensor_scan(pp[:, q, 1:T + 1], dec[:, 0:1].to_broadcast([P, T]),
                                                 pk[:, q * T:(q + 1) * T], NEG, ALU.add, ALU.max)
                last.then_inc(s["pp_ready"], 1)

            def gaps(c):
                after(v, "gaps_ready", c)
                v.wait_ge(s["pp_ready"], c + 1)
                nv.scalar_tensor_tensor(by_sequence(gap[:, 0, :]), pp[:, :, 0:T], dec[:, 0:1], by_sequence(pk[:, :]),
                                        ALU.add, ALU.subtract)
                nv.scalar_tensor_tensor(by_sequence(gap[:, 1, :]), by_sequence(pk[:, :]), col(FIRST), pp[:, :, 0:T],
                                        ALU.add, ALU.subtract).then_inc(s["delta_ready"], 1)

            def weigh_v(c):
                after(v, "states_ready", c)
                after(v, "den_ready", c)
                v.wait_ge(s["exp_ready"], c + 1)
                v.wait_ge(s["v_ready"], c + 1)
                nv.tensor_tensor(e2v[:, :], new_in_state, pv[:, :], ALU.mult)
                nv.tensor_tensor(new_v[:, :], new_in_output, pv[:, :], ALU.mult).then_inc(s["ev_ready"], 1)

            def states(c):
                after(v, "nd_ready", c)
                v.wait_ge(s["ev_ready"], c + 1)
                for q in range(SQ):
                    at = slice(q * T, (q + 1) * T)
                    nv.tensor_tensor_scan(ab[:, 0, q, 1:T + 1], old_in_state[:, at], e2v[:, at], 0.0, ALU.mult, ALU.add)
                    last = nv.tensor_tensor_scan(ab[:, 1, q, 1:T + 1], old_in_state[:, at], new_in_state[:, at], 0.0,
                                                 ALU.mult, ALU.add)
                last.then_inc(s["states_ready"], 1)

            def carried(c):
                after(v, "yT_ready", c)
                v.wait_ge(s["states_ready"], c + 1)
                for n in range(2):
                    last = nv.tensor_tensor(by_sequence(nd[:, n, :]), ab[:, n, :, 0:T], by_sequence(old_in_output), ALU.mult)
                last.then_inc(s["nd_ready"], 1)

            def one_over(c):
                after(v, "yT_ready", c)
                v.wait_ge(s["den_ready"], c + 1)
                nv.reciprocal(rec[:, :], nd[:, 1, :]).then_inc(s["rec_ready"], 1)

            def output(c):
                v.wait_ge(s["den_ready"], c + 1)
                v.wait_ge(s["th_ready"], c + 1)
                after(v, "po_ready", c)
                nv.scalar_tensor_tensor(yT[:, :], th[:, :], 1.0, nd[:, 0, :], ALU.add, ALU.mult).then_inc(s["y_half"], 1)
                v.wait_ge(s["y_half"], c + 1)
                v.wait_ge(s["rec_ready"], c + 1)
                nv.scalar_tensor_tensor(yT[:, :], yT[:, :], 0.5, rec[:, :], ALU.mult, ALU.mult).then_inc(s["yT_ready"], 1)

            def mix(c):
                v.wait_ge(s["d2_ready"], c + 1)
                after(v, "fk_ready", c * HF)
                nv.scalar_tensor_tensor(by_sequence(xk2[:, :]), d2[:, :, :], col(CMK), h2T[:, :, 0:T],
                                        ALU.mult, ALU.add).then_inc(s["mixed2"], 1)

            def x3(c):
                v.wait_ge(s["th2_ready"], c + 1)
                v.wait_ge(s["kv_ready"], c + 1)
                after(v, "x3_ready", c)
                nv.scalar_tensor_tensor(x2c[:, :], th2[:, :], 1.0, pkv[:, :], ALU.add, ALU.mult).then_inc(s["x2_step"], 1)
                v.wait_ge(s["x2_step"], c + 1)
                v.wait_ge(s["s13_ready"], c + 1)
                after(v, "xn_ready", c)
                nv.scalar_tensor_tensor(x3c[:, :, :].rearrange("p n c -> p (n c)"), x2c[:, :], 0.5,
                                        s13[:, :, :].rearrange("p n c -> p (n c)"),
                                        ALU.mult, ALU.add).then_inc(s["x3_ready"], 1)

            def logits(c):
                v.wait_ge(s["logits_psum"], c + 1)
                nv.tensor_tensor(lg[:, ds(c * CT, CT), :], pT[:, 0:CT * E].rearrange("p (n e) -> p n e", e=E),
                                 br_sb.unsqueeze(1).to_broadcast([P, CT, E]), ALU.add).then_inc(s["logits_ready"], 1)

            def turn(i, at):
                at(0, stats0)
                if isinstance(i, int) and i == 0:
                    prepare()
                at(3, stats2)
                at(2, weigh_v)
                at(4, x3)
                at(4, stats3)
                at(2, states)
                at(2, carried)
                at(1, maximum)
                at(3, mix)
                at(1, gaps)
                at(2, one_over)
                at(2, output)
                at(0, stats1)
                at(4, logits)

            pipeline(v, turn)

        @block.scalar
        def _(a):
            na = nc.scalar
            a.wait_ge(s["w_loaded"], 6 * 16)
            na.activation(dec[:, 5:6], col(DECAY), ACT.Exp).then_inc(s["consts"], 1)

            def apply(n, to, of):
                for t in range(CT):
                    last = na.activation(to[:, t, :], of[:, t, :], ACT.Identity,
                                         bias=nmr[n][:, t:t + 1], scale=rstd[n][:, t:t + 1])
                return last

            def norm0(c):
                a.wait_ge(s["nmr0"], c + 1)
                after(a, "z0w_ready", c)
                apply("0", z0, x_all[:, ds(c * CT, CT), :]).then_inc(s["z0_ready"], 1)

            def norm1(c):
                a.wait_ge(s["nmr1"], c + 1)
                after(a, "hT_psum", c)
                apply("1", z1, x0_all[:, ds(c * CT, CT), :]).then_inc(s["z1_ready"], 1)

            def norm2(c):
                a.wait_ge(s["nmr2"], c + 1)
                after(a, "h2_psum", c)
                apply("2", z2, x1c).then_inc(s["z2_ready"], 1)

            def norm3(c):
                a.wait_ge(s["nmr3"], c + 1)
                after(a, "xnT_psum", c)
                after(a, "table_written", c * 16)
                apply("3", xnc, x3c).then_inc(s["xn_ready"], 1)

            def affine1(c):
                a.wait_ge(s["hT_psum"], c + 1)
                after(a, "r_ready", c)
                na.activation(hT[:, :, 1:T + 1], pT[:, :].rearrange("p (q t) -> p q t", t=T), ACT.Identity,
                              bias=col(LN1B), scale=col(LN1W)).then_inc(s["hT_ready"], 1)

            def affine2(c):
                a.wait_ge(s["h2_psum"], c + 1)
                after(a, "mixed2", c)
                after(a, "r2_ready", c)
                na.activation(h2T[:, :, 1:T + 1], pT[:, :].rearrange("p (q t) -> p q t", t=T), ACT.Identity,
                              bias=col(LN2B), scale=col(LN2W)).then_inc(s["h2_ready"], 1)

            def by_channel(c):
                a.wait_ge(s["xnT_psum"], c + 1)
                after(a, "logits_psum", c)
                after(a, "xnT_kept", c * 16)
                na.activation(xnTc[:, :], pT[:, :], ACT.Copy).then_inc(s["xnT_ready"], 1)

            def below(c):
                a.wait_ge(s["delta_ready"], c + 1)
                after(a, "exp_ready", c)
                na.activation(below_p[:, :, :], gap[:, :, :], ACT.Relu, scale=-1.0)
                na.activation(below_m[:, :, :], gap[:, :, :], ACT.Relu).then_inc(s["gaps_ready"], 1)

            def factors(c):
                a.wait_ge(s["gaps_ready"], c + 1)
                after(a, "den_ready", c)
                na.activation(e_plus[:, :, :], below_p[:, :, :], ACT.Exp, scale=-1.0)
                na.activation(e_minus[:, :, :], below_m[:, :, :], ACT.Exp, scale=-1.0).then_inc(s["exp_ready"], 1)

            def x1(c):
                after(a, "s13_ready", c)
                after(a, "z2_ready", c)
                a.wait_ge(s["po_ready"], c + 1)
                na.activation(x1c[:, :, :], po[:, :].rearrange("p (n c) -> p n c", c=C), ACT.Copy).then_inc(s["x1_ready"], 1)

            def gate(c):
                a.wait_ge(s["r_ready"], c + 1)
                after(a, "y_half", c)
                na.activation(th[:, :], pr[:, :], ACT.Tanh, scale=0.5).then_inc(s["th_ready"], 1)

            def gate2(c):
                a.wait_ge(s["r2_ready"], c + 1)
                after(a, "x2_step", c)
                na.activation(th2[:, :], pr[:, :], ACT.Tanh, scale=0.5).then_inc(s["th2_ready"], 1)

            def relu(c, j):
                a.wait_ge(s["fk_ready"], c * HF + j + 1)
                if j < 2:
                    after(a, "kv_ready", c)
                na.activation(kf[:, j, :], pf[j % 2][:, :], ACT.Relu).then_inc(s["relu_done"], 1)

            def square(c, j):
                a.wait_ge(s["relu_done"], c * HF + j + 1)
                na.activation(kf[:, j, :], kf[:, j, :], ACT.Square).then_inc(s["sq_act"], 1)

            def turn(i, at):
                at(4, relu, 1)
                at(2, below)
                at(4, square, 1)
                at(4, relu, 2)
                at(4, relu, 3)
                at(4, square, 3)
                at(2, factors)
                at(3, x1)
                at(1, norm1)
                at(1, affine1)
                at(3, norm2)
                at(3, affine2)
                at(2, gate)
                at(4, norm3)
                at(0, norm0)
                at(3, gate2)
                at(4, by_channel)
                at(3, relu, 0)

            pipeline(a, turn)

        def over_deviation(g, ve, nm, rs, nmr_, mv_, step, c, ready):
            ng = nc.gpsimd
            ng.tensor_tensor(ve[:, :], mv_[:, :, 1], eps4[:, :], ALU.add)
            ng.tensor_tensor(nm[:, :], mv_[:, :, 0], minus4[:, :], ALU.mult).then_inc(step, 1)
            g.wait_ge(step, c * 2 + 1)
            ng.tensor_tensor(rs[:, :], ve[:, :], half[:, :], ALU.pow).then_inc(step, 1)
            g.wait_ge(step, c * 2 + 2)
            ng.tensor_tensor(nmr_[:, :], nm[:, :], rs[:, :], ALU.mult).then_inc(ready, 1)

        @block.gpsimd
        def _(g):
            ng = nc.gpsimd
            ng.memset(ident[:, :], 0.0).then_inc(s["pool_consts"], 1)
            g.wait_ge(s["pool_consts"], 1)
            ng.affine_select(out=ident[:, :], in_=ident[:, :], compare_op=ALU.not_equal, fill=1.0,
                             base=0, pattern=[[-1, P]], channel_multiplier=1).then_inc(s["pool_consts"], 1)
            g.wait_ge(s["edges"], 1)
            ng.affine_select(out=upper[:, :], in_=ones_bf[:, :], compare_op=ALU.is_gt, fill=0.0,
                             base=0, pattern=[[1, P]], channel_multiplier=-1)
            ng.iota(lane_i[:, :], pattern=[[1, P]], base=0, channel_multiplier=0)
            ng.iota(part_i[:, :], pattern=[[1, 1]], base=0, channel_multiplier=1)
            ng.iota(left_i[:, :], pattern=[[-1, NJ]], base=NJ, channel_multiplier=0)
            ng.iota(thr_i[:, :], pattern=[[P, NT]], base=0, channel_multiplier=0)
            ng.iota(keep_i[:, :], pattern=[[-1, E]], base=E, channel_multiplier=0).then_inc(s["iotas"], 1)
            def deviation(c, n):
                g.wait_ge(s["bn" + n], c * 2 + 2)
                after(g, ("z0_ready", "z1_ready", "z2_ready", "xn_ready")[int(n)], c)
                over_deviation(g, veps[n], negm[n], rstd[n], nmr[n], mv[n], s["pow" + n], c, s["nmr" + n])

            def weigh0(c):
                if isinstance(c, int) and c == 0:
                    g.wait_ge(s["w_loaded"], 6 * 16)
                g.wait_ge(s["z0_ready"], c + 1)
                after(g, "x0_ready", c)
                ng.tensor_tensor(z0w[:, :, :], z0[:, :, :], ln0w.unsqueeze(1).to_broadcast([P, CT, C]),
                                 ALU.mult).then_inc(s["z0w_ready"], 1)

            def shift0(c):
                g.wait_ge(s["z0w_ready"], c + 1)
                ng.tensor_tensor(x0_all[:, ds(c * CT, CT), :], z0w[:, :, :],
                                 ln0b.unsqueeze(1).to_broadcast([P, CT, C]), ALU.add).then_inc(s["x0_ready"], 1)

            def change(c):
                g.wait_ge(s["h2_ready"], c + 1)
                after(g, "mixed2", c)
                ng.tensor_tensor(d2[:, :, :], h2T[:, :, 1:T + 1], h2T[:, :, 0:T], ALU.subtract).then_inc(s["d2_ready"], 1)

            def add_new(c):
                g.wait_ge(s["nd_ready"], c + 1)
                ng.tensor_tensor(nd[:, 0, :], nd[:, 0, :], new_v[:, :], ALU.add)
                ng.tensor_tensor(nd[:, 1, :], nd[:, 1, :], new_in_output, ALU.add).then_inc(s["den_ready"], 1)

            def square(c, j):
                g.wait_ge(s["relu_done"], c * HF + j + 1)
                ng.tensor_tensor(kf[:, j, :], kf[:, j, :], kf[:, j, :], ALU.mult).then_inc(s["sq_pool"], 1)

            def residual(c):
                g.wait_ge(s["x1_ready"], c + 1)
                after(g, "x3_ready", c)
                ng.tensor_tensor(s13[:, :, :], x1c[:, :, :], x_all[:, ds(c * CT, CT), :], ALU.add).then_inc(s["s13_ready"], 1)

            def turn(i, at):
                at(0, deviation, "0")
                at(4, deviation, "3")
                at(3, change)
                at(2, add_new)
                at(0, weigh0)
                at(0, shift0)
                at(3, residual)
                at(3, square, 0)
                at(3, square, 2)
                at(0, deviation, "1")
                at(2, deviation, "2")

            pipeline(g, turn)

        @block.tensor
        def _(t):
            nt = nc.tensor
            t.wait_ge(s["w_loaded"], 6 * 16)
            t.wait_ge(s["mix_w_ready"], 1)
            t.wait_ge(s["pool_consts"], 2)
            t.wait_ge(s["edges"], 1)

            def turned(of):
                for n in range(CT):
                    last = nt.transpose(pT[:, n * P:(n + 1) * P], of[:, n, :], ident[:, :])
                return last

            def bank_free(i, *uses):
                for name, chunks in uses[:1] if not isinstance(i, int) else uses:
                    after(t, name, min(chunks, CH) if isinstance(i, int) else chunks)

            def mixed(c, n, to, name):
                o = to[:, :].rearrange("p (q t) -> p q t", t=T)
                nt.matmul(o, mixa[:, n, :], hT[:, :, 1:T + 1], start=True, stop=False)
                nt.matmul(o, mixb[:, n, :], hT[:, :, 0:T], start=False, stop=True).then_inc(s[name], 1)

            def keys(c):
                t.wait_ge(s["hT_ready"], c + 1)
                after(t, "delta_ready", c)
                mixed(c, 0, pk, "k_ready")

            def values(c):
                t.wait_ge(s["hT_ready"], c + 1)
                after(t, "ev_ready", c)
                mixed(c, 1, pv, "v_ready")

            def receptance(c, i):
                t.wait_ge(s["hT_ready"], c + 1)
                bank_free(i, *receptance_bank(i))
                mixed(c, 2, pr, "r_ready")

            def turn1(c, i):
                t.wait_ge(s["z1_ready"], c + 1)
                bank_free(i, *turn1_bank(i))
                turned(z1).then_inc(s["hT_psum"], 1)

            def turn2(c, i):
                t.wait_ge(s["z2_ready"], c + 1)
                bank_free(i, *turn2_bank(i))
                turned(z2).then_inc(s["h2_psum"], 1)

            def turn3(c, i):
                t.wait_ge(s["xn_ready"], c + 1)
                bank_free(i, *turn3_bank(i))
                turned(xnc).then_inc(s["xnT_psum"], 1)

            def router(c, i):
                t.wait_ge(s["xnT_ready"], c + 1)
                bank_free(i, *router_bank(i))
                for n in range(CT):
                    last = nt.matmul(pT[:, n * E:(n + 1) * E], xnTc[:, n * P:(n + 1) * P], wrt_sb[:, :],
                                     start=True, stop=True)
                last.then_inc(s["logits_psum"], 1)

            def hidden(c, j):
                if j == 0:
                    t.wait_ge(s["mixed2"], c + 1)
                after(t, "relu_done", c * HF + (j - 1))
                nt.matmul(pf[j % 2][:, :], wfk_sb[:, j * P:(j + 1) * P], xk2[:, :],
                          start=True, stop=True).then_inc(s["fk_ready"], 1)

            def receptance2(c, i):
                t.wait_ge(s["h2_ready"], c + 1)
                bank_free(i, *receptance2_bank(i))
                for n in range(CT):
                    q, at = n * P // T, n * P % T
                    nt.matmul(pr[:, n * P:(n + 1) * P], h2T[:, q, at + 1:at + 1 + P], mix2[:, 0, :], start=True, stop=False)
                    last = nt.matmul(pr[:, n * P:(n + 1) * P], h2T[:, q, at:at + P], mix2[:, 1, :], start=False, stop=True)
                last.then_inc(s["r2_ready"], 1)

            def mixed_channels(c):
                t.wait_ge(s["sq_act"], (c + 1) * (HF // 2))
                t.wait_ge(s["sq_pool"], (c + 1) * (HF // 2))
                after(t, "x2_step", c)
                for n in range(CT):
                    for j in range(HF):
                        last = nt.matmul(pkv[:, n * P:(n + 1) * P], kf[:, j, n * P:(n + 1) * P], wfv_sb[:, j, :],
                                         start=j == 0, stop=j == HF - 1)
                last.then_inc(s["kv_ready"], 1)

            def rwkv(c):
                t.wait_ge(s["yT_ready"], c + 1)
                t.wait_ge(s["x0_ready"], c + 1)
                after(t, "x1_ready", c)
                for n in range(CT):
                    to = po[:, n * P:(n + 1) * P]
                    nt.matmul(to, ident[:, :], x0_all[:, ds(c * CT + n, 1), :].rearrange("p a c -> p (a c)"), start=True, stop=False)
                    last = nt.matmul(to, yT[:, n * P:(n + 1) * P], sq_sb[:, 3, :], start=False, stop=True)
                last.then_inc(s["po_ready"], 1)

            def receptance_bank(i):
                return ("th2_ready", i - 1), ("th_ready", i)

            def receptance2_bank(i):
                return ("th_ready", i), ("th2_ready", i - 2)

            def turn1_bank(i):
                return ("logits_ready", i - 3), ("xnT_ready", i - 3), ("h2_ready", i - 2), ("hT_ready", i)

            def turn2_bank(i):
                return ("hT_ready", i + 1), ("logits_ready", i - 3), ("xnT_ready", i - 3), ("h2_ready", i - 2)

            def turn3_bank(i):
                return ("h2_ready", i - 1), ("hT_ready", i + 1), ("logits_ready", i - 3), ("xnT_ready", i - 3)

            def router_bank(i):
                return ("xnT_ready", i - 2), ("h2_ready", i - 1), ("hT_ready", i + 1), ("logits_ready", i - 3)

            def turn(i, at):
                at(3, mixed_channels)
                at(0, turn1, i)
                at(0, keys)
                at(2, turn2, i)
                at(0, values)
                at(2, receptance2, i)
                at(3, turn3, i)
                at(2, hidden, 0)
                at(2, hidden, 1)
                at(2, hidden, 2)
                at(2, hidden, 3)
                at(3, router, i)
                at(0, receptance, i)
                at(1, rwkv)

            pipeline(t, turn)

        s2 = {}
        for n in ("route prefix_ready totals_ready fall_exp gap_ready rows_zero rows_moved shared_rows_moved xn_loaded "
                  "tiles_step tiles_ready map_used map_ready rows_step owner_ready split "
                  "sh_gate sh_up sh_gelu sh_raw sh_act sh_out sh_taken sh_added "
                  "ready_gi xT_psum xT_ready gate_ready up_ready gelu_ready act_ready actT_psum "
                  "actT_ready y_ready yo_ready "
                  "weights_ready first_weighed first_added gather_begun scatter_begun fin_sum fin_ready fin_pow fin_nmr fin_out").split():
            s2[n] = sem("e_" + n)
        YB = 4
        gathered = [sem(f"gathered{m}") for m in range(U)]
        scattered = [sem(f"scattered{m}") for m in range(U)]
        y_loaded = [sem(f"y_loaded{m}") for m in range(YB)]
        stored = [sem(f"stored{m}") for m in range(2)]
        LAST = TILES // U - 1

        ps_a, ps_g, ps_t, ps_x, ps_y = banks[0:5]
        sh_ps = banks[0:2 * HS]
        sh_y, ps_map, ps_pre, ps_tot = banks[4], banks[5], banks[6], banks[7]

        first_block.close()
        experts = ctx.enter_context(nc.Block())

        @experts.sync
        def _(sp):
            sp.wait_ge(s["table_written"], CH * 16)
            sp.wait_ge(s["xnT_kept"], CH * 16)
            sp.dma_start(xn_all[:, :, :], table_v).then_inc(s2["xn_loaded"], 16)
            sp.wait_ge(s2["rows_zero"], 1)
            sp.wait_ge(s2["split"], 5)
            for lo, hi, base, zeroed, name in ((B2, NB, BS2, 1, "shared_rows_moved"), (0, B1, 0, 2, "rows_moved"),
                                               (B1, B2, BE2, 2, "rows_moved")):
                sp.wait_ge(s2["rows_zero"], zeroed)
                for n in range(3):
                    sp.dma_start(bias_rows[n:n + 1, base:base + (hi - lo) * P], bpart[n][:, lo:hi]).then_inc(s2[name], 16)
            for m in range(U):
                sp.wait_ge(scattered[m], (LAST + 1) * 16)

            def load(c, m):
                sp.dma_start(y_first[:, ds(c * CT, CT), :], routed_v[:, 0, ds(c * CT, CT), :]).then_inc(y_loaded[m], 16)
                sp.dma_start(y_second[:, ds(c * CT, CT), :], routed_v[:, 1, ds(c * CT, CT), :]).then_inc(y_loaded[m], 16)

            for m in range(YB):
                load(m, m)
            with sp.Fori(1, CH // YB) as r:
                for m in range(YB):
                    sp.wait_ge(y_loaded[m], r * 32)
                    load(r * YB + m, m)

            with sp.Fori(0, CH // 2) as r:
                for b in range(2):
                    sp.wait_ge(s2["fin_out"], r * 2 + b + 1)
                    sp.dma_start(out_v[:, ds((r * 2 + b) * CT, CT), :], fo[b][:, :, :]).then_inc(stored[b], 16)
            for b in range(2):
                sp.wait_ge(stored[b], CH // 2 * 16)

        def tiles(eng, group):
            group(0)
            with eng.Fori(1, LAST) as r:
                group(r)
            group(LAST)

        def after2(eng, name, count):
            if not (isinstance(count, int) and count <= 0):
                eng.wait_ge(name if not isinstance(name, str) else s2[name], count)

        def last_stage(eng, step):
            def steps(r):
                for m in range(YB):
                    step(r * YB + m, m, m % 2, r * (YB // 2) + m // 2, r)

            steps(0)
            if CH // YB > 2:
                with eng.Fori(1, CH // YB - 1) as r:
                    steps(r)
            steps(CH // YB - 1)

        def chunk_ahead(c, m, r):
            return None if isinstance(c, int) and c == CH - 1 else (c + 1, (m + 1) % YB, r + (m + 1) // YB)

        def later(c):
            return not (isinstance(c, int) and c == 0)

        @experts.gpsimd
        def _(g):
            ng = nc.gpsimd
            ng.memset(bias_rows[:, BS2:BS2 + C], 0.0).then_inc(s2["rows_zero"], 1)
            ng.memset(bias_rows[:, 0:BS2], 0.0).then_inc(s2["rows_zero"], 1)

            def take_wait(at, name, n):
                after2(g, name, n)
                ng.tensor_tensor(g_wait[:, at:at + 1], g_wait[:, 0:1], g_wait[:, 0:1], ALU.add).then_inc(s2[name], 1)

            ng.memset(g_wait[:, :], 0.0).then_inc(s2["rows_zero"], 1)
            g.wait_ge(s2["rows_zero"], 3)

            def gather(m, n):
                after2(g, "xT_psum", n - U + 1)
                g.wait_ge(s2["ready_gi"], n + 1)
                take_wait(1, "gather_begun", n)
                ng.indirect_dma_start(xg[m][:, :], None, table,
                                      bass.IndirectOffsetOnAxis(ap=gi[m][:, 0:1], axis=0)).then_inc(gathered[m], 16)

            def scatter(m, n):
                g.wait_ge(s2["yo_ready"], n + 1)
                take_wait(2, "scatter_begun", n)
                ng.indirect_dma_start(routed, bass.IndirectOffsetOnAxis(ap=si[m][:, 0:1], axis=0), yo[m][:, :], None,
                                      bounds_check=SLOTS - 1, oob_is_err=False).then_inc(scattered[m], 16)

            def shared_act(c):
                for j in range(HS):
                    g.wait_ge(s2["sh_gelu"], c * HS + j + 1)
                    g.wait_ge(s2["sh_raw"], c * HS + j + 1)
                    ng.tensor_tensor(ash[:, j, :], ash[:, j, :], gsh[:, j, :], ALU.mult).then_inc(s2["sh_act"], 1)

            def shared_add(c):
                g.wait_ge(s2["sh_taken"], c + 1)
                ng.tensor_tensor(x_all[:, ds(c * CT, CT), :], x_all[:, ds(c * CT, CT), :],
                                 xn_all[:, ds(c * CT, CT), :], ALU.add).then_inc(s2["sh_added"], 1)

            shared_act(0)
            g.wait_ge(s2["xn_loaded"], 16)
            with g.Fori(1, CH - 2) as c:
                shared_act(c)
                shared_add(c - 1)
            shared_act(CH - 2)
            for m in range(2):
                gather(m, m)
            shared_add(CH - 3)
            shared_act(CH - 1)
            for m in range(2, U):
                gather(m, m)
            shared_add(CH - 2)
            shared_add(CH - 1)

            def group(r):
                for m in range(U):
                    if not (isinstance(r, int) and r == LAST):
                        gather(m, r * U + m + U)
                    scatter(m, r * U + m)

            tiles(g, group)

            def deviation(c, b):
                g.wait_ge(s2["fin_ready"], c * 2 + 2)
                after2(g, "fin_out", c - 1)
                over_deviation(g, fve[b], fne[b], frs[b], fnm[b], fmv[b], s2["fin_pow"], c, s2["fin_nmr"])

            def add_first(c):
                at = ds(c * CT, CT)
                g.wait_ge(s2["first_weighed"], c + 1)
                ng.tensor_tensor(x_all[:, at, :], x_all[:, at, :], y_first[:, at, :], ALU.add).then_inc(s2["first_added"], 1)

            def step(c, m, b, uses, r):
                if later(c):
                    deviation(c - 1, 1 - b)
                if chunk_ahead(c, m, r):
                    add_first(c + 1)

            add_first(0)
            last_stage(g, step)
            deviation(CH - 1, 1)

        @experts.vector
        def _(v):
            nv = nc.vector
            done = [0]

            def routed_by(ins):
                done[0] += 1
                ins.then_inc(s2["route"], 1)
                v.wait_ge(s2["route"], done[0])

            v.wait_ge(s["expert_w_loaded"], 7 * 16)
            for n, (of, to) in enumerate(((braw, bleft), (bleft, bleft2))):
                nv.tensor_copy(bpart[n][:, :], of[:, :]).then_inc(s2["split"], 1)
                v.wait_ge(s2["split"], 2 * n + 1)
                nv.tensor_tensor(to[:, :], of[:, :], bpart[n][:, :], ALU.subtract).then_inc(s2["split"], 1)
                v.wait_ge(s2["split"], 2 * n + 2)
            nv.tensor_copy(bpart[2][:, :], bleft2[:, :]).then_inc(s2["split"], 1)

            def over(ap, n):
                return ap.unsqueeze(2).to_broadcast([P, ap.shape[1], n])

            def under(ap, n):
                return ap.unsqueeze(1).to_broadcast([P, n, ap.shape[1]])

            for k, of in enumerate((lg, lg2)):
                routed_by(nv.tensor_reduce(top[k][:, :], of[:, :, :], AX.X, ALU.max))
                routed_by(nv.tensor_tensor(eq[:, :, :], of[:, :, :], over(top[k][:, :], E), ALU.is_equal))
                routed_by(nv.tensor_tensor(eq[:, :, :], eq[:, :, :], under(keep_first[:, :], NT), ALU.mult))
                routed_by(nv.tensor_reduce(which[:, :], eq[:, :, :], AX.X, ALU.max))
                routed_by(nv.tensor_tensor(pick[k][:, :, :], under(keep_first[:, :], NT), over(which[:, :], E), ALU.is_equal))
                if k == 0:
                    routed_by(nv.scalar_tensor_tensor(lg2[:, :, :], pick[0][:, :, :], -1e30, lg[:, :, :], ALU.mult, ALU.add))
            nv.tensor_tensor(fall[:, :], top[1][:, :], top[0][:, :], ALU.subtract).then_inc(s2["gap_ready"], 1)
            routed_by(nv.tensor_tensor(sel[:, :, :], pick[0][:, :, :], pick[1][:, :, :], ALU.add))
            v.wait_ge(s2["totals_ready"], 1)
            routed_by(nv.tensor_copy(tot[:, :, :], ps_tot[:, 0:NT * E].rearrange("p (n e) -> p e n", e=E)))
            routed_by(nv.tensor_tensor_scan(incl[:, :, :].rearrange("p e n -> p (e n)"),
                                            scan_on[:, :, :].rearrange("p e n -> p (e n)"),
                                            tot[:, :, :].rearrange("p e n -> p (e n)"), 0.0, ALU.mult, ALU.add))
            routed_by(nv.tensor_tensor(more[:, :, :], over(incl[:, :, NT - 1], NT), under(thr_f[:, :], E), ALU.is_gt))
            routed_by(nv.tensor_reduce(ntl[:, :], more[:, :, :], AX.X, ALU.add))
            routed_by(nv.tensor_tensor_scan(cumt[:, :], scan_on[:, 0, 1:E + 1], ntl[:, :], 0.0, ALU.mult, ALU.add))
            routed_by(nv.tensor_tensor(start[:, :], cumt[:, :], ntl[:, :], ALU.subtract))
            routed_by(nv.tensor_scalar(start[:, :], start[:, :], float(P), None, ALU.mult))
            routed_by(nv.tensor_tensor(more[:, :, :], incl[:, :, :], tot[:, :, :], ALU.subtract))
            routed_by(nv.tensor_tensor(more[:, :, :], more[:, :, :], over(start[:, :], NT), ALU.add))
            v.wait_ge(s2["prefix_ready"], 1)
            routed_by(nv.tensor_tensor(sc_pos[:, :, :], ps_pre[:, 0:NT * E].rearrange("p (n e) -> p n e", e=E),
                                       more[:, :, :].rearrange("p e n -> p n e"), ALU.add))
            for k in range(K):
                routed_by(nv.tensor_tensor(eq[:, :, :], pick[k][:, :, :], sc_pos[:, :, :], ALU.mult))
                routed_by(nv.tensor_reduce(slot[:, k, :], eq[:, :, :], AX.X, ALU.add))
            routed_by(nv.tensor_copy(slot_i[:, :], slot[:, :, :].rearrange("p k n -> p (k n)")))
            routed_by(nv.tensor_scalar(tile_s[:, :], slot_i[:, :], P.bit_length() - 1, None, ALU.arith_shift_right))
            routed_by(nv.tensor_scalar(lane_s[:, :], slot_i[:, :], P - 1, None, ALU.bitwise_and))
            routed_by(nv.tensor_copy(tile_j[:, :], tile_s[:, :]))
            routed_by(nv.tensor_copy(lane_j[:, :], lane_s[:, :]))
            routed_by(nv.tensor_tensor(before[:, :, :], cumt[0:1, :].unsqueeze(1).to_broadcast([1, TILES, E]),
                                       lane_f[0:1, 0:TILES].unsqueeze(2).to_broadcast([1, TILES, E]), ALU.is_le))
            routed_by(nv.tensor_reduce(owner_f[:, :], before[:, :, :], AX.X, ALU.add))
            routed_by(nv.tensor_scalar(owner_f[:, :], owner_f[:, :], float(E - 1), None, ALU.min))
            nv.memset(owner[:, :], 0.0)
            for m in range(SPAN):
                last = nv.memset(places[:, m:m + 1], float(2 ** (BITS * (m if m < LOW else m - LOW))))
            routed_by(last)
            routed_by(nv.tensor_copy(owner[:, 1:TILES + 1], owner_f[:, :]))
            for lo, hi, at in ((0, U, 0), (U, SPAN, U)):
                routed_by(nv.tensor_tensor(owner_at[:, :, lo:hi], owner[:, at:at + TILES].rearrange("o (g m) -> o g m", m=U)[:, :, 0:hi - lo],
                                           places[:, lo:hi].unsqueeze(1).to_broadcast([1, GROUPS, hi - lo]), ALU.mult))
            for n, (lo, hi) in enumerate(((0, LOW), (LOW, SPAN))):
                routed_by(nv.tensor_reduce(part_of[n][:, :], owner_at[:, :, lo:hi], AX.X, ALU.add))
                routed_by(nv.tensor_copy(part_int[n][:, :], part_of[n][:, :]))
            routed_by(nv.tensor_scalar(part_int[1][:, :], part_int[1][:, :], LOW * BITS, None, ALU.logical_shift_left))
            nv.tensor_tensor(packed[:, :], part_int[0][:, :], part_int[1][:, :], ALU.bitwise_or).then_inc(s2["owner_ready"], 1)
            def map_batch(q, b):
                after2(v, "map_used", q - 1)
                nv.tensor_tensor(oh_lane[b][:, :, :], lane_j[:, ds(q * JB, JB)].unsqueeze(2).to_broadcast([P, JB, P]),
                                 lane_bf[:, :].unsqueeze(1).to_broadcast([P, JB, P]), ALU.is_equal)
                nv.tensor_tensor(oh_tile[b][:, :, :], tile_j[:, ds(q * JB, JB)].unsqueeze(2).to_broadcast([P, JB, TILES]),
                                 lane_bf[:, 0:TILES].unsqueeze(1).to_broadcast([P, JB, TILES]),
                                 ALU.is_equal).then_inc(s2["tiles_step"], 1)
                v.wait_ge(s2["tiles_step"], q + 1)
                nv.tensor_scalar(tile_val[b][:, :, 0, :], oh_tile[b][:, :, :], part_f[:, 0:1], None, ALU.mult)
                nv.tensor_tensor(tile_val[b][:, :, 1, :], oh_tile[b][:, :, :],
                                 left_bf[:, ds(q * JB, JB)].unsqueeze(2).to_broadcast([P, JB, TILES]),
                                 ALU.mult).then_inc(s2["tiles_ready"], 1)

            def map_pair(h):
                for b in range(2):
                    map_batch(h * 2 + b, b)

            map_pair(0)
            with v.Fori(1, NQ // 2) as h:
                map_pair(h)
            v.wait_ge(s2["map_ready"], 1)
            nv.tensor_scalar(row_f[:, :], ps_map[:, TILES:2 * TILES], -float(P), float(SLOTS), ALU.mult,
                             ALU.add).then_inc(s2["rows_step"], 1)
            v.wait_ge(s2["rows_step"], 1)
            nv.tensor_tensor(row_g[:, :], row_f[:, :], ps_map[:, 0:TILES], ALU.add).then_inc(s2["rows_step"], 1)
            v.wait_ge(s2["rows_step"], 2)
            nv.tensor_copy(row_out[:, :], row_g[:, :]).then_inc(s2["rows_step"], 1)
            v.wait_ge(s2["rows_step"], 3)
            nv.tensor_scalar(row_in[:, :], row_out[:, :], N - 1, None, ALU.bitwise_and).then_inc(s2["rows_step"], 1)
            v.wait_ge(s2["rows_step"], 4)
            for m in range(U):
                nv.tensor_copy(gi[m][:, :], row_in[:, m:m + 1]).then_inc(s2["ready_gi"], 1)
            def take_x(m, n):
                v.wait_ge(s2["xT_psum"], n + 1)
                after2(v, "up_ready", n - U + 1)
                nv.tensor_copy(xT[m][:, :], ps_x[:, 0:P]).then_inc(s2["xT_ready"], 1)

            take_x(0, 0)

            def group(r):
                for m in range(U):
                    n = r * U + m
                    if not (isinstance(n, int) and n == TILES - 1):
                        take_x((m + 1) % U, n + 1)
                    if not (isinstance(n, int) and n < 2):
                        give_y((m - 2) % U, n - 2, r if m >= 2 else r - 1)
                    v.wait_ge(s2["up_ready"], n + 1)
                    v.wait_ge(s2["gelu_ready"], n + 1)
                    after2(v, "actT_psum", n)
                    nv.tensor_tensor(actv[:, :], ps_a[:, 0:HR], gl[:, :], ALU.mult).then_inc(s2["act_ready"], 1)
                    if not (isinstance(r, int) and r == LAST):
                        v.wait_ge(gathered[m], (r + 1) * 16)
                        nv.tensor_copy(gi[m][:, :], row_in[:, ds(n + U, 1)]).then_inc(s2["ready_gi"], 1)

            def give_y(m, n, r):
                after2(v, scattered[m], r * 16)
                nv.tensor_copy(si[m][:, :], row_out[:, ds(n, 1)])
                v.wait_ge(s2["y_ready"], n + 1)
                nv.tensor_copy(yo[m][:, :], ps_y[:, 0:C]).then_inc(s2["yo_ready"], 1)

            tiles(v, group)
            for m in (U - 2, U - 1):
                give_y(m, LAST * U + m, LAST)

            v.wait_ge(s2["fall_exp"], 1)
            routed_by(nv.tensor_scalar(total[:, :], rel[:, :], 1.0, None, ALU.add))
            routed_by(nv.reciprocal(wt[0][:, :], total[:, :]))
            nv.tensor_tensor(wt[1][:, :], rel[:, :], wt[0][:, :], ALU.mult).then_inc(s2["weights_ready"], 1)

            v.wait_ge(s2["weights_ready"], 1)

            def step(c, m, b, uses, r):
                v.wait_ge(y_loaded[m], (r + 1) * 32)
                v.wait_ge(s2["first_added"], c + 1)
                after2(v, "fin_out", c - 1)
                for t in range(CT):
                    last = nv.scalar_tensor_tensor(fin[b][:, t, :], y_second[:, ds(c * CT + t, 1), :].rearrange("p a c -> p (a c)"),
                                                   wt[1][:, ds(c * CT + t, 1)],
                                                   x_all[:, ds(c * CT + t, 1), :].rearrange("p a c -> p (a c)"), ALU.mult, ALU.add)
                last.then_inc(s2["fin_sum"], 1)
                v.wait_ge(s2["fin_sum"], c + 1)
                for t in range(CT):
                    last = nv.bn_stats(fst[b][:, t, :], fin[b][:, t, :])
                last.then_inc(s2["fin_ready"], 1)
                v.wait_ge(s2["fin_ready"], c * 2 + 1)
                nv.memset(wait_here[:, :], 0.0)
                for t in range(CT):
                    last = nv.bn_aggr(fmv[b][:, t, :], fst[b][:, t, :])
                last.then_inc(s2["fin_ready"], 1)

            last_stage(v, step)

        @experts.scalar
        def _(a):
            na = nc.scalar
            def shared(c):
                for j in range(HS):
                    a.wait_ge(s2["sh_gate"], c * HS + j + 1)
                    after2(a, "sh_act", (c - 1) * HS + j + 1)
                    na.activation(gsh[:, j, :], sh_ps[HS + j][:, :], ACT.Gelu, bias=col(BS1 + HS + j)).then_inc(s2["sh_gelu"], 1)
                for j in range(HS):
                    a.wait_ge(s2["sh_up"], c * HS + j + 1)
                    if j == 0:
                        after2(a, "sh_out", c)
                    na.activation(ash[:, j, :], sh_ps[j][:, :], ACT.Identity, bias=col(BS1 + j)).then_inc(s2["sh_raw"], 1)

            def shared_take(c):
                a.wait_ge(s2["sh_out"], c + 1)
                na.activation(x_all[:, ds(c * CT, CT), :], sh_y[:, :].rearrange("p (n c) -> p n c", c=C),
                              ACT.Copy).then_inc(s2["sh_taken"], 1)

            shared(0)
            with a.Fori(1, CH) as c:
                shared(c)
                shared_take(c - 1)
            shared_take(CH - 1)
            def turn_act(n):
                a.wait_ge(s2["actT_psum"], n + 1)
                after2(a, "y_ready", n)
                na.activation(actT[:, :], ps_t[:, 0:HR], ACT.Copy).then_inc(s2["actT_ready"], 1)

            def group(r):
                for m in range(U):
                    n = r * U + m
                    a.wait_ge(s2["gate_ready"], n + 1)
                    after2(a, "act_ready", n)
                    na.activation(gl[:, :], ps_g[:, 0:HR], ACT.Gelu).then_inc(s2["gelu_ready"], 1)
                    if not (isinstance(n, int) and n == 0):
                        turn_act(n - 1)

            tiles(a, group)
            turn_act(TILES - 1)

            a.wait_ge(s2["gap_ready"], 1)
            na.activation(rel[:, :], fall[:, :], ACT.Exp, scale=1.0 / TAU).then_inc(s2["fall_exp"], 1)

            def normed(c, b, uses):
                a.wait_ge(s2["fin_nmr"], c + 1)
                after2(a, stored[b], uses * 16)
                for t in range(CT):
                    last = na.activation(fo[b][:, t, :], fin[b][:, t, :], ACT.Identity,
                                         bias=fnm[b][:, t:t + 1], scale=frs[b][:, t:t + 1])
                last.then_inc(s2["fin_out"], 1)

            def weigh(c, m, r):
                a.wait_ge(y_loaded[m], (r + 1) * 32)
                for t in range(CT):
                    row = y_first[:, ds(c * CT + t, 1), :].rearrange("p a c -> p (a c)")
                    last = na.activation(row, row, ACT.Copy, scale=wt[0][:, ds(c * CT + t, 1)])
                last.then_inc(s2["first_weighed"], 1)

            def step(c, m, b, uses, r):
                ahead = chunk_ahead(c, m, r)
                if ahead:
                    weigh(*ahead)
                if later(c):
                    normed(c - 1, 1 - b, uses - (1 - b))

            a.wait_ge(s2["weights_ready"], 1)
            weigh(0, 0, 0)
            last_stage(a, step)
            normed(CH - 1, 1, CH // 2 - 1)
        @experts.tensor
        def _(t):
            nt = nc.tensor
            t.wait_ge(s["expert_w_loaded"], 7 * 16)
            t.wait_ge(s["xnT_kept"], CH * 16)
            def counts():
                t.wait_ge(s2["route"], 12)
                for ps, w, name in ((ps_tot, ones_bf, "totals_ready"), (ps_pre, upper, "prefix_ready")):
                    nt.matmul(ps[:, 0:NT * E], w[:, :], sel[:, :, :].rearrange("p n e -> p (n e)"),
                              start=True, stop=True).then_inc(s2[name], 1)

            def biased(to, row, width):
                return nt.matmul(to, ones_bf[:, :], bias_rows[:, ds(row, width)], start=False, stop=True)

            GATE, UP = (HS, "sh_gate", "sh_gelu"), (0, "sh_up", "sh_raw")

            def shared_in(c, parts=(GATE, UP)):
                for half_, name, free in parts:
                    for j in range(HS):
                        after2(t, free, c * HS - HS + j + 1)
                        nt.matmul(sh_ps[half_ + j][:, :], ws1_sb[:, (half_ + j) * P:(half_ + j + 1) * P],
                                  xnT_all[:, ds(c * W, W)], start=True, stop=True).then_inc(s2[name], 1)

            def shared_out(c):
                t.wait_ge(s2["sh_act"], (c + 1) * HS)
                after2(t, "sh_taken", c)
                for n in range(CT):
                    for j in range(HS):
                        nt.matmul(sh_y[:, n * P:(n + 1) * P], ash[:, j, n * P:(n + 1) * P], ws2_sb[:, j, :],
                                  start=j == 0, stop=False)
                    last = biased(sh_y[:, n * P:(n + 1) * P], BS2, C)
                last.then_inc(s2["sh_out"], 1)

            def map_batch(q, b):
                t.wait_ge(s2["tiles_ready"], q + 1)
                for j in range(JB):
                    last = nt.matmul(ps_map[:, 0:2 * TILES], oh_lane[b][:, j, :],
                                     tile_val[b][:, j, :, :].rearrange("p a n -> p (a n)"),
                                     start=isinstance(q, int) and q == 0 and j == 0,
                                     stop=isinstance(q, int) and q == NQ - 1 and j == JB - 1)
                last.then_inc(s2["map_used"], 1)

            def turn_x(m, n, r):
                t.wait_ge(gathered[m], (r + 1) * 16)
                after2(t, "xT_ready", n)
                nt.transpose(ps_x[:, 0:P], xg[m][:, :], ident[:, :]).then_inc(s2["xT_psum"], 1)

            def experts_of(r):
                word = t.value_load(packed[0:1, ds(r, 1)])
                return [t.snap((word >> (BITS * m)) & (2 ** BITS - 1)).with_bounds(min_val=0, max_val=E - 1) for m in range(SPAN)]

            def hidden(m, to, e, off):
                nt.matmul(to[:, 0:HR], xT[m][:, :], we1_sb[:, ds(e, 1), off:off + HR].rearrange("p a h -> p (a h)"),
                          start=True, stop=False)
                return biased(to[:, 0:HR], e * H1 + off, HR)

            def turn_act(n):
                t.wait_ge(s2["act_ready"], n + 1)
                after2(t, "actT_ready", n)
                for j in range(HK):
                    last = nt.transpose(ps_t[:, j * P:(j + 1) * P], actv[:, j * P:(j + 1) * P], ident[:, :])
                last.then_inc(s2["actT_psum"], 1)

            def second(n, e):
                if isinstance(n, int) and n == 0:
                    t.wait_ge(s2["sh_taken"], CH)
                t.wait_ge(s2["actT_ready"], n + 1)
                after2(t, "yo_ready", n)
                for j in range(HK):
                    nt.matmul(ps_y[:, 0:C], actT[:, j * P:(j + 1) * P],
                              we2_sb[:, ds(e, 1), j, :].rearrange("p a c -> p (a c)"), start=j == 0, stop=False)
                biased(ps_y[:, 0:C], BE2 + e * C, C).then_inc(s2["y_ready"], 1)

            def gate_of(m, n, e):
                t.wait_ge(s2["xT_ready"], n + 1)
                after2(t, "gelu_ready", n)
                hidden(m, ps_g, e, HR).then_inc(s2["gate_ready"], 1)

            def up_of(m, n, e):
                after2(t, "act_ready", n)
                hidden(m, ps_a, e, 0).then_inc(s2["up_ready"], 1)

            LEAD = CH - NQ // 2 - 1
            shared_in(0)
            shared_in(1, (GATE,))
            counts()
            shared_in(1, (UP,))
            t.wait_ge(s2["shared_rows_moved"], 3 * 16)
            shared_out(0)
            for c in range(2, LEAD):
                shared_in(c)
                shared_out(c - 1)

            def pair(h, last=False):
                shared_in(h + LEAD)
                map_batch(h * 2, 0)
                shared_out(h + LEAD - 1)
                map_batch(h * 2 + 1, 1)
                if last:
                    t.wait_ge(s2["map_used"], NQ)
                    nt.matmul(ps_pre[:, 0:1], ones_bf[:, :], ones_bf[:, 0:1], start=True, stop=True).then_inc(s2["map_ready"], 1)

            pair(0)
            with t.Fori(1, NQ // 2 - 1) as h:
                pair(h)
            pair(NQ // 2 - 1, last=True)

            shared_in(CH - 1)
            shared_out(CH - 2)
            t.wait_ge(s2["sh_gelu"], CH * HS)
            t.wait_ge(s2["sh_raw"], CH * HS)
            turn_x(0, 0, 0)
            t.wait_ge(s2["owner_ready"], 1)
            t.wait_ge(s2["rows_moved"], 6 * 16)
            gate_of(0, 0, experts_of(0)[1])
            shared_out(CH - 1)
            turn_x(1, 1, 0)

            def group(r):
                e = experts_of(r)
                for m in range(U):
                    n = r * U + m
                    if m:
                        gate_of(m, n, e[m + 1])
                        if not (isinstance(n, int) and n == TILES - 1):
                            turn_x((m + 1) % U, n + 1, r + (m + 1) // U)
                        if not (isinstance(n, int) and n < 2):
                            second(n - 2, e[m - 1])
                    if not (isinstance(n, int) and n == 0):
                        turn_act(n - 1)
                    up_of(m, n, e[m + 1])
                n = (r + 1) * U
                if not (isinstance(n, int) and n == TILES):
                    gate_of(0, n, e[U + 1])
                    turn_x(1, n + 1, r + 1)
                second(n - 2, e[U - 1])
                return e[U]

            group(0)
            with t.Fori(1, LAST) as r:
                group(r)
            e_end = group(LAST)
            turn_act(TILES - 1)
            second(TILES - 1, e_end)




def kernel(**inputs):
    import numpy as np
    import concourse.bacc as bacc
    from concourse.bass_utils import run_bass_kernel_spmd

    a = {k.removeprefix("L0_"): np.asarray(v) for k, v in inputs.items()}
    columns = [a[f"attn_{n}"] for n in ("ln1_w", "ln1_b", "ln2_w", "ln2_b", "time_decay", "time_first",
                                        "tmk", "tmv", "tmr", "cmk", "cmr")]
    columns += list(a["ffn_bs1"].reshape(-1, 128))
    arrays = {
        "x": a["attn_x"],
        "vecs": np.stack(columns, axis=1),
        "rows": np.concatenate([a["attn_ln0_w"], a["attn_ln0_b"], a["ffn_br"]]),
        "sqw": np.stack([a[f"attn_{n}"].T for n in ("Wk", "Wv", "Wr", "Wo", "Wfr")]),
        "wfk": a["attn_Wfk"].T,
        "wfv": a["attn_Wfv"].T,
        "wrt": a["ffn_Wr"],
        "ws1": a["ffn_Ws1"],
        "ws2": a["ffn_Ws2"],
        "we1": a["ffn_We1"],
        "we2": a["ffn_We2"],
        "be1": a["ffn_be1"],
        "be2": a["ffn_be2"],
        "bs2": a["ffn_bs2"],
    }
    arrays = {k: np.ascontiguousarray(v) for k, v in arrays.items()}
    nc = bacc.Bacc("TRN2", target_bir_lowering=False, num_devices=1)
    aps = {k: nc.dram_tensor(k, v.shape, mybir.dt.from_np(v.dtype), kind="ExternalInput").ap() for k, v in arrays.items()}
    out = nc.dram_tensor("out", a["attn_x"].shape, mybir.dt.float32, kind="ExternalOutput").ap()
    build(nc, out=out, **aps)
    return run_bass_kernel_spmd(nc, [arrays], core_ids=[0]).results[0]["out"]
```
